# Optimizing a Trainium2 kernel written in Bass

```python
import numpy as np
import jax
import jax.numpy as jnp

def _softmax(x, axis=-1):
    return jax.nn.softmax(x, axis=axis)

def _gelu(x):
    return jax.nn.gelu(x, approximate=True)

def _silu(x):
    return jax.nn.silu(x)

def _sigmoid(x):
    return jax.nn.sigmoid(x)

def _layernorm(x, axis=-1, eps=1e-05):
    m = jnp.mean(x, axis=axis, keepdims=True)
    v = jnp.var(x, axis=axis, keepdims=True)
    return (x - m) / jnp.sqrt(v + eps)

def _scatter_add(tgt, idx, src, axis=0):
    return tgt.at[idx].add(src)

def _segment_sum(src, seg, n):
    return jax.ops.segment_sum(src, seg, n)
kernel_name = 'mk_macaron_d1_jaxref_r4_ead143'

def setup_inputs(seed: int=0):
    np.random.seed(seed)
    _w = jnp.asarray

    def _L0_attn_setup():
        import jax, jax.numpy as jnp
        import numpy as np
        B, T, D, H = (1, 1024, 256, 16)
        HD = D // H
        W_LOCAL = 64
        N_GLOBAL = 64
        key = jax.random.key(seed)
        ks = jax.random.split(key, 7)
        s = 0.02
        return {'hidden_states': jax.random.normal(ks[0], (B, T, D), dtype=jnp.float32), 'Wqkv': jax.random.normal(ks[1], (D, 3 * D), dtype=jnp.float32) * s, 'bqkv': jnp.zeros((3 * D,), dtype=jnp.float32), 'Wout': jax.random.normal(ks[2], (D, D), dtype=jnp.float32) * s, 'bout': jnp.zeros((D,), dtype=jnp.float32), 'Wg': jax.random.normal(ks[3], (D, 1), dtype=jnp.float32) * s, 'bg': jnp.zeros((1,), dtype=jnp.float32)}
    _L0_attn_in = _L0_attn_setup()

    def _L0_ffn_setup():
        import jax, jax.numpy as jnp
        import numpy as np
        import math
        EMBED_DIM = 256
        FFN_DIM = 1024
        N_EXPERTS = 8
        TOP_K = 2
        CAP_FACTOR = 1.25
        key = jax.random.key(seed)
        k0, k1, k2, k3 = jax.random.split(key, 4)
        B, S = (4, 512)
        x = jax.random.normal(k0, (B, S, EMBED_DIM), dtype=jnp.float32)
        Wr = jax.random.normal(k1, (EMBED_DIM, N_EXPERTS), dtype=jnp.float32) * 0.02
        W1 = jax.random.normal(k2, (N_EXPERTS, EMBED_DIM, FFN_DIM), dtype=jnp.float32) * 0.02
        W2 = jax.random.normal(k3, (N_EXPERTS, FFN_DIM, EMBED_DIM), dtype=jnp.float32) * 0.02
        return {'x': x, 'Wr': Wr, 'W1': W1, 'W2': W2}
    _L0_ffn_in = _L0_ffn_setup()
    _d = {'L0_attn_hidden_states': _L0_attn_in['hidden_states'], 'L0_attn_Wqkv': _L0_attn_in['Wqkv'], 'L0_attn_bqkv': _L0_attn_in['bqkv'], 'L0_attn_Wout': _L0_attn_in['Wout'], 'L0_attn_bout': _L0_attn_in['bout'], 'L0_attn_Wg': _L0_attn_in['Wg'], 'L0_attn_bg': _L0_attn_in['bg'], 'L0_ffn_Wr': _L0_ffn_in['Wr'], 'L0_ffn_W1': _L0_ffn_in['W1'], 'L0_ffn_W2': _L0_ffn_in['W2']}
    _x0 = _d['L0_attn_hidden_states']
    _d['L0_attn_hidden_states'] = jax.random.normal(jax.random.fold_in(jax.random.key(seed), 1), (4, 2048, 256), dtype=_x0.dtype)
    del _x0
    return _d

def reference(L0_attn_hidden_states, L0_attn_Wqkv, L0_attn_bqkv, L0_attn_Wout, L0_attn_bout, L0_attn_Wg, L0_attn_bg, L0_ffn_Wr, L0_ffn_W1, L0_ffn_W2):

    def _L0_attn_ref(hidden_states, Wqkv, bqkv, Wout, bout, Wg, bg):
        import jax, jax.numpy as jnp
        import numpy as np
        B, T, D, H = (1, 1024, 256, 16)
        HD = D // H
        W_LOCAL = 64
        N_GLOBAL = 64
        b, t, d = hidden_states.shape
        scale = 1.0 / jnp.sqrt(jnp.asarray(HD, hidden_states.dtype))
        qkv = hidden_states @ Wqkv + bqkv
        q, k, v = jnp.split(qkv, 3, axis=-1)
        q, k, v = (x.reshape(b, t, H, HD).transpose(0, 2, 1, 3) for x in (q, k, v))
        idx = jnp.arange(t)
        local_mask = jnp.abs(idx[None, :] - idx[:, None]) <= W_LOCAL
        scores = jnp.einsum('bhqd,bhkd->bhqk', q, k) * scale
        scores = jnp.where(local_mask[None, None], scores, -jnp.inf)
        attn_local = jnp.einsum('bhqk,bhkd->bhqd', jax.nn.softmax(scores, axis=-1), v)
        ng = min(N_GLOBAL, t)
        k_g = k[:, :, :ng, :]
        v_g = v[:, :, :ng, :]
        scores_g = jnp.einsum('bhqd,bhgd->bhqg', q, k_g) * scale
        attn_global = jnp.einsum('bhqg,bhgd->bhqd', jax.nn.softmax(scores_g, axis=-1), v_g)
        gate = jax.nn.sigmoid(hidden_states @ Wg + bg).reshape(b, 1, t, 1)
        out = (1.0 - gate) * attn_local + gate * attn_global
        out = out.transpose(0, 2, 1, 3).reshape(b, t, d)
        return out @ Wout + bout

    def _L0_ffn_ref(x, Wr, W1, W2):
        import jax, jax.numpy as jnp
        import numpy as np
        import math
        EMBED_DIM = 256
        FFN_DIM = 1024
        N_EXPERTS = 8
        TOP_K = 2
        CAP_FACTOR = 1.25
        B, S, D = x.shape
        t = B * S
        xf = x.reshape(t, D)
        probs = jax.nn.softmax(xf.astype(jnp.float32) @ Wr, axis=-1)
        topk_probs, topk_experts = jax.lax.top_k(probs, TOP_K)
        cap = max(math.ceil(t * TOP_K * CAP_FACTOR / N_EXPERTS), 1)
        y = jnp.zeros_like(xf)
        for e in range(N_EXPERTS):
            mask = topk_experts == e
            gate = jnp.sum(jnp.where(mask, topk_probs, 0.0), axis=-1)
            has = jnp.any(mask, axis=-1)
            g_masked = jnp.where(has, gate, -jnp.inf)
            vals, idx = jax.lax.top_k(g_masked, cap)
            g = jnp.where(jnp.isfinite(vals), vals, 0.0)
            xe = xf[idx]
            h = jax.nn.relu(xe @ W1[e]) @ W2[e]
            y = y.at[idx].add(g[:, None] * h)
        return y.reshape(B, S, D)
    x = L0_attn_hidden_states
    x = x + 0.5 * _L0_ffn_ref(_layernorm(x, axis=-1), L0_ffn_Wr, L0_ffn_W1, L0_ffn_W2)
    x = x + _L0_attn_ref(_layernorm(x, axis=-1), L0_attn_Wqkv, L0_attn_bqkv, L0_attn_Wout, L0_attn_bout, L0_attn_Wg, L0_attn_bg)
    x = x + 0.5 * _L0_ffn_ref(_layernorm(x, axis=-1), L0_ffn_Wr, L0_ffn_W1, L0_ffn_W2)
    return x

_drawn_inputs = setup_inputs


def setup_inputs(seed=0):
    import zlib

    import numpy as np

    out = dict(_drawn_inputs(seed))
    spreads = {'L0_attn_bqkv': (0.0, 0.1), 'L0_attn_bout': (0.0, 0.1)}
    factors = {'L0_attn_Wqkv': 6.934, 'L0_attn_Wg': 8.0}
    for name, (base, spread) in spreads.items():
        noise = np.random.default_rng([zlib.crc32(name.encode()), seed]).standard_normal(out[name].shape)
        drawn = base * np.exp(spread * noise) if base else spread * noise
        out[name] = jnp.asarray(drawn.astype(out[name].dtype))
    for name, factor in factors.items():
        out[name] = (out[name] * factor).astype(out[name].dtype)
    return out
```

```python
import concourse.bass as bass
from concourse import mybir
from contextlib import ExitStack

FP32, FP16, BF16, I32 = mybir.dt.float32, mybir.dt.float16, mybir.dt.bfloat16, mybir.dt.int32
ALU = mybir.AluOpType
ACT = mybir.ActivationFunctionType
AX = mybir.AxisListType

P = 128
BATCH, SEQ, D = 4, 2048, 256
TOK = BATCH * SEQ
HEADS, HD = 16, 16
PAIRS = HEADS // 2
WINDOW = 64
N_GLOBAL = 64
EXPERTS, FFN, TOP_K = 8, 1024, 2
CAP = -(-TOK * TOP_K * 5 // (4 * EXPERTS))
EPS = 1e-5
KD = D // P
KF = FFN // P

GROUP = 4
GTOK = GROUP * P
GROUPS = TOK // GTOK

SLOTS = 256
HALVES = SLOTS // P
TILES = (TOK * TOP_K + EXPERTS * (SLOTS - 1)) // SLOTS
LIST_PAD = EXPERTS * TOK

SEQP = SEQ + 2 * WINDOW
QT = 64
SPAN = 4 * QT
SPAN_K = SPAN + 2 * WINDOW
SPANS = TOK // SPAN
LOCAL = QT + 2 * WINDOW
KEYS = LOCAL + N_GLOBAL
VW = 2 * (HD + 1)
VROW = PAIRS * 2 * VW
QUADS = 8

W_FFN = 32.0
W_ATT = 4.0
GATE_SCALE = 0.5 / (W_FFN * W_FFN)
SCORE_SCALE = HD ** -0.5 / (W_ATT * W_ATT)
PAD_Q, PAD_K = 60000.0, -60000.0
MASKED = -1e30


class Memory:

    semaphores = []

    def __init__(self, nc, ctx, phase):
        self.nc, self.ctx, self.phase = nc, ctx, phase

    def sb(self, name, shape, dt=FP32):
        return self.ctx.enter_context(self.nc.sbuf_tensor(f"{self.phase}_{name}", shape, dt))

    def ps(self, name, shape=(P, 512), dt=FP32):
        return self.ctx.enter_context(self.nc.psum_tensor(f"{self.phase}_{name}", list(shape), dt))

    def sem(self, name):
        s = self.ctx.enter_context(self.nc.semaphore(f"{self.phase}_{name}"))
        self.semaphores.append(s)
        return s

    def lasting_sem(self, name):
        return self.ctx.enter_context(self.nc.semaphore(name))


class Chain:

    def __init__(self, eng, sem, base=0):
        self.eng, self.sem, self.base, self.n = eng, sem, base, 0

    def __call__(self, ins):
        self.n += 1
        ins.then_inc(self.sem, 1)
        self.eng.wait_ge(self.sem, self.base + self.n)


def clear_semaphores(nc):
    with nc.Block() as block:
        @block.gpsimd
        def _(pool):
            for s in Memory.semaphores:
                pool.sem_clear(s)
    Memory.semaphores.clear()


def constants(m):
    c = {}
    c["ident"] = m.sb("ident", [P, P])
    c["ident16"] = m.sb("ident16", [P, P], BF16)
    c["before"] = m.sb("before", [P, P], BF16)
    c["ones16"] = m.sb("ones16", [P, P], BF16)
    c["mask"] = m.sb("mask", [P, 2, KEYS], BF16)
    c["first"] = m.sb("first", [P, EXPERTS])
    c["base"] = m.sb("base", [P, EXPERTS])
    c["token"] = m.sb("token", [P, GROUP])
    c["power"] = m.sb("power", [P, GROUP])
    c["count"] = m.sb("count", [P, EXPERTS])
    c["start_of"] = m.sb("start_of", [1, TILES], I32)
    c["expert_of"] = m.sb("expert_of", [1, TILES], I32)
    c["list_out"] = [[m.lasting_sem(f"list_out{b}{n}") for n in range(2 * GROUP)] for b in range(2)]
    c["x_in"] = [[m.lasting_sem(f"x_in{b}{h}") for h in range(HALVES)] for b in range(2)]
    c["added"] = [[m.lasting_sem(f"added{b}{h}") for h in range(HALVES)] for b in range(2)]
    c["w1"] = m.sb("w1", [P, EXPERTS, 2, KD * FFN], FP16)
    c["w2"] = m.sb("w2", [P, EXPERTS, 2, KF * D], FP16)
    return c


FILL_LINKS = 19


def fill_phase(nc, ctx, c, scratch):
    m = Memory(nc, ctx, "fill")
    zeros = m.sb("zeros", [P, 4 * VROW], FP16)
    empty = m.sb("empty", [P, 512, 2], I32)
    padk = m.sb("padk", [P, 2 * WINDOW], FP16)
    pool_done, filled = m.sem("pool_done"), m.sem("filled")
    zero32 = zeros[:, 0:2 * D].bitcast(FP32)
    with nc.Block() as block:
        @block.gpsimd
        def _(pool):
            link = Chain(pool, pool_done)
            for t in (c["ident"], c["ident16"]):
                link(pool.memset(t[:, :], 0.0))
                link(pool.affine_select(out=t[:, :], in_=t[:, :], compare_op=ALU.not_equal, fill=1.0,
                                        base=0, pattern=[[-1, P]], channel_multiplier=1))
            link(pool.memset(c["before"][:, :], 1.0))
            link(pool.affine_select(out=c["before"][:, :], in_=c["before"][:, :], compare_op=ALU.is_gt,
                                    fill=0.0, base=0, pattern=[[1, P]], channel_multiplier=-1))
            link(pool.memset(c["ones16"][:, :], 1.0))
            link(pool.memset(c["mask"][:, :, :], 0.0))
            for half in (0, QT):
                local = c["mask"][half:half + QT, :, 0:LOCAL]
                link(pool.affine_select(out=local, in_=local, compare_op=ALU.is_ge, fill=MASKED,
                                        base=0, pattern=[[0, 2], [1, LOCAL]], channel_multiplier=-1))
                link(pool.affine_select(out=local, in_=local, compare_op=ALU.is_ge, fill=MASKED,
                                        base=2 * WINDOW, pattern=[[0, 2], [-1, LOCAL]],
                                        channel_multiplier=1))
            for t, base, step in ((c["first"], EXPERTS, -1), (c["base"], 0, TOK)):
                link(pool.iota(t[:, :], pattern=[[step, EXPERTS]], base=base, channel_multiplier=0,
                               allow_small_or_imprecise_dtypes=True))
            link(pool.memset(c["power"][:, :], -0.5))
            link(pool.memset(empty[:, :, :], 0))
            link(pool.iota(empty[:, :, 0], pattern=[[0, 512 // SLOTS], [1, SLOTS]], base=TOK,
                           channel_multiplier=0))
            link(pool.memset(zeros[:, :], 0.0))
            link(pool.memset(padk[:, :], PAD_K))
            assert link.n == FILL_LINKS, link.n

        @block.sync
        def _(sp):
            sp.wait_ge(pool_done, FILL_LINKS)
            n = 0
            for name in ("list1", "list2"):
                sp.dma_start(scratch[name][0:LIST_PAD, :].rearrange("(p s) e -> p s e", p=P),
                             empty[:, :, :]).then_inc(filled, 16)
                sp.dma_start(scratch[name][LIST_PAD:LIST_PAD + SLOTS, :].rearrange("(p s) e -> p s e", p=1),
                             empty[0:1, 0:SLOTS, :]).then_inc(filled, 16)
                n += 2
            for name in ("xn1", "acc1", "xn2", "acc2"):
                for h in range(HALVES):
                    sp.dma_start(scratch[name][TOK + h * P:TOK + (h + 1) * P, :], zero32).then_inc(filled, 16)
                    n += 1
            ks = scratch["ks"].rearrange("(r p) (b t) -> r p b t", p=P, b=BATCH)
            zk = zeros[:, 0:BATCH * WINDOW].rearrange("p (b t) -> p b t", b=BATCH)
            for side in (0, SEQP - WINDOW):
                for r in range(2 * D // P):
                    sp.dma_start(ks[r, :, :, side:side + WINDOW], zk).then_inc(filled, 16)
                    n += 1
                vs = scratch["vs"].rearrange("(b t) n -> t b n", b=BATCH)
                sp.dma_start(vs[side:side + WINDOW, :, :],
                             zeros[0:WINDOW, :].rearrange("p (b n) -> p b n", b=BATCH)).then_inc(filled, 16)
                sp.dma_start(scratch["padk"][0:1, side:side + WINDOW], padk[0:1, 0:WINDOW]).then_inc(filled, 16)
                n += 2
            sp.dma_start(scratch["padk"][0:1, WINDOW:WINDOW + SEQ].rearrange("a (p s) -> (a p) s", p=16),
                         zeros[0:16, 0:SEQ // 16]).then_inc(filled, 16)
            n += 1
            sp.wait_ge(filled, 16 * n)


ROUTER_LINKS = 2 * 24


def router_phase(nc, ctx, c, scratch, which, x_src, weights):
    m = Memory(nc, ctx, f"route{which}")
    first_time = which == 1
    xn_d, acc_d, list_d = scratch[f"xn{which}"], scratch[f"acc{which}"], scratch[f"list{which}"]
    two = range(2)
    x = [m.sb(f"x{b}", [P, GROUP, D]) for b in two]
    xn = [m.sb(f"xn{b}", [P, GROUP, D]) for b in two]
    xnT = [m.sb(f"xnT{b}", [P, KD, GTOK]) for b in two]
    wr = m.sb("wr", [P, KD, EXPERTS])
    stats = m.sb("stats", [P, GROUP, 6])
    mv = [m.sb(f"mv{b}", [P, GROUP, 2]) for b in two]
    ve = [m.sb(f"ve{b}", [P, GROUP]) for b in two]
    rstd = [m.sb(f"rstd{b}", [P, GROUP]) for b in two]
    shift = [m.sb(f"shift{b}", [P, GROUP]) for b in two]
    logits = m.sb("logits", [P, GROUP, EXPERTS])
    best = m.sb("best", [P, 2, GROUP])
    key = m.sb("key", [P, GROUP, EXPERTS])
    keymax = m.sb("keymax", [P, GROUP])
    pick = [[m.sb(f"pick{b}{k}", [P, GROUP, EXPERTS]) for k in two] for b in two]
    rest = m.sb("rest", [P, GROUP, EXPERTS])
    ex = [m.sb(f"ex{b}", [P, GROUP, EXPERTS + 1]) for b in two]
    total = m.sb("total", [P, GROUP])
    chosen = [m.sb(f"chosen{b}", [P, GROUP, EXPERTS], BF16) for b in two]
    place = m.sb("place", [P, GROUP, EXPERTS])
    placed = m.sb("placed", [P, GROUP, EXPERTS])
    slot = m.sb("slot", [P, GROUP])
    run = m.sb("run", [P, EXPERTS])
    slot_i = [m.sb(f"slot_i{b}", [P, 2, GROUP], I32) for b in two]
    entry = [m.sb(f"entry{b}", [P, 2, GROUP, 2], I32) for b in two]
    psT = [m.ps(f"psT{k}") for k in range(KD)]
    psR = [m.ps(f"psR{b}") for b in two]

    def both(name):
        return [m.sem(f"{name}{b}") for b in two]

    x_in, xn_out, x_out = both("x_in"), both("xn_out"), both("x_out")
    list_out, list_base = c["list_out"], 16 * (GROUPS // 2) * (which - 1)
    wr_in, start = m.sem("wr_in"), m.sem("start")
    ve_ready, rstd_ready, shift_ready = both("ve_ready"), both("rstd_ready"), both("shift_ready")
    xn_ready, turned, kept0, kept1 = both("xn_ready"), both("turned"), both("kept0"), both("kept1")
    logits_ready, exp_in, exp_out = both("logits_ready"), both("exp_in"), both("exp_out")
    chosen_ready, places_ready, entries_ready = both("chosen_ready"), both("places_ready"), both("entries_ready")
    dve_done = m.sem("dve_done")
    if first_time:
        w32 = [m.sb(f"w32_{k}", [P, 2 * FFN]) for k in two]
        w_in, w_hi, w_lo = both("w_in"), both("w_hi"), both("w_lo")
        w_parts = (c["w1"], c["w2"])
    else:
        at = [m.sb(f"at{b}", [P, GROUP, D]) for b in two]
        atT = [m.sb(f"atT{h}", [P, KD, GTOK], FP16) for h in two]
        wout32 = m.sb("wout32", [P, KD, D])
        wout = m.sb("wout", [P, 2, KD, D], FP16)
        bout = m.sb("bout", [P, D])
        psP = [m.ps(f"psP{k}") for k in two]
        at_in, biased, at_turned = both("at_in"), both("biased"), both("at_turned")
        at_hi, at_lo, projected, x_ready = both("at_hi"), both("at_lo"), both("projected"), both("x_ready")
        wout_in, wout_hi, wout_lo = m.sem("wout_in"), m.sem("wout_hi"), m.sem("wout_lo")

    def groups(ap):
        return ap[0:TOK, :].rearrange("(g j p) d -> g p j d", p=P, j=GROUP)

    def group(ap, g):
        return groups(ap)[bass.ds(g, 1)].rearrange("a p j d -> p (a j) d")

    def at_group(g):
        return scratch["att"].rearrange("(g j p) d -> g p j d", p=P, j=GROUP)[bass.ds(g, 1)].rearrange(
            "a p j d -> p (a j) d")

    with nc.Block() as block:
        @block.sync
        def _(sp):
            sp.dma_start(wr[:, :, :], weights["wr"].rearrange("(k p) e -> p k e", p=P)).then_inc(wr_in, 16)
            if not first_time:
                for k in two:
                    for j in range(PAIRS):
                        sp.dma_start(wout32[j * HD:(j + 1) * HD, k, :],
                                     weights["wout"][(2 * j + k) * HD:(2 * j + k + 1) * HD, :]).then_inc(wout_in, 16)
                sp.dma_start(bout[:, :], weights["bout"].partition_broadcast(P)).then_inc(wout_in, 16)
            with sp.Fori(0, GROUPS // 2) as i:
                for b in two:
                    sp.wait_ge(x_out[b], 16 * i)
                    sp.dma_start(x[b][:, :, :], group(x_src, 2 * i + b)).then_inc(x_in[b], 16)
                    if first_time:
                        w, n = (weights["w1"], KD) if b == 0 else (weights["w2"], KF)
                        sp.wait_ge(w_hi[b], i)
                        sp.wait_ge(w_lo[b], i)
                        sp.dma_start(w32[b][:, :].rearrange("p (k n) -> p k n", k=n),
                                     w.rearrange("e (k p) n -> e p k n", p=P)[bass.ds(i, 1)].rearrange(
                                         "a p k n -> p (a k) n")).then_inc(w_in[b], 16)
                    else:
                        sp.wait_ge(at_turned[b], i)
                        sp.dma_start(at[b][:, :, :], at_group(2 * i + b)).then_inc(at_in[b], 16)

        @block.gpsimd
        def _(pool):
            pool.iota(c["token"][:, :], pattern=[[P, GROUP]], base=0, channel_multiplier=1,
                      allow_small_or_imprecise_dtypes=True).then_inc(start, 1)
            with pool.Fori(0, GROUPS // 2) as i:
                if not first_time:
                    for b in two:
                        pool.wait_ge(x_in[b], 16 * i + 16)
                        if b == 0:
                            pool.wait_ge(wout_in, 16 * (2 * PAIRS + 1))
                        for j in range(GROUP):
                            ins = pool.tensor_tensor(x[b][:, j, :], x[b][:, j, :], bout[:, :], ALU.add)
                        ins.then_inc(biased[b], 1)
                for b in two:
                    pool.wait_ge(ve_ready[b], i + 1)
                    pool.tensor_tensor(rstd[b][:, :], ve[b][:, :], c["power"][:, :], ALU.pow).then_inc(rstd_ready[b], 1)
                for b in two:
                    pool.wait_ge(entries_ready[b], i + 1)
                    pool.nop(nofuse=True)
                    for k in two:
                        for j in range(GROUP):
                            pool.indirect_dma_start(
                                out=list_d[:, :],
                                out_offset=bass.IndirectOffsetOnAxis(ap=slot_i[b][:, k, j:j + 1], axis=0),
                                in_=entry[b][:, k, j, :], in_offset=None).then_inc(list_out[b][k * GROUP + j], 16)
            for b in two:
                for s in list_out[b]:
                    pool.wait_ge(s, list_base + 16 * (GROUPS // 2))

        @block.scalar
        def _(act):
            if not first_time:
                act.wait_ge(wout_in, 16 * (2 * PAIRS + 1))
                act.activation(wout[:, 0, :, :], wout32[:, :, :], ACT.Copy, scale=W_ATT).then_inc(wout_hi, 1)
            with act.Fori(0, GROUPS // 2) as i:
                if not first_time:
                    for b in two:
                        act.wait_ge(at_turned[b], i + 1)
                        act.wait_ge(projected[1 - b], i + b)
                        for k in range(KD):
                            ins = act.activation(atT[0][:, k, :], psT[k][:, :], ACT.Copy)
                        ins.then_inc(at_hi[b], 1)
                for b in two:
                    act.wait_ge(shift_ready[b], i + 1)
                    act.wait_ge(xn_out[b], 16 * i)
                    for j in range(GROUP):
                        ins = act.activation(xn[b][:, j, :], x[b][:, j, :], ACT.Identity,
                                             scale=rstd[b][:, j:j + 1], bias=shift[b][:, j:j + 1])
                    ins.then_inc(xn_ready[b], 1)
                    act.wait_ge(xn_ready[b], i + 1)
                    act.dma_start(group(xn_d, 2 * i + b), xn[b][:, :, :]).then_inc(xn_out[b], 16)
                    act.dma_start(group(acc_d, 2 * i + b), x[b][:, :, :]).then_inc(x_out[b], 16)
                for b in two:
                    act.wait_ge(turned[b], i + 1)
                    act.wait_ge(logits_ready[b], i)
                    act.activation(xnT[b][:, 0, :], psT[0][:, :], ACT.Copy).then_inc(kept0[b], 1)
                    act.wait_ge(exp_in[b], i + 1)
                    act.activation(ex[b][:, :, :], ex[b][:, :, :], ACT.Exp).then_inc(exp_out[b], 1)
                    if first_time:
                        act.wait_ge(w_in[b], 16 * i + 16)
                        act.activation(w_parts[b][:, bass.ds(i, 1), 0, :].rearrange("p a n -> p (a n)"),
                                       w32[b][:, :], ACT.Copy, scale=W_FFN).then_inc(w_hi[b], 1)
            for b in two:
                act.wait_ge(xn_out[b], 16 * (GROUPS // 2))
                act.wait_ge(x_out[b], 16 * (GROUPS // 2))

        @block.tensor
        def _(pe):
            pe.wait_ge(wr_in, 16)
            if not first_time:
                pe.wait_ge(wout_lo, 1)
            with pe.Fori(0, GROUPS // 2) as i:
                if not first_time:
                    for b in two:
                        pe.wait_ge(at_in[b], 16 * i + 16)
                        if b == 0:
                            pe.wait_ge(kept0[1], i)
                            pe.wait_ge(kept1[1], i)
                        else:
                            pe.wait_ge(at_hi[0], i + 1)
                            pe.wait_ge(at_lo[0], i + 1)
                        for j in range(GROUP):
                            for k in range(KD):
                                ins = pe.transpose(psT[k][:, j * P:(j + 1) * P], at[b][:, j, k * P:(k + 1) * P],
                                                   c["ident"][:, :])
                        ins.then_inc(at_turned[b], 1)
                        pe.wait_ge(at_hi[b], i + 1)
                        pe.wait_ge(at_lo[b], i + 1)
                        for j in range(GROUP):
                            out = psP[j // 2][:, (j % 2) * D:(j % 2 + 1) * D]
                            if j % 2 == 0:
                                pe.wait_ge(x_ready[1 - b], i + b)
                            n = 0
                            for k in range(KD):
                                for ah, wh in ((0, 0), (0, 1), (1, 0)):
                                    ins = pe.matmul(out, atT[ah][:, k, j * P:(j + 1) * P], wout[:, wh, k, :],
                                                    start=(n == 0), stop=(n == 3 * KD - 1))
                                    n += 1
                        ins.then_inc(projected[b], 1)
                for b in two:
                    pe.wait_ge(xn_ready[b], i + 1)
                    if b == 0 and first_time:
                        pe.wait_ge(kept0[1], i)
                        pe.wait_ge(kept1[1], i)
                    elif b == 0:
                        pe.wait_ge(at_hi[1], i + 1)
                        pe.wait_ge(at_lo[1], i + 1)
                    else:
                        pe.wait_ge(kept0[0], i + 1)
                        pe.wait_ge(kept1[0], i + 1)
                    for j in range(GROUP):
                        for k in range(KD):
                            ins = pe.transpose(psT[k][:, j * P:(j + 1) * P], xn[b][:, j, k * P:(k + 1) * P],
                                               c["ident"][:, :])
                    ins.then_inc(turned[b], 1)
                    pe.wait_ge(kept0[b], i + 1)
                    pe.wait_ge(kept1[b], i + 1)
                    pe.wait_ge(entries_ready[b], i)
                    for j in range(GROUP):
                        for k in range(KD):
                            ins = pe.matmul(psR[b][:, j * EXPERTS:(j + 1) * EXPERTS], xnT[b][:, k, j * P:(j + 1) * P],
                                            wr[:, k, :], start=(k == 0), stop=(k == KD - 1))
                    ins.then_inc(logits_ready[b], 1)
                for b in two:
                    pe.wait_ge(chosen_ready[b], i + 1)
                    for j in range(GROUP):
                        out = psR[b][:, 64 + j * EXPERTS:64 + (j + 1) * EXPERTS]
                        pe.matmul(out, c["before"][:, :], chosen[b][:, j, :], start=True, stop=(j == 0))
                        for earlier in range(j):
                            pe.matmul(out, c["ones16"][:, :], chosen[b][:, earlier, :], start=False,
                                      stop=(earlier == j - 1))
                    for j in range(GROUP):
                        ins = pe.matmul(psR[b][:, 128:128 + EXPERTS], c["ones16"][:, :], chosen[b][:, j, :],
                                        start=(j == 0), stop=(j == GROUP - 1))
                    ins.then_inc(places_ready[b], 1)

        @block.vector
        def _(dve):
            lone = Chain(dve, dve_done)
            lone(dve.tensor_copy(run[:, :], c["base"][:, :]))
            dve.wait_ge(start, 1)
            if not first_time:
                dve.wait_ge(wout_hi, 1)
                dve.scalar_tensor_tensor(wout[:, 1, :, :], wout32[:, :, :], W_ATT, wout[:, 0, :, :],
                                         ALU.mult, ALU.subtract).then_inc(wout_lo, 1)

            def wide(t):
                return t.unsqueeze(2).to_broadcast([P, GROUP, EXPERTS])

            def over(t):
                return t[:, :].unsqueeze(1).to_broadcast([P, GROUP, EXPERTS])

            with dve.Fori(0, GROUPS // 2) as i:
                link = Chain(dve, dve_done, 1 + ROUTER_LINKS * i)
                for b in two:
                    if not first_time:
                        dve.wait_ge(at_hi[b], i + 1)
                        for k in range(KD):
                            ins = dve.tensor_tensor(atT[1][:, k, :], psT[k][:, :], atT[0][:, k, :], ALU.subtract)
                        ins.then_inc(at_lo[b], 1)
                        dve.wait_ge(projected[b], i + 1)
                        dve.wait_ge(biased[b], i + 1)
                        for h in range(GROUP // 2):
                            ins = dve.scalar_tensor_tensor(
                                x[b][:, 2 * h:2 * h + 2, :].rearrange("p j d -> p (j d)"), psP[h][:, :],
                                1.0 / W_ATT, x[b][:, 2 * h:2 * h + 2, :].rearrange("p j d -> p (j d)"),
                                ALU.mult, ALU.add)
                        ins.then_inc(x_ready[b], 1)
                        dve.wait_ge(x_ready[b], i + 1)
                for b in two:
                    dve.wait_ge(x_in[b], 16 * i + 16)
                    for j in range(GROUP):
                        ins = dve.bn_stats(stats[:, j, :], x[b][:, j, :])
                    link(ins)
                    dve.nop(nofuse=True)
                    for j in range(GROUP):
                        ins = dve.bn_aggr(mv[b][:, j, :], stats[:, j, :])
                    link(ins)
                    dve.tensor_scalar(ve[b][:, :], mv[b][:, :, 1], EPS, None, ALU.add).then_inc(ve_ready[b], 1)
                for b in two:
                    dve.wait_ge(rstd_ready[b], i + 1)
                    dve.scalar_tensor_tensor(shift[b][:, :], mv[b][:, :, 0], -1.0, rstd[b][:, :],
                                             ALU.mult, ALU.mult).then_inc(shift_ready[b], 1)
                for b in two:
                    dve.wait_ge(turned[b], i + 1)
                    dve.wait_ge(logits_ready[b], i)
                    dve.tensor_copy(xnT[b][:, 1, :], psT[1][:, :]).then_inc(kept1[b], 1)
                    dve.wait_ge(logits_ready[b], i + 1)
                    link(dve.tensor_copy(logits[:, :, :].rearrange("p j e -> p (j e)"),
                                         psR[b][:, 0:GROUP * EXPERTS]))
                    for k in two:
                        of = logits if k == 0 else rest
                        link(dve.tensor_reduce(best[:, k, :], of[:, :, :], AX.X, ALU.max))
                        link(dve.tensor_tensor(key[:, :, :], of[:, :, :], wide(best[:, k, :]), ALU.is_equal))
                        link(dve.tensor_tensor(key[:, :, :], key[:, :, :], over(c["first"]), ALU.mult))
                        link(dve.tensor_reduce(keymax[:, :], key[:, :, :], AX.X, ALU.max))
                        link(dve.tensor_tensor(pick[b][k][:, :, :], key[:, :, :], wide(keymax[:, :]), ALU.is_equal))
                        if k == 0:
                            link(dve.scalar_tensor_tensor(rest[:, :, :], pick[b][0][:, :, :], MASKED,
                                                          logits[:, :, :], ALU.mult, ALU.add))
                    dve.tensor_tensor(chosen[b][:, :, :], pick[b][0][:, :, :], pick[b][1][:, :, :],
                                      ALU.add).then_inc(chosen_ready[b], 1)
                    dve.tensor_tensor(ex[b][:, :, 0:EXPERTS], logits[:, :, :], wide(best[:, 0, :]), ALU.subtract)
                    dve.tensor_tensor(ex[b][:, :, EXPERTS], best[:, 1, :], best[:, 0, :],
                                      ALU.subtract).then_inc(exp_in[b], 1)
                    if first_time:
                        dve.wait_ge(w_hi[b], i + 1)
                        dve.scalar_tensor_tensor(
                            w_parts[b][:, bass.ds(i, 1), 1, :].rearrange("p a n -> p (a n)"), w32[b][:, :], W_FFN,
                            w_parts[b][:, bass.ds(i, 1), 0, :].rearrange("p a n -> p (a n)"),
                            ALU.mult, ALU.subtract).then_inc(w_lo[b], 1)
                    for s in list_out[b]:
                        dve.wait_ge(s, list_base + 16 * i)
                    dve.wait_ge(exp_out[b], i + 1)
                    link(dve.tensor_reduce(total[:, :], ex[b][:, :, 0:EXPERTS], AX.X, ALU.add))
                    link(dve.reciprocal(total[:, :], total[:, :]))
                    dve.tensor_scalar(entry[b][:, 0, :, 1].bitcast(FP32), total[:, :], GATE_SCALE, None, ALU.mult)
                    dve.scalar_tensor_tensor(entry[b][:, 1, :, 1].bitcast(FP32), ex[b][:, :, EXPERTS], GATE_SCALE,
                                             total[:, :], ALU.mult, ALU.mult)
                for b in two:
                    dve.wait_ge(places_ready[b], i + 1)
                    link(dve.tensor_tensor(place[:, :, :], psR[b][:, 64:64 + GROUP * EXPERTS].rearrange(
                        "p (j e) -> p j e", j=GROUP), over(run), ALU.add))
                    link(dve.tensor_tensor(run[:, :], run[:, :], psR[b][:, 128:128 + EXPERTS], ALU.add))
                    for k in two:
                        link(dve.tensor_tensor(placed[:, :, :], pick[b][k][:, :, :], place[:, :, :], ALU.mult))
                        link(dve.tensor_reduce(slot[:, :], placed[:, :, :], AX.X, ALU.add))
                        link(dve.tensor_copy(slot_i[b][:, k, :], slot[:, :]))
                        dve.tensor_copy(entry[b][:, k, :, 0], c["token"][:, :])
                    dve.tensor_scalar(c["token"][:, :], c["token"][:, :], float(GTOK), None,
                                      ALU.add).then_inc(entries_ready[b], 1)
                    dve.wait_ge(entries_ready[b], i + 1)
                assert link.n == ROUTER_LINKS, link.n
            dve.tensor_tensor(c["count"][:, :], run[:, :], c["base"][:, :], ALU.subtract).then_inc(dve_done, 1)
            dve.wait_ge(dve_done, ROUTER_LINKS * (GROUPS // 2) + 2)


SEARCH_BITS = 31
SEARCH_LINKS = 5


def table_phase(nc, ctx, c, scratch, which, cap=CAP):
    m = Memory(nc, ctx, f"table{which}")
    counts_i = m.sb("counts_i", [1, EXPERTS], I32)
    tiles_of = m.sb("tiles_of", [1, EXPERTS])
    last = m.sb("last", [1, EXPERTS])
    ones = m.sb("ones", [1, EXPERTS])
    tile = m.sb("tile", [1, TILES])
    expert = m.sb("expert", [1, TILES])
    begin = m.sb("begin", [1, TILES])
    step = m.sb("step", [1, TILES])
    live = m.sb("live", [1, TILES])
    most = m.sb("most", [1, 1])
    over_cap = m.sb("over_cap", [1, 1], I32)
    iotas, chain, tables_done = m.sem("iotas"), m.sem("chain"), m.sem("tables_done")
    S = TOK * EXPERTS // P
    entries = m.sb("entries", [P, S, 2], I32)
    gates = m.sb("gates", [P, S])
    above = m.sb("above", [P, S])
    equal = m.sb("equal", [P, S])
    rank = m.sb("rank", [P, S])
    one_row = m.sb("one_row", [P, S])
    same = m.sb("same", [P, P])
    earlier = m.sb("earlier", [P, P])
    bit = m.sb("bit", [P, 1], I32)
    one_i = m.sb("one_i", [P, 1], I32)
    floor_i = m.sb("floor_i", [P, 1], I32)
    guess = m.sb("guess", [P, 1], I32)
    in_row = m.sb("in_row", [P, 2])
    enough = m.sb("enough", [P, 1], I32)
    room = m.sb("room", [P, 1])
    ps = m.ps("ps", [P, 512])
    entries_in, entries_out = m.sem("entries_in"), m.sem("entries_out")
    rows_ready, sums_ready = m.sem("rows_ready"), m.sem("sums_ready")
    search, gates_done = m.sem("search"), m.sem("gates_done")
    pool_links = 10
    lists = scratch[f"list{which}"][0:LIST_PAD, :].rearrange("(p s) e -> p s e", p=P)

    with nc.Block() as block:
        @block.gpsimd
        def _(pool):
            link = Chain(pool, iotas)
            link(pool.iota(tile[:, :], pattern=[[1, TILES]], base=0, channel_multiplier=0,
                           allow_small_or_imprecise_dtypes=True))
            link(pool.memset(ones[:, :], 1.0))
            for t, least in ((same, 0), (earlier, 1)):
                v = t[:, :].rearrange("p (e r) -> p e r", r=P // EXPERTS)
                link(pool.memset(t[:, :], 1.0))
                link(pool.affine_select(out=v, in_=v, compare_op=ALU.is_ge, fill=0.0, base=0,
                                        pattern=[[-(P // EXPERTS), EXPERTS], [0, P // EXPERTS]],
                                        channel_multiplier=1))
                end = P // EXPERTS - 1 if least == 0 else -1
                link(pool.affine_select(out=v, in_=v, compare_op=ALU.is_ge, fill=0.0, base=end,
                                        pattern=[[P // EXPERTS, EXPERTS], [least, P // EXPERTS]],
                                        channel_multiplier=-1))
            link(pool.memset(one_row[:, :], 1.0))
            link(pool.memset(one_i[:, :], 1))
            assert link.n == pool_links, link.n

        @block.vector
        def _(dve):
            link = Chain(dve, chain)
            count = c["count"][0:1, :]
            dve.wait_ge(iotas, pool_links)
            link(dve.tensor_reduce(most[:, :], count, AX.X, ALU.max))
            link(dve.tensor_scalar(over_cap[:, :], most[:, :], float(cap), None, ALU.is_gt))
            link(dve.tensor_scalar(counts_i[:, :], count, float(SLOTS - 1), None, ALU.add))
            link(dve.tensor_scalar(counts_i[:, :], counts_i[:, :], SLOTS.bit_length() - 1, None,
                                   ALU.arith_shift_right))
            link(dve.tensor_copy(tiles_of[:, :], counts_i[:, :]))
            link(dve.tensor_tensor_scan(last[:, :], ones[:, :], tiles_of[:, :], 0.0, ALU.mult, ALU.add))
            link(dve.memset(expert[:, :], 0.0))
            link(dve.memset(begin[:, :], 0.0))
            for e in range(EXPERTS - 1):
                link(dve.tensor_scalar(step[:, :], tile[:, :], last[:, e:e + 1], None, ALU.is_ge))
                link(dve.tensor_tensor(expert[:, :], expert[:, :], step[:, :], ALU.add))
                link(dve.scalar_tensor_tensor(begin[:, :], step[:, :], tiles_of[:, e:e + 1], begin[:, :],
                                              ALU.mult, ALU.add))
            link(dve.tensor_tensor(begin[:, :], tile[:, :], begin[:, :], ALU.subtract))
            link(dve.tensor_scalar(begin[:, :], begin[:, :], float(SLOTS), float(-LIST_PAD), ALU.mult, ALU.add))
            link(dve.scalar_tensor_tensor(begin[:, :], expert[:, :], float(TOK), begin[:, :], ALU.mult, ALU.add))
            link(dve.tensor_scalar(live[:, :], tile[:, :], last[:, EXPERTS - 1:EXPERTS], None, ALU.is_lt))
            link(dve.tensor_tensor(begin[:, :], begin[:, :], live[:, :], ALU.mult))
            link(dve.tensor_scalar(c["start_of"][:, :], begin[:, :], float(LIST_PAD), None, ALU.add))
            link(dve.tensor_copy(c["expert_of"][:, :], expert[:, :]))
            dve.sem_inc(tables_done, 1)
            flag = dve.value_load(over_cap[0:1, 0:1], min_val=0, max_val=1)
            with dve.If(flag > 0):
                s = Chain(dve, search)
                dve.wait_ge(entries_in, 16)
                s(dve.tensor_copy(gates[:, :], entries[:, :, 1].bitcast(FP32)))
                s(dve.memset(floor_i[:, :], 0))
                s(dve.memset(bit[:, :], 1 << (SEARCH_BITS - 1)))
                with dve.Fori(0, SEARCH_BITS) as i:
                    t = Chain(dve, search, 3 + i * SEARCH_LINKS)
                    t(dve.tensor_tensor(guess[:, :], floor_i[:, :], bit[:, :], ALU.bitwise_or))
                    dve.tensor_scalar(above[:, :], gates[:, :], guess[:, :].bitcast(FP32), None, ALU.is_ge, ALU.add,
                                      accum_out=in_row[:, 0:1]).then_inc(rows_ready, 1)
                    dve.wait_ge(sums_ready, i + 1)
                    t(dve.tensor_scalar(enough[:, :], ps[:, 0:1], float(cap), -1.0, ALU.is_ge, ALU.mult))
                    t(dve.tensor_tensor(enough[:, :], enough[:, :], bit[:, :], ALU.bitwise_and))
                    t(dve.tensor_tensor(floor_i[:, :], floor_i[:, :], enough[:, :], ALU.bitwise_or))
                    t(dve.tensor_tensor(bit[:, :], bit[:, :], one_i[:, :], ALU.logical_shift_right))
                    assert t.n == SEARCH_LINKS
                s = Chain(dve, search, 3 + SEARCH_BITS * SEARCH_LINKS)
                level = floor_i[:, :].bitcast(FP32)
                s(dve.tensor_scalar(above[:, :], gates[:, :], level, None, ALU.is_gt, ALU.add,
                                    accum_out=in_row[:, 0:1]))
                s(dve.tensor_scalar(equal[:, :], gates[:, :], level, None, ALU.is_equal, ALU.add,
                                    accum_out=in_row[:, 1:2]))
                dve.sem_inc(rows_ready, 1)
                dve.wait_ge(sums_ready, SEARCH_BITS + 1)
                s(dve.tensor_scalar(room[:, :], ps[:, 0:1], -1.0, float(cap), ALU.mult, ALU.add))
                s(dve.tensor_tensor(room[:, :], room[:, :], ps[:, 1:2], ALU.subtract))
                s(dve.tensor_tensor_scan(rank[:, :], one_row[:, :], equal[:, :], 0.0, ALU.mult, ALU.add))
                s(dve.scalar_tensor_tensor(equal[:, :], rank[:, :], room[:, :], equal[:, :], ALU.is_le, ALU.mult))
                s(dve.tensor_tensor(above[:, :], above[:, :], equal[:, :], ALU.add))
                s(dve.tensor_tensor(entries[:, :, 1].bitcast(FP32), gates[:, :], above[:, :], ALU.mult))
                dve.sem_inc(gates_done, 1)

        @block.tensor
        def _(pe):
            pe.wait_ge(tables_done, 1)
            flag = pe.value_load(over_cap[0:1, 0:1], min_val=0, max_val=1)
            with pe.If(flag > 0):
                with pe.Fori(0, SEARCH_BITS) as i:
                    pe.wait_ge(rows_ready, i + 1)
                    pe.matmul(ps[:, 0:1], same[:, :], in_row[:, 0:1], start=True, stop=True).then_inc(sums_ready, 1)
                pe.wait_ge(rows_ready, SEARCH_BITS + 1)
                pe.matmul(ps[:, 0:1], same[:, :], in_row[:, 0:1], start=True, stop=True)
                pe.matmul(ps[:, 1:2], earlier[:, :], in_row[:, 1:2], start=True, stop=True).then_inc(sums_ready, 1)

        @block.sync
        def _(sp):
            sp.wait_ge(tables_done, 1)
            flag = sp.value_load(over_cap[0:1, 0:1], min_val=0, max_val=1)
            with sp.If(flag > 0):
                sp.dma_start(entries[:, :, :], lists).then_inc(entries_in, 16)
                sp.wait_ge(gates_done, 1)
                sp.dma_start(lists, entries[:, :, :]).then_inc(entries_out, 16)
                sp.wait_ge(entries_out, 16)


def ffn_phase(nc, ctx, c, scratch, which):
    m = Memory(nc, ctx, f"ffn{which}")
    xn_d, acc_d, list_d = scratch[f"xn{which}"], scratch[f"acc{which}"], scratch[f"list{which}"]
    two = range(2)
    PAIRS_F = KF // 2
    wanted = [m.sb(f"wanted{b}", [P, HALVES, 2], I32) for b in two]
    entry = [m.sb(f"entry{b}", [P, HALVES, 2], I32) for b in two]
    x = [m.sb(f"x{b}", [P, HALVES, D]) for b in two]
    xT = [[m.sb(f"xT{b}{h}", [P, KD, SLOTS], FP16) for h in two] for b in two]
    hT = [[m.sb(f"hT{b}{h}", [P, KF, SLOTS], FP16) for h in two] for b in two]
    y = [m.sb(f"y{b}", [P, HALVES, D]) for b in two]
    psT = m.ps("psT")
    psH = [m.ps(f"psH{f}") for f in range(PAIRS_F)]
    psY = [m.ps(f"psY{b}") for b in two]

    def both(name):
        return [m.sem(f"{name}{b}") for b in two]

    wanted_in = both("wanted_in")
    entry_in, turned, xT_hi, xT_lo = both("entry_in"), both("turned"), both("xT_hi"), both("xT_lo")
    summed, y_ready = both("summed"), both("y_ready")
    x_in, added = c["x_in"], c["added"]
    tiles_of_buffer = [(TILES + 1 - b) // 2 for b in two]
    base = [16 * n * (which - 1) for n in tiles_of_buffer]
    hidden = [m.sem(f"hidden{f}") for f in range(PAIRS_F)]
    h_hi = [m.sem(f"h_hi{f}") for f in range(PAIRS_F)]
    h_lo = [m.sem(f"h_lo{f}") for f in range(PAIRS_F)]
    turns = (TILES - 3) // 2
    assert TILES == 2 * turns + 3

    def tile_loop(eng, body):
        with eng.Fori(0, turns) as i:
            for b in two:
                body(2 * i + b, i, b)
        for n in range(2 * turns, TILES):
            body(n, n // 2, n % 2)

    def follows(n, by):
        return not isinstance(n, int) or n + by < TILES

    with nc.Block() as block:
        @block.sync
        def _(sp):
            def load_entries(dst, n, done):
                start = sp.value_load(c["start_of"][0:1, bass.ds(n, 1)], min_val=0, max_val=LIST_PAD)
                sp.dma_start(dst[:, :, :],
                             list_d[bass.ds(start, SLOTS), :].rearrange("(h p) e -> p h e", p=P)).then_inc(done, 16)

            def tile(n, i, b):
                if follows(n, 2):
                    for h in two:
                        sp.wait_ge(x_in[b][h], base[b] + 16 * i + 16)
                    load_entries(wanted[b], n + 2, wanted_in[b])
                for h in two:
                    sp.wait_ge(added[b][h], base[b] + 16 * i)
                load_entries(entry[b], n, entry_in[b])

            for b in two:
                load_entries(wanted[b], b, wanted_in[b])
            tile_loop(sp, tile)

        @block.gpsimd
        def _(pool):
            def gather(i, b):
                pool.wait_ge(wanted_in[b], 16 * i + 16)
                pool.wait_ge(turned[b], i)
                pool.nop(nofuse=True)
                for h in two:
                    pool.indirect_dma_start(
                        out=x[b][:, h, :], out_offset=None, in_=xn_d[:, :],
                        in_offset=bass.IndirectOffsetOnAxis(ap=wanted[b][:, h, 0:1], axis=0)
                    ).then_inc(x_in[b][h], 16)

            def tile(n, i, b):
                if follows(n, 2):
                    gather(i + 1, b)
                pool.wait_ge(y_ready[b], i + 1)
                pool.wait_ge(entry_in[b], 16 * i + 16)
                for h in two:
                    pool.wait_ge(added[1 - b][h], base[1 - b] + 16 * (i + b))
                pool.nop(nofuse=True)
                for h in two:
                    pool.indirect_dma_start(
                        out=acc_d[:, :], in_=y[b][:, h, :], in_offset=None, compute_op=ALU.add,
                        out_offset=bass.IndirectOffsetOnAxis(ap=entry[b][:, h, 0:1], axis=0)
                    ).then_inc(added[b][h], 16)

            for b in two:
                gather(0, b)
            tile_loop(pool, tile)
            for b in two:
                for h in two:
                    pool.wait_ge(added[b][h], base[b] + 16 * tiles_of_buffer[b])

        @block.tensor
        def _(pe):
            def turn_tokens(i, b):
                for h in two:
                    pe.wait_ge(x_in[b][h], base[b] + 16 * i + 16)
                pe.wait_ge(xT_hi[1 - b], i + b)
                pe.wait_ge(xT_lo[1 - b], i + b)
                for k in range(KD):
                    for h in two:
                        ins = pe.transpose(psT[:, k * SLOTS + h * P:k * SLOTS + (h + 1) * P],
                                           x[b][:, h, k * P:(k + 1) * P], c["ident"][:, :])
                ins.then_inc(turned[b], 1)

            def tile(n, i, b):
                e = pe.value_load(c["expert_of"][0:1, bass.ds(n, 1)], min_val=0, max_val=EXPERTS - 1)
                w1 = c["w1"][:, bass.ds(e, 1), :, :].rearrange("p a h n -> p (a h) n")
                w2 = c["w2"][:, bass.ds(e, 1), :, :].rearrange("p a h n -> p (a h) n")
                terms = ((0, 0), (0, 1), (1, 0))
                pe.wait_ge(xT_hi[b], i + 1)
                pe.wait_ge(xT_lo[b], i + 1)
                for f2 in range(PAIRS_F):
                    pe.wait_ge(h_hi[f2], n)
                    pe.wait_ge(h_lo[f2], n)
                    for f in two:
                        col = (2 * f2 + f) * P
                        for k in range(KD):
                            for wh, xh in terms:
                                ins = pe.matmul(psH[f2][:, f * SLOTS:(f + 1) * SLOTS],
                                                w1[:, wh, k * FFN + col:k * FFN + col + P], xT[b][xh][:, k, :],
                                                start=(k == 0 and (wh, xh) == terms[0]),
                                                stop=(k == KD - 1 and (wh, xh) == terms[-1]))
                    ins.then_inc(hidden[f2], 1)
                if follows(n, 1):
                    turn_tokens(i + b, 1 - b)
                pe.wait_ge(y_ready[b], i)
                for h in two:
                    for f in range(KF):
                        if h == 0 and f % 2 == 0:
                            pe.wait_ge(h_hi[f // 2], n + 1)
                            pe.wait_ge(h_lo[f // 2], n + 1)
                        for wh, hh in terms:
                            ins = pe.matmul(psY[b][:, h * D:(h + 1) * D], hT[b][hh][:, f, h * P:(h + 1) * P],
                                            w2[:, wh, f * D:(f + 1) * D],
                                            start=(f == 0 and (wh, hh) == terms[0]),
                                            stop=(f == KF - 1 and (wh, hh) == terms[-1]))
                ins.then_inc(summed[b], 1)

            turn_tokens(0, 0)
            tile_loop(pe, tile)

        @block.scalar
        def _(act):
            def tokens_hi(i, b):
                act.wait_ge(turned[b], i + 1)
                act.activation(xT[b][0][:, :, :].rearrange("p k n -> p (k n)"), psT[:, :],
                               ACT.Copy).then_inc(xT_hi[b], 1)

            def tile(n, i, b):
                for f2 in range(PAIRS_F):
                    act.wait_ge(hidden[f2], n + 1)
                    act.activation(hT[b][0][:, 2 * f2:2 * f2 + 2, :].rearrange("p f n -> p (f n)"),
                                   psH[f2][:, :], ACT.Relu).then_inc(h_hi[f2], 1)
                if follows(n, 1):
                    tokens_hi(i + b, 1 - b)
                act.wait_ge(summed[b], i + 1)
                act.wait_ge(entry_in[b], 16 * i + 16)
                for h in two:
                    act.wait_ge(added[b][h], base[b] + 16 * i)
                for h in two:
                    ins = act.activation(y[b][:, h, :], psY[b][:, h * D:(h + 1) * D], ACT.Copy,
                                         scale=entry[b][:, h, 1:2].bitcast(FP32))
                ins.then_inc(y_ready[b], 1)

            tokens_hi(0, 0)
            tile_loop(act, tile)

        @block.vector
        def _(dve):
            def tokens_lo(i, b):
                dve.wait_ge(xT_hi[b], i + 1)
                dve.tensor_tensor(xT[b][1][:, :, :].rearrange("p k n -> p (k n)"), psT[:, :],
                                  xT[b][0][:, :, :].rearrange("p k n -> p (k n)"),
                                  ALU.subtract).then_inc(xT_lo[b], 1)

            def tile(n, i, b):
                for f2 in range(PAIRS_F):
                    dve.wait_ge(h_hi[f2], n + 1)
                    dve.scalar_tensor_tensor(
                        hT[b][1][:, 2 * f2:2 * f2 + 2, :].rearrange("p f n -> p (f n)"), psH[f2][:, :], 0.0,
                        hT[b][0][:, 2 * f2:2 * f2 + 2, :].rearrange("p f n -> p (f n)"),
                        ALU.max, ALU.subtract).then_inc(h_lo[f2], 1)
                if follows(n, 1):
                    tokens_lo(i + b, 1 - b)

            tokens_lo(0, 0)
            tile_loop(dve, tile)


def qkv_phase(nc, ctx, c, scratch, weights):
    m = Memory(nc, ctx, "qkv")
    two = range(2)
    NG = 3 * D + 1
    x = [m.sb(f"x{b}", [P, GROUP, D]) for b in two]
    xn = [m.sb(f"xn{b}", [P, GROUP, D]) for b in two]
    xT = [[m.sb(f"xT{b}{h}", [P, KD, GTOK], FP16) for h in two] for b in two]
    stats = m.sb("stats", [P, GROUP, 6])
    mv = [m.sb(f"mv{b}", [P, GROUP, 2]) for b in two]
    ve = [m.sb(f"ve{b}", [P, GROUP]) for b in two]
    rstd = [m.sb(f"rstd{b}", [P, GROUP]) for b in two]
    shift = [m.sb(f"shift{b}", [P, GROUP]) for b in two]
    w32 = m.sb("w32", [P, KD, NG])
    w = m.sb("w", [P, 2, KD, NG + 1], FP16)
    bias_qk = m.sb("bias_qk", [P, 4])
    bias_v = m.sb("bias_v", [P, D])
    bias_g = m.sb("bias_g", [P, 1])
    qk = [m.sb(f"qk{b}", [P, 4, 2, GTOK], FP16) for b in two]
    v32 = [m.sb(f"v32{b}", [P, GROUP, D]) for b in two]
    vrow = [m.sb(f"vrow{b}", [P, GROUP, VROW], FP16) for b in two]
    z = [m.sb(f"z{b}", [P, GROUP]) for b in two]
    gate = [m.sb(f"gate{b}", [P, GROUP, 2]) for b in two]
    psT = [m.ps(f"psT{k}") for k in range(KD)]
    psQ = [m.ps(f"psQ{k}") for k in two]
    psV = [m.ps(f"psV{k}") for k in range(GROUP)]

    def both(name):
        return [m.sem(f"{name}{b}") for b in two]

    w_in, w_hi, w_lo, consts, chain = m.sem("w_in"), m.sem("w_hi"), m.sem("w_lo"), m.sem("consts"), m.sem("chain")
    x_in, ve_ready, rstd_ready, shift_ready, xn_ready = (
        both("x_in"), both("ve_ready"), both("rstd_ready"), both("shift_ready"), both("xn_ready"))
    turned, xT_hi, xT_lo = both("turned"), both("xT_hi"), both("xT_lo")
    qk_sum, qk_hi, qk_lo = both("qk_sum"), both("qk_hi"), both("qk_lo")
    qk_out, v_out, gate_out = both("qk_out"), both("v_out"), both("gate_out")
    v_sum, v_ready, v_hi, v_rows = both("v_sum"), both("v_ready"), both("v_hi"), both("v_rows")
    exp_ready, gate_ready = both("exp_ready"), both("gate_ready")
    turns = GROUPS // 2
    QKV_LINKS = 2 * 4

    def group(ap, g):
        return ap[0:TOK, :].rearrange("(g j p) d -> g p j d", p=P, j=GROUP)[bass.ds(g, 1)].rearrange(
            "a p j d -> p (a j) d")

    with nc.Block() as block:
        @block.sync
        def _(sp):
            sp.dma_start(w32[:, :, 0:3 * D], weights["wqkv"].rearrange("(k p) n -> p k n", p=P)).then_inc(w_in, 16)
            sp.dma_start(w32[:, :, 3 * D:NG], weights["wg"].rearrange("(k p) n -> p k n", p=P),
                         allow_slow_non_contiguous=True).then_inc(w_in, 16)
            sp.dma_start(bias_qk[:, :], weights["bqkv"][0:2 * D].rearrange("(c p) -> p c", p=P),
                         allow_slow_non_contiguous=True).then_inc(w_in, 16)
            sp.dma_start(bias_v[:, :], weights["bqkv"][2 * D:3 * D].partition_broadcast(P)).then_inc(w_in, 16)
            sp.dma_start(bias_g[:, :], weights["bg"].partition_broadcast(P)).then_inc(w_in, 16)
            with sp.Fori(0, turns) as i:
                for b in two:
                    sp.wait_ge(xn_ready[b], i)
                    sp.dma_start(x[b][:, :, :], group(scratch["acc1"], 2 * i + b)).then_inc(x_in[b], 16)
                for b in two:
                    tok = 2 * GTOK * i + GTOK * b
                    padded = tok + 2 * WINDOW * (i // (SEQ // GTOK // 2)) + WINDOW
                    for half in two:
                        rows = scratch["qs" if half == 0 else "ks"].rearrange("(h r p) t -> r p h t", h=2, p=P)
                        first = tok if half == 0 else padded
                        for r in range(KD):
                            n = 2 * half + r
                            sp.wait_ge(qk_hi[n % 2], 4 * i + 2 * b + n // 2 + 1)
                            sp.wait_ge(qk_lo[n % 2], 4 * i + 2 * b + n // 2 + 1)
                            sp.dma_start(rows[r][:, :, bass.ds(first, GTOK)], qk[b][:, n, :, :]).then_inc(qk_out[b], 16)
                    sp.wait_ge(v_rows[b], i + 1)
                    sp.dma_start(scratch["vs"][bass.ds(padded, GTOK), :].rearrange("(j p) n -> p j n", p=P),
                                 vrow[b][:, :, :]).then_inc(v_out[b], 16)
                    sp.wait_ge(gate_ready[b], i + 1)
                    sp.dma_start(group(scratch["gate"], 2 * i + b), gate[b][:, :, :]).then_inc(gate_out[b], 16)
            for b in two:
                sp.wait_ge(qk_out[b], 64 * turns)
                sp.wait_ge(v_out[b], 16 * turns)
                sp.wait_ge(gate_out[b], 16 * turns)

        @block.gpsimd
        def _(pool):
            for b in two:
                ins = pool.memset(vrow[b][:, :, :], 0.0)
            ins.then_inc(consts, 1)
            pool.wait_ge(consts, 1)
            for b in two:
                for j in range(GROUP):
                    ones = vrow[b][:, j, :].rearrange("p (r h a n) -> p r h a n", r=PAIRS, h=2, a=2)
                    ins = pool.memset(ones[:, :, 0, :, HD], 1.0)
            ins.then_inc(consts, 1)
            pool.wait_ge(consts, 2)
            with pool.Fori(0, turns) as i:
                for b in two:
                    pool.wait_ge(ve_ready[b], i + 1)
                    pool.tensor_tensor(rstd[b][:, :], ve[b][:, :], c["power"][:, :], ALU.pow).then_inc(rstd_ready[b], 1)
                for b in two:
                    pool.wait_ge(v_ready[b], i + 1)
                    pool.wait_ge(v_out[b], 16 * i)
                    pool.nop(nofuse=True)
                    for part in two:
                        for j in range(GROUP):
                            rows = vrow[b][:, j, :].rearrange("p (r h a n) -> p r h a n", r=PAIRS, h=2, a=2)
                            hi, lo = rows[:, :, 0, :, 0:HD], rows[:, :, 1, :, 0:HD]
                            v = v32[b][:, j, :].rearrange("p (r a n) -> p r a n", r=PAIRS, a=2)
                            if part == 0:
                                ins = pool.tensor_copy(hi, v)
                            else:
                                ins = pool.tensor_tensor(lo, v, hi, ALU.subtract)
                        if part == 0:
                            ins.then_inc(v_hi[b], 1)
                            pool.wait_ge(v_hi[b], i + 1)
                    ins.then_inc(v_rows[b], 1)

        @block.scalar
        def _(act):
            act.wait_ge(w_in, 80)
            act.activation(w[:, 0, :, 0:NG], w32[:, :, :], ACT.Copy, scale=W_ATT).then_inc(w_hi, 1)
            with act.Fori(0, turns) as i:
                for b in two:
                    act.wait_ge(shift_ready[b], i + 1)
                    act.wait_ge(turned[b], i)
                    for j in range(GROUP):
                        ins = act.activation(xn[b][:, j, :], x[b][:, j, :], ACT.Identity,
                                             scale=rstd[b][:, j:j + 1], bias=shift[b][:, j:j + 1])
                    ins.then_inc(xn_ready[b], 1)
                for b in two:
                    act.wait_ge(turned[b], i + 1)
                    for k in range(KD):
                        ins = act.activation(xT[b][0][:, k, :], psT[k][:, :], ACT.Copy)
                    ins.then_inc(xT_hi[b], 1)
                    act.wait_ge(qk_out[b], 64 * i)
                    for n in range(4):
                        act.wait_ge(qk_sum[n % 2], 4 * i + 2 * b + n // 2 + 1)
                        act.activation(qk[b][:, n, 0, :], psQ[n % 2][:, :], ACT.Identity,
                                       bias=bias_qk[:, n:n + 1]).then_inc(qk_hi[n % 2], 1)
                    act.wait_ge(v_ready[b], i + 1)
                    for j in range(GROUP):
                        ins = act.activation(z[b][:, j:j + 1], psV[j][:, D:D + 1], ACT.Exp, scale=-1.0 / W_ATT,
                                             bias=bias_g[:, :])
                    ins.then_inc(exp_ready[b], 1)

        @block.tensor
        def _(pe):
            pe.wait_ge(w_lo, 1)
            terms = ((0, 0), (0, 1), (1, 0))
            with pe.Fori(0, turns) as i:
                for b in two:
                    pe.wait_ge(xn_ready[b], i + 1)
                    pe.wait_ge(xT_hi[1 - b], i + b)
                    pe.wait_ge(xT_lo[1 - b], i + b)
                    for j in range(GROUP):
                        for k in range(KD):
                            ins = pe.transpose(psT[k][:, j * P:(j + 1) * P], xn[b][:, j, k * P:(k + 1) * P],
                                               c["ident"][:, :])
                    ins.then_inc(turned[b], 1)
                    pe.wait_ge(xT_hi[b], i + 1)
                    pe.wait_ge(xT_lo[b], i + 1)
                    for n in range(4):
                        pe.wait_ge(qk_hi[n % 2], 4 * i + 2 * b + n // 2)
                        pe.wait_ge(qk_lo[n % 2], 4 * i + 2 * b + n // 2)
                        for k in range(KD):
                            for wh, xh in terms:
                                ins = pe.matmul(psQ[n % 2][:, :], w[:, wh, k, n * P:(n + 1) * P], xT[b][xh][:, k, :],
                                                start=(k == 0 and (wh, xh) == terms[0]),
                                                stop=(k == KD - 1 and (wh, xh) == terms[-1]))
                        ins.then_inc(qk_sum[n % 2], 1)
                    pe.wait_ge(v_ready[1 - b], i + b)
                    pe.wait_ge(exp_ready[1 - b], i + b)
                    for j in range(GROUP):
                        for k in range(KD):
                            for wh, xh in terms:
                                ins = pe.matmul(psV[j][:, 0:D + 1], xT[b][xh][:, k, j * P:(j + 1) * P],
                                                w[:, wh, k, 2 * D:NG],
                                                start=(k == 0 and (wh, xh) == terms[0]),
                                                stop=(k == KD - 1 and (wh, xh) == terms[-1]))
                    ins.then_inc(v_sum[b], 1)

        @block.vector
        def _(dve):
            dve.wait_ge(w_hi, 1)
            dve.scalar_tensor_tensor(w[:, 1, :, 0:NG], w32[:, :, :], W_ATT, w[:, 0, :, 0:NG],
                                     ALU.mult, ALU.subtract).then_inc(w_lo, 1)
            first = Chain(dve, chain)
            first(dve.tensor_scalar(bias_qk[:, :], bias_qk[:, :], W_ATT, None, ALU.mult))
            first(dve.tensor_scalar(bias_g[:, :], bias_g[:, :], -1.0, None, ALU.mult))
            dve.wait_ge(w_lo, 1)
            with dve.Fori(0, turns) as i:
                link = Chain(dve, chain, 2 + QKV_LINKS * i)
                for b in two:
                    dve.wait_ge(x_in[b], 16 * i + 16)
                    for j in range(GROUP):
                        ins = dve.bn_stats(stats[:, j, :], x[b][:, j, :])
                    link(ins)
                    dve.nop(nofuse=True)
                    for j in range(GROUP):
                        ins = dve.bn_aggr(mv[b][:, j, :], stats[:, j, :])
                    link(ins)
                    dve.tensor_scalar(ve[b][:, :], mv[b][:, :, 1], EPS, None, ALU.add).then_inc(ve_ready[b], 1)
                for b in two:
                    dve.wait_ge(rstd_ready[b], i + 1)
                    dve.scalar_tensor_tensor(shift[b][:, :], mv[b][:, :, 0], -1.0, rstd[b][:, :],
                                             ALU.mult, ALU.mult).then_inc(shift_ready[b], 1)
                for b in two:
                    dve.wait_ge(xT_hi[b], i + 1)
                    for k in range(KD):
                        ins = dve.tensor_tensor(xT[b][1][:, k, :], psT[k][:, :], xT[b][0][:, k, :], ALU.subtract)
                    ins.then_inc(xT_lo[b], 1)
                    for n in range(4):
                        dve.wait_ge(qk_hi[n % 2], 4 * i + 2 * b + n // 2 + 1)
                        dve.scalar_tensor_tensor(qk[b][:, n, 1, :], psQ[n % 2][:, :], bias_qk[:, n:n + 1],
                                                 qk[b][:, n, 0, :], ALU.add, ALU.subtract).then_inc(qk_lo[n % 2], 1)
                    dve.wait_ge(v_sum[b], i + 1)
                    dve.wait_ge(v_rows[b], i)
                    for j in range(GROUP):
                        ins = dve.scalar_tensor_tensor(v32[b][:, j, :], psV[j][:, 0:D], 1.0 / W_ATT, bias_v[:, :],
                                                       ALU.mult, ALU.add)
                    ins.then_inc(v_ready[b], 1)
                    dve.wait_ge(exp_ready[b], i + 1)
                    dve.wait_ge(gate_out[b], 16 * i)
                    link(dve.tensor_scalar(z[b][:, :], z[b][:, :], 1.0, None, ALU.add))
                    link(dve.reciprocal(gate[b][:, :, 1], z[b][:, :]))
                    dve.tensor_scalar(gate[b][:, :, 0], gate[b][:, :, 1], -1.0, 1.0,
                                      ALU.mult, ALU.add).then_inc(gate_ready[b], 1)
                assert link.n == QKV_LINKS, link.n


def attention_phase(nc, ctx, c, scratch):
    m = Memory(nc, ctx, "att")
    two = range(2)
    TILES_S = SPAN // QT
    BODY = 2 * QUADS
    TURNS = SPANS // 2
    UNITS = PAIRS // 2
    q = [m.sb(f"q{b}", [P, PAIRS, TILES_S, 2, QT], FP16) for b in two]
    k = [m.sb(f"k{b}", [P, PAIRS, SPAN_K + N_GLOBAL], FP16) for b in two]
    v0 = [m.sb(f"v0{b}", [P, TILES_S, VROW], FP16) for b in two]
    v1 = [m.sb(f"v1{b}", [P, TILES_S, 2, VROW], FP16) for b in two]
    gate = [m.sb(f"gate{b}", [P, TILES_S, 2]) for b in two]
    most = [m.sb(f"most{b}", [P, UNITS, 2]) for b in two]
    shift = [m.sb(f"shift{b}", [P, UNITS, 2]) for b in two]
    prob = [m.sb(f"prob{b}", [P, UNITS, KEYS]) for b in two]
    probT = [[[m.sb(f"probT{b}{n}{h}", [P, 2, 2, P], FP16) for h in two] for n in two] for b in two]
    share = m.sb("share", [P, UNITS, 2])
    parts = m.sb("parts", [P, UNITS, 2, HD])
    out = [m.sb(f"out{b}", [P, 2, UNITS, HD]) for b in two]
    psS = [m.ps(f"psS{b}", [P, UNITS, KEYS]) for b in two]
    psT = [m.ps(f"psT{n}", [P, 2, 2, P]) for n in two]
    psO = [m.ps(f"psO{b}", [P, 512]) for b in two]

    def both(name):
        return [m.sem(f"{name}{b}") for b in two]

    cleared, loaded = m.sem("cleared"), both("loaded")
    scored, reduced, maxed, exped = both("scored"), both("reduced"), both("maxed"), both("exped")
    inverted, shared = both("inverted"), both("shared")
    turned = [both(f"turned{n}") for n in two]
    p_hi = [both(f"p_hi{n}") for n in two]
    p_lo = [both(f"p_lo{n}") for n in two]
    summed, taken, stored, out_ready = both("summed"), both("taken"), both("stored"), both("out_ready")
    LOADS = 6 * (TILES_S + 2) + 4 + TILES_S + 2

    def quad(i, s):
        i, s = i + s // BODY, s % BODY
        return i, s, s % 2, (BODY // 2) * i + s // 2

    def exists(i, s):
        return not isinstance(i, int) or i * BODY + s < TURNS * BODY

    def quad_loop(eng, step):
        with eng.Fori(0, TURNS - 1) as i:
            for s in range(BODY):
                step(i, s)
        for s in range(BODY):
            step(TURNS - 1, s)

    with nc.Block() as block:
        @block.gpsimd
        def _(pool):
            link = Chain(pool, cleared)
            for b in two:
                pool.memset(q[b][:, :, :, :, :], 0.0)
                pool.memset(v1[b][:, :, :, :], 0.0)
                link(pool.memset(k[b][:, :, :], 0.0))
                for h in two:
                    one = q[b][QT * h:QT * h + QT, :, :, h, :].rearrange("p r t n -> p (r t) n")
                    link(pool.affine_select(out=one, in_=one, compare_op=ALU.not_equal, fill=PAD_Q,
                                            base=-3 * HD, pattern=[[0, PAIRS * TILES_S], [0, QT]], channel_multiplier=1))
            with pool.Fori(0, TURNS) as i:
                for b in two:
                    for t in range(TILES_S):
                        pool.wait_ge(out_ready[b], TILES_S * i + t + 1)
                        for a in two:
                            pool.dma_start(scratch["att"][bass.ds(2 * SPAN * i + SPAN * b + QT * t, QT), a * P:(a + 1) * P],
                                           out[t % 2][QT * a:QT * a + QT, :, :, :].rearrange("p h u n -> p (h u n)")
                                           ).then_inc(stored[t % 2], 16)
            for n in two:
                pool.wait_ge(stored[n], 32 * SPANS * TILES_S // 2)

        @block.sync
        def _(sp):
            sp.wait_ge(cleared, 6)
            qs = scratch["qs"].rearrange("(h r a d) t -> h a d r t", h=2, a=2, d=HD)
            ks = scratch["ks"].rearrange("(h r a d) t -> h a d r t", h=2, a=2, d=HD)
            vs = scratch["vs"]
            with sp.Fori(0, TURNS) as i:
                for b in two:
                    batch = i // (SEQ // SPAN // 2)
                    tok = 2 * SPAN * i + SPAN * b
                    first = tok + 2 * WINDOW * batch
                    at = 2 * SPAN * (i % (SEQ // SPAN // 2)) + SPAN * b
                    globals_ = SEQP * batch + WINDOW
                    sp.wait_ge(out_ready[b], TILES_S * i)
                    n = 0
                    for a in two:
                        for part, (qh, kh) in enumerate(((0, 0), (0, 1), (1, 0))):
                            r0 = QT * a + HD * part
                            for t in range(TILES_S):
                                sp.dma_start(q[b][r0:r0 + HD, :, t, a, :],
                                             qs[qh, a][:, :, bass.ds(tok + QT * t, QT)]).then_inc(loaded[b], 16)
                            sp.dma_start(k[b][r0:r0 + HD, :, 0:SPAN_K], ks[kh, a][:, :, bass.ds(first, SPAN_K)]
                                         ).then_inc(loaded[b], 16)
                            sp.dma_start(k[b][r0:r0 + HD, :, SPAN_K:SPAN_K + N_GLOBAL],
                                         ks[kh, a][:, :, bass.ds(globals_, N_GLOBAL)]).then_inc(loaded[b], 16)
                            n += TILES_S + 2
                        r0 = QT * a + 3 * HD
                        sp.dma_start(k[b][r0:r0 + 1, :, 0:SPAN_K],
                                     scratch["padk"][0:1, bass.ds(at, SPAN_K)].unsqueeze(1).to_broadcast(
                                         [1, PAIRS, SPAN_K])).then_inc(loaded[b], 16)
                        sp.dma_start(gate[b][QT * a:QT * a + QT, :, :],
                                     scratch["gate"][bass.ds(tok, SPAN), :].rearrange("(t q) e -> q t e", q=QT)
                                     ).then_inc(loaded[b], 16)
                        n += 2
                    for t in range(TILES_S):
                        sp.dma_start(v0[b][:, t, :], vs[bass.ds(first + QT * t, P), :]).then_inc(loaded[b], 16)
                    sp.dma_start(v1[b][0:QT, :, 0, :],
                                 vs[bass.ds(first + P, SPAN), :].rearrange("(t p) n -> p t n", p=QT)).then_inc(loaded[b], 16)
                    sp.dma_start(v1[b][QT:P, :, 1, :],
                                 vs[bass.ds(globals_, N_GLOBAL), :].unsqueeze(1).to_broadcast(
                                     [N_GLOBAL, TILES_S, VROW])).then_inc(loaded[b], 16)
                    n += TILES_S + 2
                    assert n == LOADS, n

        @block.tensor
        def _(pe):
            def scores(i, s):
                i, s, b, n = quad(i, s)
                sb, t, half = s // QUADS, s % QUADS // 2, s % 2
                if s % QUADS == 0:
                    pe.wait_ge(loaded[sb], 16 * LOADS * i + 16 * LOADS)
                pe.wait_ge(exped[b], n)
                for u in range(UNITS):
                    r = half * UNITS + u
                    if u % 2 == 0:
                        pe.matmul(psS[b][:, u:u + 2, :].rearrange("p u n -> p (u n)"), c["ident16"][:, :],
                                  c["mask"][:, :, :].rearrange("p u n -> p (u n)"), start=True, stop=True)
                    lhs = q[sb][:, r, t, :, :].rearrange("p a n -> p (a n)")
                    pe.matmul(psS[b][:, u, 0:LOCAL], lhs, k[sb][:, r, t * QT:t * QT + LOCAL],
                              start=False, stop=True, skip_group_check=True)
                    ins = pe.matmul(psS[b][:, u, LOCAL:KEYS], lhs, k[sb][:, r, SPAN_K:SPAN_K + N_GLOBAL],
                                    start=False, stop=True, skip_group_check=True)
                ins.then_inc(scored[b], 1)

            def turn(i, s):
                i, s, b, n = quad(i, s)
                pe.wait_ge(exped[b], n + 1)
                for h in two:
                    pe.wait_ge(p_lo[h][1 - b], n + b)
                    for u in two:
                        for blk in two:
                            ins = pe.transpose(psT[h][:, u, blk, :],
                                               prob[b][:, 2 * h + u, blk * P:(blk + 1) * P], c["ident"][:, :])
                    ins.then_inc(turned[h][b], 1)

            def values(i, s):
                i, s, b, n = quad(i, s)
                sb, t, half = s // QUADS, s % QUADS // 2, s % 2
                pe.wait_ge(taken[b], n)
                for u in range(UNITS):
                    if u % 2 == 0:
                        pe.wait_ge(p_hi[u // 2][b], n + 1)
                        pe.wait_ge(p_lo[u // 2][b], n + 1)
                    r = half * UNITS + u
                    pT = probT[b][u // 2]
                    o = psO[b][:, u * 2 * VW:(u + 1) * 2 * VW]
                    for step, (ph, vh) in enumerate(((0, 0), (0, 1), (1, 0))):
                        col = (2 * r + vh) * VW
                        pe.matmul(o, pT[ph][:, u % 2, 1, :], v1[sb][:, t, :, col:col + VW],
                                  start=(step == 0), stop=(step == 2))
                    for step, (ph, vh) in enumerate(((0, 0), (0, 1), (1, 0))):
                        col = (2 * r + vh) * VW
                        ins = pe.matmul(o[:, 0:VW], pT[ph][:, u % 2, 0, :], v0[sb][:, t, col:col + VW],
                                        start=False, stop=True, skip_group_check=True)
                ins.then_inc(summed[b], 1)

            scores(0, 0)
            scores(0, 1)
            turn(0, 0)

            def step(i, s):
                if exists(i, s + 2):
                    scores(i, s + 2)
                if exists(i, s + 1):
                    turn(i, s + 1)
                values(i, s)
            quad_loop(pe, step)

        @block.scalar
        def _(act):
            def exps(i, s):
                i, s, b, n = quad(i, s)
                act.wait_ge(maxed[b], n + 1)
                act.wait_ge(turned[1][b], n)
                for u in range(UNITS):
                    for seg, (lo, hi) in enumerate(((0, LOCAL), (LOCAL, KEYS))):
                        ins = act.activation(prob[b][:, u, lo:hi], psS[b][:, u, lo:hi], ACT.Exp, scale=SCORE_SCALE,
                                             bias=shift[b][:, u, seg:seg + 1])
                ins.then_inc(exped[b], 1)

            def high(i, s):
                i, s, b, n = quad(i, s)
                for h in two:
                    act.wait_ge(turned[h][b], n + 1)
                    act.activation(probT[b][h][0][:, :, :, :].rearrange("p u k n -> p (u k n)"),
                                   psT[h][:, :, :, :].rearrange("p u k n -> p (u k n)"),
                                   ACT.Copy).then_inc(p_hi[h][b], 1)

            exps(0, 0)
            exps(0, 1)

            def step(i, s):
                high(i, s)
                if exists(i, s + 2):
                    exps(i, s + 2)
            quad_loop(act, step)

        @block.vector
        def _(dve):
            def maxima(i, s):
                i, s, b, n = quad(i, s)
                dve.wait_ge(scored[b], n + 1)
                dve.tensor_reduce(most[b][:, :, 0], psS[b][:, :, 0:LOCAL], AX.X, ALU.max)
                dve.tensor_reduce(most[b][:, :, 1], psS[b][:, :, LOCAL:KEYS], AX.X, ALU.max).then_inc(reduced[b], 1)
                dve.wait_ge(reduced[b], n + 1)
                dve.tensor_scalar(shift[b][:, :, :], most[b][:, :, :], -SCORE_SCALE, None, ALU.mult).then_inc(maxed[b], 1)

            def low(i, s):
                i, s, b, n = quad(i, s)
                for h in two:
                    dve.wait_ge(p_hi[h][b], n + 1)
                    dve.tensor_tensor(probT[b][h][1][:, :, :, :].rearrange("p u k n -> p (u k n)"),
                                      psT[h][:, :, :, :].rearrange("p u k n -> p (u k n)"),
                                      probT[b][h][0][:, :, :, :].rearrange("p u k n -> p (u k n)"),
                                      ALU.subtract).then_inc(p_lo[h][b], 1)

            def outputs(i, s):
                i, s, b, n = quad(i, s)
                sb, t, half = s // QUADS, s % QUADS // 2, s % 2
                sums = psO[b][:, 0:UNITS * 2 * VW].rearrange("p (u g n) -> p u g n", u=UNITS, g=2)
                dve.wait_ge(summed[b], n + 1)
                for a in two:
                    rows = slice(QT * a, QT * a + QT)
                    ins = dve.reciprocal(share[rows, :, :], sums[rows, :, :, (HD + 1) * a + HD])
                ins.then_inc(inverted[b], 1)
                dve.wait_ge(inverted[b], n + 1)
                dve.tensor_tensor(share[:, :, :], share[:, :, :],
                                  gate[sb][:, t, :].unsqueeze(1).to_broadcast([P, UNITS, 2]),
                                  ALU.mult).then_inc(shared[b], 1)
                dve.wait_ge(shared[b], n + 1)
                for a in two:
                    rows = slice(QT * a, QT * a + QT)
                    ins = dve.tensor_tensor(parts[rows, :, :, :], sums[rows, :, :, (HD + 1) * a:(HD + 1) * a + HD],
                                            share[rows, :, :].unsqueeze(3).to_broadcast([QT, UNITS, 2, HD]), ALU.mult)
                ins.then_inc(taken[b], 1)
                dve.wait_ge(taken[b], n + 1)
                if half == 0:
                    dve.wait_ge(stored[t % 2], 32 * (4 * i + 2 * sb + t // 2))
                ins = dve.tensor_tensor(out[t % 2][:, half, :, :], parts[:, :, 0, :], parts[:, :, 1, :], ALU.add)
                if half == 1:
                    ins.then_inc(out_ready[sb], 1)

            maxima(0, 0)
            maxima(0, 1)

            def step(i, s):
                low(i, s)
                if exists(i, s + 2):
                    maxima(i, s + 2)
                outputs(i, s)
            quad_loop(dve, step)


def copy_phase(nc, ctx, scratch, out):
    m = Memory(nc, ctx, "copy")
    copied = m.sem("copied")
    PIECES = 8
    rows = TOK // PIECES
    with nc.Block() as block:
        @block.sync
        def _(sp):
            for n in range(PIECES):
                sp.dma_start(out[n * rows:(n + 1) * rows, :].rearrange("(p r) d -> p (r d)", p=P),
                             scratch["acc2"][n * rows:(n + 1) * rows, :].rearrange("(p r) d -> p (r d)", p=P)
                             ).then_inc(copied, 16)
            sp.wait_ge(copied, 16 * PIECES)


def macaron(nc, x, wqkv, bqkv, wout, bout, wg, bg, wr, w1, w2, out):
    scratch = {}

    def dram(name, shape, dt=FP32):
        scratch[name] = nc.dram_tensor(f"scratch_{name}", shape, dt, kind="Internal").ap()

    for which in (1, 2):
        dram(f"xn{which}", [TOK + SLOTS, D])
        dram(f"acc{which}", [TOK + SLOTS, D])
        dram(f"list{which}", [LIST_PAD + SLOTS, 2], I32)
    dram("qs", [2 * D, TOK], FP16)
    dram("ks", [2 * D, BATCH * SEQP], FP16)
    dram("vs", [BATCH * SEQP, VROW], FP16)
    dram("padk", [1, SEQP], FP16)
    dram("gate", [TOK, 2])
    dram("att", [TOK, D])
    weights = dict(wqkv=wqkv, bqkv=bqkv, wout=wout, bout=bout, wg=wg, bg=bg, wr=wr, w1=w1, w2=w2)
    with ExitStack() as ctx:
        c = constants(Memory(nc, ctx, "const"))

        def phase(build, *args):
            with ExitStack() as inner:
                build(nc, inner, *args)

        phase(fill_phase, c, scratch)
        phase(router_phase, c, scratch, 1, x.rearrange("b t d -> (b t) d"), weights)
        phase(table_phase, c, scratch, 1)
        phase(ffn_phase, c, scratch, 1)
        phase(qkv_phase, c, scratch, weights)
        clear_semaphores(nc)
        phase(attention_phase, c, scratch)
        phase(router_phase, c, scratch, 2, scratch["acc1"], weights)
        phase(table_phase, c, scratch, 2)
        phase(ffn_phase, c, scratch, 2)
        phase(copy_phase, scratch, out.rearrange("b t d -> (b t) d"))


_INS = ["L0_attn_hidden_states", "L0_attn_Wqkv", "L0_attn_bqkv", "L0_attn_Wout", "L0_attn_bout", "L0_attn_Wg",
        "L0_attn_bg", "L0_ffn_Wr", "L0_ffn_W1", "L0_ffn_W2"]


def kernel(**inputs):
    import numpy as np
    import concourse.bacc as bacc
    from concourse.bass_utils import run_bass_kernel_spmd

    nc = bacc.Bacc("TRN2", target_bir_lowering=False, num_devices=1)
    arrays, args = {}, []
    for name in _INS:
        a = np.ascontiguousarray(inputs[name])
        arrays[f"in_{name}"] = a
        args.append(nc.dram_tensor(f"in_{name}", a.shape, mybir.dt.from_np(a.dtype), kind="ExternalInput").ap())
    out = nc.dram_tensor("out", (BATCH, SEQ, D), FP32, kind="ExternalOutput").ap()
    macaron(nc, *args, out)
    r = run_bass_kernel_spmd(nc, [arrays], core_ids=[0])
    return r.results[0]["out"]
```

```python
import concourse.bass as bass
from concourse import mybir
from contextlib import ExitStack

FP32, FP16, BF16, I32 = mybir.dt.float32, mybir.dt.float16, mybir.dt.bfloat16, mybir.dt.int32
ALU = mybir.AluOpType
ACT = mybir.ActivationFunctionType
AX = mybir.AxisListType

P = 128
BATCH, SEQ, D = 4, 2048, 256
TOK = BATCH * SEQ
HEADS, HD = 16, 16
PAIRS = HEADS // 2
WINDOW = 64
N_GLOBAL = 64
EXPERTS, FFN, TOP_K = 8, 1024, 2
CAP = -(-TOK * TOP_K * 5 // (4 * EXPERTS))
EPS = 1e-5
KD = D // P
KF = FFN // P

GROUP = 4
GTOK = GROUP * P
GROUPS = TOK // GTOK

SLOTS = 256
HALVES = SLOTS // P
TILES = (TOK * TOP_K + EXPERTS * (SLOTS - 1)) // SLOTS
LIST_PAD = EXPERTS * TOK

SEQP = SEQ + 2 * WINDOW
QT = 64
SPAN = 4 * QT
SPAN_K = SPAN + 2 * WINDOW
SPANS = TOK // SPAN
LOCAL = QT + 2 * WINDOW
KEYS = LOCAL + N_GLOBAL
VW = 2 * (HD + 1)
VROW = PAIRS * 2 * VW

W_FFN = 32.0
W_ATT = 4.0
GATE_SCALE = 0.5 / (W_FFN * W_FFN)
SCORE_SCALE = HD ** -0.5 / (W_ATT * W_ATT)
PAD_Q, PAD_K = 60000.0, -60000.0
MASKED = -1e30


class Memory:

    semaphores = []

    def __init__(self, nc, ctx, phase):
        self.nc, self.ctx, self.phase = nc, ctx, phase

    def sb(self, name, shape, dt=FP32):
        return self.ctx.enter_context(self.nc.sbuf_tensor(f"{self.phase}_{name}", shape, dt))

    def ps(self, name, shape=(P, 512), dt=FP32):
        return self.ctx.enter_context(self.nc.psum_tensor(f"{self.phase}_{name}", list(shape), dt))

    def sem(self, name):
        s = self.ctx.enter_context(self.nc.semaphore(f"{self.phase}_{name}"))
        self.semaphores.append(s)
        return s

    def lasting_sem(self, name):
        return self.ctx.enter_context(self.nc.semaphore(name))


class Chain:

    def __init__(self, eng, sem, base=0):
        self.eng, self.sem, self.base, self.n = eng, sem, base, 0

    def __call__(self, ins):
        self.n += 1
        ins.then_inc(self.sem, 1)
        self.eng.wait_ge(self.sem, self.base + self.n)


def clear_semaphores(nc):
    with nc.Block() as block:
        @block.gpsimd
        def _(pool):
            for s in Memory.semaphores:
                pool.sem_clear(s)
    Memory.semaphores.clear()


def constants(m):
    c = {}
    c["ident"] = m.sb("ident", [P, P])
    c["ident16"] = m.sb("ident16", [P, P], BF16)
    c["before"] = m.sb("before", [P, P], BF16)
    c["ones16"] = m.sb("ones16", [P, P], BF16)
    c["mask"] = m.sb("mask", [P, 2, KEYS], BF16)
    c["first"] = m.sb("first", [P, EXPERTS])
    c["base"] = m.sb("base", [P, EXPERTS])
    c["token"] = m.sb("token", [P, GROUP])
    c["power"] = m.sb("power", [P, GROUP])
    c["count"] = m.sb("count", [P, EXPERTS])
    c["start_of"] = m.sb("start_of", [1, TILES], I32)
    c["expert_of"] = m.sb("expert_of", [1, TILES], I32)
    c["list_out"] = [[m.lasting_sem(f"list_out{b}{n}") for n in range(2 * GROUP)] for b in range(2)]
    c["x_in"] = [[m.lasting_sem(f"x_in{b}{h}") for h in range(HALVES)] for b in range(2)]
    c["added"] = [[m.lasting_sem(f"added{b}{h}") for h in range(HALVES)] for b in range(2)]
    c["w1"] = m.sb("w1", [P, EXPERTS, 2, KD * FFN], FP16)
    c["w2"] = m.sb("w2", [P, EXPERTS, 2, KF * D], FP16)
    return c


FILL_LINKS = 19


def fill_phase(nc, ctx, c, scratch):
    m = Memory(nc, ctx, "fill")
    zeros = m.sb("zeros", [P, 4 * VROW], FP16)
    empty = m.sb("empty", [P, 512, 2], I32)
    padk = m.sb("padk", [P, 2 * WINDOW], FP16)
    pool_done, filled = m.sem("pool_done"), m.sem("filled")
    zero32 = zeros[:, 0:2 * D].bitcast(FP32)
    with nc.Block() as block:
        @block.gpsimd
        def _(pool):
            link = Chain(pool, pool_done)
            for t in (c["ident"], c["ident16"]):
                link(pool.memset(t[:, :], 0.0))
                link(pool.affine_select(out=t[:, :], in_=t[:, :], compare_op=ALU.not_equal, fill=1.0,
                                        base=0, pattern=[[-1, P]], channel_multiplier=1))
            link(pool.memset(c["before"][:, :], 1.0))
            link(pool.affine_select(out=c["before"][:, :], in_=c["before"][:, :], compare_op=ALU.is_gt,
                                    fill=0.0, base=0, pattern=[[1, P]], channel_multiplier=-1))
            link(pool.memset(c["ones16"][:, :], 1.0))
            link(pool.memset(c["mask"][:, :, :], 0.0))
            for half in (0, QT):
                local = c["mask"][half:half + QT, :, 0:LOCAL]
                link(pool.affine_select(out=local, in_=local, compare_op=ALU.is_ge, fill=MASKED,
                                        base=0, pattern=[[0, 2], [1, LOCAL]], channel_multiplier=-1))
                link(pool.affine_select(out=local, in_=local, compare_op=ALU.is_ge, fill=MASKED,
                                        base=2 * WINDOW, pattern=[[0, 2], [-1, LOCAL]],
                                        channel_multiplier=1))
            for t, base, step in ((c["first"], EXPERTS, -1), (c["base"], 0, TOK)):
                link(pool.iota(t[:, :], pattern=[[step, EXPERTS]], base=base, channel_multiplier=0,
                               allow_small_or_imprecise_dtypes=True))
            link(pool.memset(c["power"][:, :], -0.5))
            link(pool.memset(empty[:, :, :], 0))
            link(pool.iota(empty[:, :, 0], pattern=[[0, 512 // SLOTS], [1, SLOTS]], base=TOK,
                           channel_multiplier=0))
            link(pool.memset(zeros[:, :], 0.0))
            link(pool.memset(padk[:, :], PAD_K))
            assert link.n == FILL_LINKS, link.n

        @block.sync
        def _(sp):
            sp.wait_ge(pool_done, FILL_LINKS)
            n = 0
            for name in ("list1", "list2"):
                sp.dma_start(scratch[name][0:LIST_PAD, :].rearrange("(p s) e -> p s e", p=P),
                             empty[:, :, :]).then_inc(filled, 16)
                sp.dma_start(scratch[name][LIST_PAD:LIST_PAD + SLOTS, :].rearrange("(p s) e -> p s e", p=1),
                             empty[0:1, 0:SLOTS, :]).then_inc(filled, 16)
                n += 2
            for name in ("xn1", "acc1", "xn2", "acc2"):
                for h in range(HALVES):
                    sp.dma_start(scratch[name][TOK + h * P:TOK + (h + 1) * P, :], zero32).then_inc(filled, 16)
                    n += 1
            ks = scratch["ks"].rearrange("(r p) (b t) -> r p b t", p=P, b=BATCH)
            zk = zeros[:, 0:BATCH * WINDOW].rearrange("p (b t) -> p b t", b=BATCH)
            for side in (0, SEQP - WINDOW):
                for r in range(2 * D // P):
                    sp.dma_start(ks[r, :, :, side:side + WINDOW], zk).then_inc(filled, 16)
                    n += 1
                vs = scratch["vs"].rearrange("(b t) n -> t b n", b=BATCH)
                sp.dma_start(vs[side:side + WINDOW, :, :],
                             zeros[0:WINDOW, :].rearrange("p (b n) -> p b n", b=BATCH)).then_inc(filled, 16)
                sp.dma_start(scratch["padk"][0:1, side:side + WINDOW], padk[0:1, 0:WINDOW]).then_inc(filled, 16)
                n += 2
            sp.dma_start(scratch["padk"][0:1, WINDOW:WINDOW + SEQ].rearrange("a (p s) -> (a p) s", p=16),
                         zeros[0:16, 0:SEQ // 16]).then_inc(filled, 16)
            n += 1
            sp.wait_ge(filled, 16 * n)


ROUTER_LINKS = 2 * 24


def router_phase(nc, ctx, c, scratch, which, x_src, weights):
    m = Memory(nc, ctx, f"route{which}")
    first_time = which == 1
    xn_d, acc_d, list_d = scratch[f"xn{which}"], scratch[f"acc{which}"], scratch[f"list{which}"]
    two = range(2)
    x = [m.sb(f"x{b}", [P, GROUP, D]) for b in two]
    xn = [m.sb(f"xn{b}", [P, GROUP, D]) for b in two]
    xnT = [m.sb(f"xnT{b}", [P, KD, GTOK]) for b in two]
    wr = m.sb("wr", [P, KD, EXPERTS])
    stats = m.sb("stats", [P, GROUP, 6])
    mv = [m.sb(f"mv{b}", [P, GROUP, 2]) for b in two]
    ve = [m.sb(f"ve{b}", [P, GROUP]) for b in two]
    rstd = [m.sb(f"rstd{b}", [P, GROUP]) for b in two]
    shift = [m.sb(f"shift{b}", [P, GROUP]) for b in two]
    logits = m.sb("logits", [P, GROUP, EXPERTS])
    best = m.sb("best", [P, 2, GROUP])
    key = m.sb("key", [P, GROUP, EXPERTS])
    keymax = m.sb("keymax", [P, GROUP])
    pick = [[m.sb(f"pick{b}{k}", [P, GROUP, EXPERTS]) for k in two] for b in two]
    rest = m.sb("rest", [P, GROUP, EXPERTS])
    ex = [m.sb(f"ex{b}", [P, GROUP, EXPERTS + 1]) for b in two]
    total = m.sb("total", [P, GROUP])
    chosen = [m.sb(f"chosen{b}", [P, GROUP, EXPERTS], BF16) for b in two]
    place = m.sb("place", [P, GROUP, EXPERTS])
    placed = m.sb("placed", [P, GROUP, EXPERTS])
    slot = m.sb("slot", [P, GROUP])
    run = m.sb("run", [P, EXPERTS])
    slot_i = [m.sb(f"slot_i{b}", [P, 2, GROUP], I32) for b in two]
    entry = [m.sb(f"entry{b}", [P, 2, GROUP, 2], I32) for b in two]
    psT = [m.ps(f"psT{k}") for k in range(KD)]
    psR = [m.ps(f"psR{b}") for b in two]

    def both(name):
        return [m.sem(f"{name}{b}") for b in two]

    x_in, xn_out, x_out = both("x_in"), both("xn_out"), both("x_out")
    list_out, list_base = c["list_out"], 16 * (GROUPS // 2) * (which - 1)
    wr_in, start = m.sem("wr_in"), m.sem("start")
    ve_ready, rstd_ready, shift_ready = both("ve_ready"), both("rstd_ready"), both("shift_ready")
    xn_ready, turned, kept0, kept1 = both("xn_ready"), both("turned"), both("kept0"), both("kept1")
    logits_ready, exp_in, exp_out = both("logits_ready"), both("exp_in"), both("exp_out")
    chosen_ready, places_ready, entries_ready = both("chosen_ready"), both("places_ready"), both("entries_ready")
    dve_done = m.sem("dve_done")
    if first_time:
        w32 = [m.sb(f"w32_{k}", [P, 2 * FFN]) for k in two]
        w_in, w_hi, w_lo = both("w_in"), both("w_hi"), both("w_lo")
        w_parts = (c["w1"], c["w2"])
    else:
        at = [m.sb(f"at{b}", [P, GROUP, D]) for b in two]
        atT = [m.sb(f"atT{h}", [P, KD, GTOK], FP16) for h in two]
        wout32 = m.sb("wout32", [P, KD, D])
        wout = m.sb("wout", [P, 2, KD, D], FP16)
        bout = m.sb("bout", [P, D])
        psP = [m.ps(f"psP{k}") for k in two]
        at_in, biased, at_turned = both("at_in"), both("biased"), both("at_turned")
        at_hi, at_lo, projected, x_ready = both("at_hi"), both("at_lo"), both("projected"), both("x_ready")
        wout_in, wout_hi, wout_lo = m.sem("wout_in"), m.sem("wout_hi"), m.sem("wout_lo")

    def groups(ap):
        return ap[0:TOK, :].rearrange("(g j p) d -> g p j d", p=P, j=GROUP)

    def group(ap, g):
        return groups(ap)[bass.ds(g, 1)].rearrange("a p j d -> p (a j) d")

    def at_group(g):
        return scratch["att"].rearrange("(g j p) d -> g p j d", p=P, j=GROUP)[bass.ds(g, 1)].rearrange(
            "a p j d -> p (a j) d")

    with nc.Block() as block:
        @block.sync
        def _(sp):
            sp.dma_start(wr[:, :, :], weights["wr"].rearrange("(k p) e -> p k e", p=P)).then_inc(wr_in, 16)
            if not first_time:
                for k in two:
                    for j in range(PAIRS):
                        sp.dma_start(wout32[j * HD:(j + 1) * HD, k, :],
                                     weights["wout"][(2 * j + k) * HD:(2 * j + k + 1) * HD, :]).then_inc(wout_in, 16)
                sp.dma_start(bout[:, :], weights["bout"].partition_broadcast(P)).then_inc(wout_in, 16)
            with sp.Fori(0, GROUPS // 2) as i:
                for b in two:
                    sp.wait_ge(x_out[b], 16 * i)
                    sp.dma_start(x[b][:, :, :], group(x_src, 2 * i + b)).then_inc(x_in[b], 16)
                    if first_time:
                        w, n = (weights["w1"], KD) if b == 0 else (weights["w2"], KF)
                        sp.wait_ge(w_hi[b], i)
                        sp.wait_ge(w_lo[b], i)
                        sp.dma_start(w32[b][:, :].rearrange("p (k n) -> p k n", k=n),
                                     w.rearrange("e (k p) n -> e p k n", p=P)[bass.ds(i, 1)].rearrange(
                                         "a p k n -> p (a k) n")).then_inc(w_in[b], 16)
                    else:
                        sp.wait_ge(at_turned[b], i)
                        sp.dma_start(at[b][:, :, :], at_group(2 * i + b)).then_inc(at_in[b], 16)

        @block.gpsimd
        def _(pool):
            pool.iota(c["token"][:, :], pattern=[[P, GROUP]], base=0, channel_multiplier=1,
                      allow_small_or_imprecise_dtypes=True).then_inc(start, 1)
            with pool.Fori(0, GROUPS // 2) as i:
                if not first_time:
                    for b in two:
                        pool.wait_ge(x_in[b], 16 * i + 16)
                        if b == 0:
                            pool.wait_ge(wout_in, 16 * (2 * PAIRS + 1))
                        for j in range(GROUP):
                            ins = pool.tensor_tensor(x[b][:, j, :], x[b][:, j, :], bout[:, :], ALU.add)
                        ins.then_inc(biased[b], 1)
                for b in two:
                    pool.wait_ge(ve_ready[b], i + 1)
                    pool.tensor_tensor(rstd[b][:, :], ve[b][:, :], c["power"][:, :], ALU.pow).then_inc(rstd_ready[b], 1)
                for b in two:
                    pool.wait_ge(entries_ready[b], i + 1)
                    pool.nop(nofuse=True)
                    for k in two:
                        for j in range(GROUP):
                            pool.indirect_dma_start(
                                out=list_d[:, :],
                                out_offset=bass.IndirectOffsetOnAxis(ap=slot_i[b][:, k, j:j + 1], axis=0),
                                in_=entry[b][:, k, j, :], in_offset=None).then_inc(list_out[b][k * GROUP + j], 16)
            for b in two:
                for s in list_out[b]:
                    pool.wait_ge(s, list_base + 16 * (GROUPS // 2))

        @block.scalar
        def _(act):
            if not first_time:
                act.wait_ge(wout_in, 16 * (2 * PAIRS + 1))
                act.activation(wout[:, 0, :, :], wout32[:, :, :], ACT.Copy, scale=W_ATT).then_inc(wout_hi, 1)
            with act.Fori(0, GROUPS // 2) as i:
                if not first_time:
                    for b in two:
                        act.wait_ge(at_turned[b], i + 1)
                        act.wait_ge(projected[1 - b], i + b)
                        for k in range(KD):
                            ins = act.activation(atT[0][:, k, :], psT[k][:, :], ACT.Copy)
                        ins.then_inc(at_hi[b], 1)
                for b in two:
                    act.wait_ge(shift_ready[b], i + 1)
                    act.wait_ge(xn_out[b], 16 * i)
                    for j in range(GROUP):
                        ins = act.activation(xn[b][:, j, :], x[b][:, j, :], ACT.Identity,
                                             scale=rstd[b][:, j:j + 1], bias=shift[b][:, j:j + 1])
                    ins.then_inc(xn_ready[b], 1)
                    act.wait_ge(xn_ready[b], i + 1)
                    act.dma_start(group(xn_d, 2 * i + b), xn[b][:, :, :]).then_inc(xn_out[b], 16)
                    act.dma_start(group(acc_d, 2 * i + b), x[b][:, :, :]).then_inc(x_out[b], 16)
                for b in two:
                    act.wait_ge(turned[b], i + 1)
                    act.wait_ge(logits_ready[b], i)
                    act.activation(xnT[b][:, 0, :], psT[0][:, :], ACT.Copy).then_inc(kept0[b], 1)
                    act.wait_ge(exp_in[b], i + 1)
                    act.activation(ex[b][:, :, :], ex[b][:, :, :], ACT.Exp).then_inc(exp_out[b], 1)
                    if first_time:
                        act.wait_ge(w_in[b], 16 * i + 16)
                        act.activation(w_parts[b][:, bass.ds(i, 1), 0, :].rearrange("p a n -> p (a n)"),
                                       w32[b][:, :], ACT.Copy, scale=W_FFN).then_inc(w_hi[b], 1)
            for b in two:
                act.wait_ge(xn_out[b], 16 * (GROUPS // 2))
                act.wait_ge(x_out[b], 16 * (GROUPS // 2))

        @block.tensor
        def _(pe):
            pe.wait_ge(wr_in, 16)
            if not first_time:
                pe.wait_ge(wout_lo, 1)
            with pe.Fori(0, GROUPS // 2) as i:
                if not first_time:
                    for b in two:
                        pe.wait_ge(at_in[b], 16 * i + 16)
                        if b == 0:
                            pe.wait_ge(kept0[1], i)
                            pe.wait_ge(kept1[1], i)
                        else:
                            pe.wait_ge(at_hi[0], i + 1)
                            pe.wait_ge(at_lo[0], i + 1)
                        for j in range(GROUP):
                            for k in range(KD):
                                ins = pe.transpose(psT[k][:, j * P:(j + 1) * P], at[b][:, j, k * P:(k + 1) * P],
                                                   c["ident"][:, :])
                        ins.then_inc(at_turned[b], 1)
                        pe.wait_ge(at_hi[b], i + 1)
                        pe.wait_ge(at_lo[b], i + 1)
                        for j in range(GROUP):
                            out = psP[j // 2][:, (j % 2) * D:(j % 2 + 1) * D]
                            if j % 2 == 0:
                                pe.wait_ge(x_ready[1 - b], i + b)
                            n = 0
                            for k in range(KD):
                                for ah, wh in ((0, 0), (0, 1), (1, 0)):
                                    ins = pe.matmul(out, atT[ah][:, k, j * P:(j + 1) * P], wout[:, wh, k, :],
                                                    start=(n == 0), stop=(n == 3 * KD - 1))
                                    n += 1
                        ins.then_inc(projected[b], 1)
                for b in two:
                    pe.wait_ge(xn_ready[b], i + 1)
                    if b == 0 and first_time:
                        pe.wait_ge(kept0[1], i)
                        pe.wait_ge(kept1[1], i)
                    elif b == 0:
                        pe.wait_ge(at_hi[1], i + 1)
                        pe.wait_ge(at_lo[1], i + 1)
                    else:
                        pe.wait_ge(kept0[0], i + 1)
                        pe.wait_ge(kept1[0], i + 1)
                    for j in range(GROUP):
                        for k in range(KD):
                            ins = pe.transpose(psT[k][:, j * P:(j + 1) * P], xn[b][:, j, k * P:(k + 1) * P],
                                               c["ident"][:, :])
                    ins.then_inc(turned[b], 1)
                    pe.wait_ge(kept0[b], i + 1)
                    pe.wait_ge(kept1[b], i + 1)
                    pe.wait_ge(entries_ready[b], i)
                    for j in range(GROUP):
                        for k in range(KD):
                            ins = pe.matmul(psR[b][:, j * EXPERTS:(j + 1) * EXPERTS], xnT[b][:, k, j * P:(j + 1) * P],
                                            wr[:, k, :], start=(k == 0), stop=(k == KD - 1))
                    ins.then_inc(logits_ready[b], 1)
                for b in two:
                    pe.wait_ge(chosen_ready[b], i + 1)
                    for j in range(GROUP):
                        out = psR[b][:, 64 + j * EXPERTS:64 + (j + 1) * EXPERTS]
                        pe.matmul(out, c["before"][:, :], chosen[b][:, j, :], start=True, stop=(j == 0))
                        for earlier in range(j):
                            pe.matmul(out, c["ones16"][:, :], chosen[b][:, earlier, :], start=False,
                                      stop=(earlier == j - 1))
                    for j in range(GROUP):
                        ins = pe.matmul(psR[b][:, 128:128 + EXPERTS], c["ones16"][:, :], chosen[b][:, j, :],
                                        start=(j == 0), stop=(j == GROUP - 1))
                    ins.then_inc(places_ready[b], 1)

        @block.vector
        def _(dve):
            lone = Chain(dve, dve_done)
            lone(dve.tensor_copy(run[:, :], c["base"][:, :]))
            dve.wait_ge(start, 1)
            if not first_time:
                dve.wait_ge(wout_hi, 1)
                dve.scalar_tensor_tensor(wout[:, 1, :, :], wout32[:, :, :], W_ATT, wout[:, 0, :, :],
                                         ALU.mult, ALU.subtract).then_inc(wout_lo, 1)

            def wide(t):
                return t.unsqueeze(2).to_broadcast([P, GROUP, EXPERTS])

            def over(t):
                return t[:, :].unsqueeze(1).to_broadcast([P, GROUP, EXPERTS])

            with dve.Fori(0, GROUPS // 2) as i:
                link = Chain(dve, dve_done, 1 + ROUTER_LINKS * i)
                for b in two:
                    if not first_time:
                        dve.wait_ge(at_hi[b], i + 1)
                        for k in range(KD):
                            ins = dve.tensor_tensor(atT[1][:, k, :], psT[k][:, :], atT[0][:, k, :], ALU.subtract)
                        ins.then_inc(at_lo[b], 1)
                        dve.wait_ge(projected[b], i + 1)
                        dve.wait_ge(biased[b], i + 1)
                        for h in range(GROUP // 2):
                            ins = dve.scalar_tensor_tensor(
                                x[b][:, 2 * h:2 * h + 2, :].rearrange("p j d -> p (j d)"), psP[h][:, :],
                                1.0 / W_ATT, x[b][:, 2 * h:2 * h + 2, :].rearrange("p j d -> p (j d)"),
                                ALU.mult, ALU.add)
                        ins.then_inc(x_ready[b], 1)
                        dve.wait_ge(x_ready[b], i + 1)
                for b in two:
                    dve.wait_ge(x_in[b], 16 * i + 16)
                    for j in range(GROUP):
                        ins = dve.bn_stats(stats[:, j, :], x[b][:, j, :])
                    link(ins)
                    dve.nop(nofuse=True)
                    for j in range(GROUP):
                        ins = dve.bn_aggr(mv[b][:, j, :], stats[:, j, :])
                    link(ins)
                    dve.tensor_scalar(ve[b][:, :], mv[b][:, :, 1], EPS, None, ALU.add).then_inc(ve_ready[b], 1)
                for b in two:
                    dve.wait_ge(rstd_ready[b], i + 1)
                    dve.scalar_tensor_tensor(shift[b][:, :], mv[b][:, :, 0], -1.0, rstd[b][:, :],
                                             ALU.mult, ALU.mult).then_inc(shift_ready[b], 1)
                for b in two:
                    dve.wait_ge(turned[b], i + 1)
                    dve.wait_ge(logits_ready[b], i)
                    dve.tensor_copy(xnT[b][:, 1, :], psT[1][:, :]).then_inc(kept1[b], 1)
                    dve.wait_ge(logits_ready[b], i + 1)
                    link(dve.tensor_copy(logits[:, :, :].rearrange("p j e -> p (j e)"),
                                         psR[b][:, 0:GROUP * EXPERTS]))
                    for k in two:
                        of = logits if k == 0 else rest
                        link(dve.tensor_reduce(best[:, k, :], of[:, :, :], AX.X, ALU.max))
                        link(dve.tensor_tensor(key[:, :, :], of[:, :, :], wide(best[:, k, :]), ALU.is_equal))
                        link(dve.tensor_tensor(key[:, :, :], key[:, :, :], over(c["first"]), ALU.mult))
                        link(dve.tensor_reduce(keymax[:, :], key[:, :, :], AX.X, ALU.max))
                        link(dve.tensor_tensor(pick[b][k][:, :, :], key[:, :, :], wide(keymax[:, :]), ALU.is_equal))
                        if k == 0:
                            link(dve.scalar_tensor_tensor(rest[:, :, :], pick[b][0][:, :, :], MASKED,
                                                          logits[:, :, :], ALU.mult, ALU.add))
                    dve.tensor_tensor(chosen[b][:, :, :], pick[b][0][:, :, :], pick[b][1][:, :, :],
                                      ALU.add).then_inc(chosen_ready[b], 1)
                    dve.tensor_tensor(ex[b][:, :, 0:EXPERTS], logits[:, :, :], wide(best[:, 0, :]), ALU.subtract)
                    dve.tensor_tensor(ex[b][:, :, EXPERTS], best[:, 1, :], best[:, 0, :],
                                      ALU.subtract).then_inc(exp_in[b], 1)
                    if first_time:
                        dve.wait_ge(w_hi[b], i + 1)
                        dve.scalar_tensor_tensor(
                            w_parts[b][:, bass.ds(i, 1), 1, :].rearrange("p a n -> p (a n)"), w32[b][:, :], W_FFN,
                            w_parts[b][:, bass.ds(i, 1), 0, :].rearrange("p a n -> p (a n)"),
                            ALU.mult, ALU.subtract).then_inc(w_lo[b], 1)
                    for s in list_out[b]:
                        dve.wait_ge(s, list_base + 16 * i)
                    dve.wait_ge(exp_out[b], i + 1)
                    link(dve.tensor_reduce(total[:, :], ex[b][:, :, 0:EXPERTS], AX.X, ALU.add))
                    link(dve.reciprocal(total[:, :], total[:, :]))
                    dve.tensor_scalar(entry[b][:, 0, :, 1].bitcast(FP32), total[:, :], GATE_SCALE, None, ALU.mult)
                    dve.scalar_tensor_tensor(entry[b][:, 1, :, 1].bitcast(FP32), ex[b][:, :, EXPERTS], GATE_SCALE,
                                             total[:, :], ALU.mult, ALU.mult)
                for b in two:
                    dve.wait_ge(places_ready[b], i + 1)
                    link(dve.tensor_tensor(place[:, :, :], psR[b][:, 64:64 + GROUP * EXPERTS].rearrange(
                        "p (j e) -> p j e", j=GROUP), over(run), ALU.add))
                    link(dve.tensor_tensor(run[:, :], run[:, :], psR[b][:, 128:128 + EXPERTS], ALU.add))
                    for k in two:
                        link(dve.tensor_tensor(placed[:, :, :], pick[b][k][:, :, :], place[:, :, :], ALU.mult))
                        link(dve.tensor_reduce(slot[:, :], placed[:, :, :], AX.X, ALU.add))
                        link(dve.tensor_copy(slot_i[b][:, k, :], slot[:, :]))
                        dve.tensor_copy(entry[b][:, k, :, 0], c["token"][:, :])
                    dve.tensor_scalar(c["token"][:, :], c["token"][:, :], float(GTOK), None,
                                      ALU.add).then_inc(entries_ready[b], 1)
                    dve.wait_ge(entries_ready[b], i + 1)
                assert link.n == ROUTER_LINKS, link.n
            dve.tensor_tensor(c["count"][:, :], run[:, :], c["base"][:, :], ALU.subtract).then_inc(dve_done, 1)
            dve.wait_ge(dve_done, ROUTER_LINKS * (GROUPS // 2) + 2)


SEARCH_BITS = 31
SEARCH_LINKS = 5


def table_phase(nc, ctx, c, scratch, which, cap=CAP):
    m = Memory(nc, ctx, f"table{which}")
    counts_i = m.sb("counts_i", [1, EXPERTS], I32)
    tiles_of = m.sb("tiles_of", [1, EXPERTS])
    last = m.sb("last", [1, EXPERTS])
    ones = m.sb("ones", [1, EXPERTS])
    tile = m.sb("tile", [1, TILES])
    expert = m.sb("expert", [1, TILES])
    begin = m.sb("begin", [1, TILES])
    step = m.sb("step", [1, TILES])
    live = m.sb("live", [1, TILES])
    most = m.sb("most", [1, 1])
    over_cap = m.sb("over_cap", [1, 1], I32)
    iotas, chain, tables_done = m.sem("iotas"), m.sem("chain"), m.sem("tables_done")
    S = TOK * EXPERTS // P
    entries = m.sb("entries", [P, S, 2], I32)
    gates = m.sb("gates", [P, S])
    above = m.sb("above", [P, S])
    equal = m.sb("equal", [P, S])
    rank = m.sb("rank", [P, S])
    one_row = m.sb("one_row", [P, S])
    same = m.sb("same", [P, P])
    earlier = m.sb("earlier", [P, P])
    bit = m.sb("bit", [P, 1], I32)
    one_i = m.sb("one_i", [P, 1], I32)
    floor_i = m.sb("floor_i", [P, 1], I32)
    guess = m.sb("guess", [P, 1], I32)
    in_row = m.sb("in_row", [P, 2])
    enough = m.sb("enough", [P, 1], I32)
    room = m.sb("room", [P, 1])
    ps = m.ps("ps", [P, 512])
    entries_in, entries_out = m.sem("entries_in"), m.sem("entries_out")
    rows_ready, sums_ready = m.sem("rows_ready"), m.sem("sums_ready")
    search, gates_done = m.sem("search"), m.sem("gates_done")
    pool_links = 10
    lists = scratch[f"list{which}"][0:LIST_PAD, :].rearrange("(p s) e -> p s e", p=P)

    with nc.Block() as block:
        @block.gpsimd
        def _(pool):
            link = Chain(pool, iotas)
            link(pool.iota(tile[:, :], pattern=[[1, TILES]], base=0, channel_multiplier=0,
                           allow_small_or_imprecise_dtypes=True))
            link(pool.memset(ones[:, :], 1.0))
            for t, least in ((same, 0), (earlier, 1)):
                v = t[:, :].rearrange("p (e r) -> p e r", r=P // EXPERTS)
                link(pool.memset(t[:, :], 1.0))
                link(pool.affine_select(out=v, in_=v, compare_op=ALU.is_ge, fill=0.0, base=0,
                                        pattern=[[-(P // EXPERTS), EXPERTS], [0, P // EXPERTS]],
                                        channel_multiplier=1))
                end = P // EXPERTS - 1 if least == 0 else -1
                link(pool.affine_select(out=v, in_=v, compare_op=ALU.is_ge, fill=0.0, base=end,
                                        pattern=[[P // EXPERTS, EXPERTS], [least, P // EXPERTS]],
                                        channel_multiplier=-1))
            link(pool.memset(one_row[:, :], 1.0))
            link(pool.memset(one_i[:, :], 1))
            assert link.n == pool_links, link.n

        @block.vector
        def _(dve):
            link = Chain(dve, chain)
            count = c["count"][0:1, :]
            dve.wait_ge(iotas, pool_links)
            link(dve.tensor_reduce(most[:, :], count, AX.X, ALU.max))
            link(dve.tensor_scalar(over_cap[:, :], most[:, :], float(cap), None, ALU.is_gt))
            link(dve.tensor_scalar(counts_i[:, :], count, float(SLOTS - 1), None, ALU.add))
            link(dve.tensor_scalar(counts_i[:, :], counts_i[:, :], SLOTS.bit_length() - 1, None,
                                   ALU.arith_shift_right))
            link(dve.tensor_copy(tiles_of[:, :], counts_i[:, :]))
            link(dve.tensor_tensor_scan(last[:, :], ones[:, :], tiles_of[:, :], 0.0, ALU.mult, ALU.add))
            link(dve.memset(expert[:, :], 0.0))
            link(dve.memset(begin[:, :], 0.0))
            for e in range(EXPERTS - 1):
                link(dve.tensor_scalar(step[:, :], tile[:, :], last[:, e:e + 1], None, ALU.is_ge))
                link(dve.tensor_tensor(expert[:, :], expert[:, :], step[:, :], ALU.add))
                link(dve.scalar_tensor_tensor(begin[:, :], step[:, :], tiles_of[:, e:e + 1], begin[:, :],
                                              ALU.mult, ALU.add))
            link(dve.tensor_tensor(begin[:, :], tile[:, :], begin[:, :], ALU.subtract))
            link(dve.tensor_scalar(begin[:, :], begin[:, :], float(SLOTS), float(-LIST_PAD), ALU.mult, ALU.add))
            link(dve.scalar_tensor_tensor(begin[:, :], expert[:, :], float(TOK), begin[:, :], ALU.mult, ALU.add))
            link(dve.tensor_scalar(live[:, :], tile[:, :], last[:, EXPERTS - 1:EXPERTS], None, ALU.is_lt))
            link(dve.tensor_tensor(begin[:, :], begin[:, :], live[:, :], ALU.mult))
            link(dve.tensor_scalar(c["start_of"][:, :], begin[:, :], float(LIST_PAD), None, ALU.add))
            link(dve.tensor_copy(c["expert_of"][:, :], expert[:, :]))
            dve.sem_inc(tables_done, 1)
            flag = dve.value_load(over_cap[0:1, 0:1], min_val=0, max_val=1)
            with dve.If(flag > 0):
                s = Chain(dve, search)
                dve.wait_ge(entries_in, 16)
                s(dve.tensor_copy(gates[:, :], entries[:, :, 1].bitcast(FP32)))
                s(dve.memset(floor_i[:, :], 0))
                s(dve.memset(bit[:, :], 1 << (SEARCH_BITS - 1)))
                with dve.Fori(0, SEARCH_BITS) as i:
                    t = Chain(dve, search, 3 + i * SEARCH_LINKS)
                    t(dve.tensor_tensor(guess[:, :], floor_i[:, :], bit[:, :], ALU.bitwise_or))
                    dve.tensor_scalar(above[:, :], gates[:, :], guess[:, :].bitcast(FP32), None, ALU.is_ge, ALU.add,
                                      accum_out=in_row[:, 0:1]).then_inc(rows_ready, 1)
                    dve.wait_ge(sums_ready, i + 1)
                    t(dve.tensor_scalar(enough[:, :], ps[:, 0:1], float(cap), -1.0, ALU.is_ge, ALU.mult))
                    t(dve.tensor_tensor(enough[:, :], enough[:, :], bit[:, :], ALU.bitwise_and))
                    t(dve.tensor_tensor(floor_i[:, :], floor_i[:, :], enough[:, :], ALU.bitwise_or))
                    t(dve.tensor_tensor(bit[:, :], bit[:, :], one_i[:, :], ALU.logical_shift_right))
                    assert t.n == SEARCH_LINKS
                s = Chain(dve, search, 3 + SEARCH_BITS * SEARCH_LINKS)
                level = floor_i[:, :].bitcast(FP32)
                s(dve.tensor_scalar(above[:, :], gates[:, :], level, None, ALU.is_gt, ALU.add,
                                    accum_out=in_row[:, 0:1]))
                s(dve.tensor_scalar(equal[:, :], gates[:, :], level, None, ALU.is_equal, ALU.add,
                                    accum_out=in_row[:, 1:2]))
                dve.sem_inc(rows_ready, 1)
                dve.wait_ge(sums_ready, SEARCH_BITS + 1)
                s(dve.tensor_scalar(room[:, :], ps[:, 0:1], -1.0, float(cap), ALU.mult, ALU.add))
                s(dve.tensor_tensor(room[:, :], room[:, :], ps[:, 1:2], ALU.subtract))
                s(dve.tensor_tensor_scan(rank[:, :], one_row[:, :], equal[:, :], 0.0, ALU.mult, ALU.add))
                s(dve.scalar_tensor_tensor(equal[:, :], rank[:, :], room[:, :], equal[:, :], ALU.is_le, ALU.mult))
                s(dve.tensor_tensor(above[:, :], above[:, :], equal[:, :], ALU.add))
                s(dve.tensor_tensor(entries[:, :, 1].bitcast(FP32), gates[:, :], above[:, :], ALU.mult))
                dve.sem_inc(gates_done, 1)

        @block.tensor
        def _(pe):
            pe.wait_ge(tables_done, 1)
            flag = pe.value_load(over_cap[0:1, 0:1], min_val=0, max_val=1)
            with pe.If(flag > 0):
                with pe.Fori(0, SEARCH_BITS) as i:
                    pe.wait_ge(rows_ready, i + 1)
                    pe.matmul(ps[:, 0:1], same[:, :], in_row[:, 0:1], start=True, stop=True).then_inc(sums_ready, 1)
                pe.wait_ge(rows_ready, SEARCH_BITS + 1)
                pe.matmul(ps[:, 0:1], same[:, :], in_row[:, 0:1], start=True, stop=True)
                pe.matmul(ps[:, 1:2], earlier[:, :], in_row[:, 1:2], start=True, stop=True).then_inc(sums_ready, 1)

        @block.sync
        def _(sp):
            sp.wait_ge(tables_done, 1)
            flag = sp.value_load(over_cap[0:1, 0:1], min_val=0, max_val=1)
            with sp.If(flag > 0):
                sp.dma_start(entries[:, :, :], lists).then_inc(entries_in, 16)
                sp.wait_ge(gates_done, 1)
                sp.dma_start(lists, entries[:, :, :]).then_inc(entries_out, 16)
                sp.wait_ge(entries_out, 16)


def ffn_phase(nc, ctx, c, scratch, which):
    m = Memory(nc, ctx, f"ffn{which}")
    xn_d, acc_d, list_d = scratch[f"xn{which}"], scratch[f"acc{which}"], scratch[f"list{which}"]
    two = range(2)
    PAIRS_F = KF // 2
    wanted = [m.sb(f"wanted{b}", [P, HALVES, 2], I32) for b in two]
    entry = [m.sb(f"entry{b}", [P, HALVES, 2], I32) for b in two]
    x = [m.sb(f"x{b}", [P, HALVES, D]) for b in two]
    xT = [[m.sb(f"xT{b}{h}", [P, KD, SLOTS], FP16) for h in two] for b in two]
    hT = [[m.sb(f"hT{b}{h}", [P, KF, SLOTS], FP16) for h in two] for b in two]
    y = [m.sb(f"y{b}", [P, HALVES, D]) for b in two]
    psT = m.ps("psT")
    psH = [m.ps(f"psH{f}") for f in range(PAIRS_F)]
    psY = [m.ps(f"psY{b}") for b in two]

    def both(name):
        return [m.sem(f"{name}{b}") for b in two]

    wanted_in = both("wanted_in")
    entry_in, turned, xT_hi, xT_lo = both("entry_in"), both("turned"), both("xT_hi"), both("xT_lo")
    summed, y_ready = both("summed"), both("y_ready")
    x_in, added = c["x_in"], c["added"]
    tiles_of_buffer = [(TILES + 1 - b) // 2 for b in two]
    base = [16 * n * (which - 1) for n in tiles_of_buffer]
    hidden = [m.sem(f"hidden{f}") for f in range(PAIRS_F)]
    h_hi = [m.sem(f"h_hi{f}") for f in range(PAIRS_F)]
    h_lo = [m.sem(f"h_lo{f}") for f in range(PAIRS_F)]
    turns = (TILES - 3) // 2
    assert TILES == 2 * turns + 3

    def tile_loop(eng, body):
        with eng.Fori(0, turns) as i:
            for b in two:
                body(2 * i + b, i, b)
        for n in range(2 * turns, TILES):
            body(n, n // 2, n % 2)

    def follows(n, by):
        return not isinstance(n, int) or n + by < TILES

    with nc.Block() as block:
        @block.sync
        def _(sp):
            def load_entries(dst, n, done):
                start = sp.value_load(c["start_of"][0:1, bass.ds(n, 1)], min_val=0, max_val=LIST_PAD)
                sp.dma_start(dst[:, :, :],
                             list_d[bass.ds(start, SLOTS), :].rearrange("(h p) e -> p h e", p=P)).then_inc(done, 16)

            def tile(n, i, b):
                if follows(n, 2):
                    for h in two:
                        sp.wait_ge(x_in[b][h], base[b] + 16 * i + 16)
                    load_entries(wanted[b], n + 2, wanted_in[b])
                for h in two:
                    sp.wait_ge(added[b][h], base[b] + 16 * i)
                load_entries(entry[b], n, entry_in[b])

            for b in two:
                load_entries(wanted[b], b, wanted_in[b])
            tile_loop(sp, tile)

        @block.gpsimd
        def _(pool):
            def gather(i, b):
                pool.wait_ge(wanted_in[b], 16 * i + 16)
                pool.wait_ge(turned[b], i)
                pool.nop(nofuse=True)
                for h in two:
                    pool.indirect_dma_start(
                        out=x[b][:, h, :], out_offset=None, in_=xn_d[:, :],
                        in_offset=bass.IndirectOffsetOnAxis(ap=wanted[b][:, h, 0:1], axis=0)
                    ).then_inc(x_in[b][h], 16)

            def tile(n, i, b):
                if follows(n, 2):
                    gather(i + 1, b)
                pool.wait_ge(y_ready[b], i + 1)
                pool.wait_ge(entry_in[b], 16 * i + 16)
                for h in two:
                    pool.wait_ge(added[1 - b][h], base[1 - b] + 16 * (i + b))
                pool.nop(nofuse=True)
                for h in two:
                    pool.indirect_dma_start(
                        out=acc_d[:, :], in_=y[b][:, h, :], in_offset=None, compute_op=ALU.add,
                        out_offset=bass.IndirectOffsetOnAxis(ap=entry[b][:, h, 0:1], axis=0)
                    ).then_inc(added[b][h], 16)

            for b in two:
                gather(0, b)
            tile_loop(pool, tile)
            for b in two:
                for h in two:
                    pool.wait_ge(added[b][h], base[b] + 16 * tiles_of_buffer[b])

        @block.tensor
        def _(pe):
            def turn_tokens(i, b):
                for h in two:
                    pe.wait_ge(x_in[b][h], base[b] + 16 * i + 16)
                pe.wait_ge(xT_hi[1 - b], i + b)
                pe.wait_ge(xT_lo[1 - b], i + b)
                for k in range(KD):
                    for h in two:
                        ins = pe.transpose(psT[:, k * SLOTS + h * P:k * SLOTS + (h + 1) * P],
                                           x[b][:, h, k * P:(k + 1) * P], c["ident"][:, :])
                ins.then_inc(turned[b], 1)

            def tile(n, i, b):
                e = pe.value_load(c["expert_of"][0:1, bass.ds(n, 1)], min_val=0, max_val=EXPERTS - 1)
                w1 = c["w1"][:, bass.ds(e, 1), :, :].rearrange("p a h n -> p (a h) n")
                w2 = c["w2"][:, bass.ds(e, 1), :, :].rearrange("p a h n -> p (a h) n")
                terms = ((0, 0), (0, 1), (1, 0))
                pe.wait_ge(xT_hi[b], i + 1)
                pe.wait_ge(xT_lo[b], i + 1)
                for f2 in range(PAIRS_F):
                    pe.wait_ge(h_hi[f2], n)
                    pe.wait_ge(h_lo[f2], n)
                    for f in two:
                        col = (2 * f2 + f) * P
                        for k in range(KD):
                            for wh, xh in terms:
                                ins = pe.matmul(psH[f2][:, f * SLOTS:(f + 1) * SLOTS],
                                                w1[:, wh, k * FFN + col:k * FFN + col + P], xT[b][xh][:, k, :],
                                                start=(k == 0 and (wh, xh) == terms[0]),
                                                stop=(k == KD - 1 and (wh, xh) == terms[-1]))
                    ins.then_inc(hidden[f2], 1)
                if follows(n, 1):
                    turn_tokens(i + b, 1 - b)
                pe.wait_ge(y_ready[b], i)
                for h in two:
                    for f in range(KF):
                        if h == 0 and f % 2 == 0:
                            pe.wait_ge(h_hi[f // 2], n + 1)
                            pe.wait_ge(h_lo[f // 2], n + 1)
                        for wh, hh in terms:
                            ins = pe.matmul(psY[b][:, h * D:(h + 1) * D], hT[b][hh][:, f, h * P:(h + 1) * P],
                                            w2[:, wh, f * D:(f + 1) * D],
                                            start=(f == 0 and (wh, hh) == terms[0]),
                                            stop=(f == KF - 1 and (wh, hh) == terms[-1]))
                ins.then_inc(summed[b], 1)

            turn_tokens(0, 0)
            tile_loop(pe, tile)

        @block.scalar
        def _(act):
            def tokens_hi(i, b):
                act.wait_ge(turned[b], i + 1)
                act.activation(xT[b][0][:, :, :].rearrange("p k n -> p (k n)"), psT[:, :],
                               ACT.Copy).then_inc(xT_hi[b], 1)

            def tile(n, i, b):
                for f2 in range(PAIRS_F):
                    act.wait_ge(hidden[f2], n + 1)
                    act.activation(hT[b][0][:, 2 * f2:2 * f2 + 2, :].rearrange("p f n -> p (f n)"),
                                   psH[f2][:, :], ACT.Relu).then_inc(h_hi[f2], 1)
                if follows(n, 1):
                    tokens_hi(i + b, 1 - b)
                act.wait_ge(summed[b], i + 1)
                act.wait_ge(entry_in[b], 16 * i + 16)
                for h in two:
                    act.wait_ge(added[b][h], base[b] + 16 * i)
                for h in two:
                    ins = act.activation(y[b][:, h, :], psY[b][:, h * D:(h + 1) * D], ACT.Copy,
                                         scale=entry[b][:, h, 1:2].bitcast(FP32))
                ins.then_inc(y_ready[b], 1)

            tokens_hi(0, 0)
            tile_loop(act, tile)

        @block.vector
        def _(dve):
            def tokens_lo(i, b):
                dve.wait_ge(xT_hi[b], i + 1)
                dve.tensor_tensor(xT[b][1][:, :, :].rearrange("p k n -> p (k n)"), psT[:, :],
                                  xT[b][0][:, :, :].rearrange("p k n -> p (k n)"),
                                  ALU.subtract).then_inc(xT_lo[b], 1)

            def tile(n, i, b):
                for f2 in range(PAIRS_F):
                    dve.wait_ge(h_hi[f2], n + 1)
                    dve.scalar_tensor_tensor(
                        hT[b][1][:, 2 * f2:2 * f2 + 2, :].rearrange("p f n -> p (f n)"), psH[f2][:, :], 0.0,
                        hT[b][0][:, 2 * f2:2 * f2 + 2, :].rearrange("p f n -> p (f n)"),
                        ALU.max, ALU.subtract).then_inc(h_lo[f2], 1)
                if follows(n, 1):
                    tokens_lo(i + b, 1 - b)

            tokens_lo(0, 0)
            tile_loop(dve, tile)



def group_turn(i, s):
    return i + s // 2, s % 2


def group_exists(i, s):
    return s >= 0 and (not isinstance(i, int) or 2 * i + s < GROUPS)


def group_steps(eng, ahead, step):
    for s in range(-ahead, 0):
        step(0, s)
    with eng.Fori(0, GROUPS // 2 - 2) as i:
        for s in range(2):
            step(i, s)
    for s in range(4):
        step(GROUPS // 2 - 2 + s // 2, s % 2)


def qkv_phase(nc, ctx, c, scratch, weights):
    m = Memory(nc, ctx, "qkv")
    two = range(2)
    NG = 3 * D + 1
    x = [m.sb(f"x{b}", [P, GROUP, D]) for b in two]
    xn = [m.sb(f"xn{b}", [P, GROUP, D]) for b in two]
    xT = [[m.sb(f"xT{b}{h}", [P, KD, GTOK], FP16) for h in two] for b in two]
    stats = [m.sb(f"stats{b}", [P, GROUP, 6]) for b in two]
    mv = [m.sb(f"mv{b}", [P, GROUP, 2]) for b in two]
    ve = [m.sb(f"ve{b}", [P, GROUP]) for b in two]
    rstd = [m.sb(f"rstd{b}", [P, GROUP]) for b in two]
    shift = [m.sb(f"shift{b}", [P, GROUP]) for b in two]
    w32 = m.sb("w32", [P, KD, NG])
    w = m.sb("w", [P, 2, KD, NG + 1], FP16)
    bias_qk = m.sb("bias_qk", [P, 4])
    bias_v = m.sb("bias_v", [P, D])
    bias_g = m.sb("bias_g", [P, 1])
    qk = [m.sb(f"qk{b}", [P, 4, 2, GTOK], FP16) for b in two]
    v32 = [m.sb(f"v32{b}", [P, GROUP, D]) for b in two]
    vrow = [m.sb(f"vrow{b}", [P, GROUP, VROW], FP16) for b in two]
    z = [m.sb(f"z{b}", [P, GROUP]) for b in two]
    gate = [m.sb(f"gate{b}", [P, GROUP, 2]) for b in two]
    psT = [m.ps(f"psT{k}") for k in range(KD)]
    psQ = [m.ps(f"psQ{k}") for k in two]
    psV = [m.ps(f"psV{k}") for k in range(GROUP)]

    def both(name):
        return [m.sem(f"{name}{b}") for b in two]

    stats_ready, mean_ready, z_ready, gate_there = (
        both("stats_ready"), both("mean_ready"), both("z_ready"), both("gate_there"))
    w_in, w_hi, w_lo, consts, chain = m.sem("w_in"), m.sem("w_hi"), m.sem("w_lo"), m.sem("consts"), m.sem("chain")
    x_in, ve_ready, rstd_ready, shift_ready, xn_ready = (
        both("x_in"), both("ve_ready"), both("rstd_ready"), both("shift_ready"), both("xn_ready"))
    turned, xT_hi, xT_lo = both("turned"), both("xT_hi"), both("xT_lo")
    qk_sum, qk_hi, qk_lo = both("qk_sum"), both("qk_hi"), both("qk_lo")
    qk_out, v_out, gate_out = both("qk_out"), both("v_out"), both("gate_out")
    v_sum, v_ready, v_hi, v_rows = both("v_sum"), both("v_ready"), both("v_hi"), both("v_rows")
    exp_ready, gate_ready = both("exp_ready"), both("gate_ready")
    turns = GROUPS // 2

    def group(ap, g):
        return ap[0:TOK, :].rearrange("(g j p) d -> g p j d", p=P, j=GROUP)[bass.ds(g, 1)].rearrange(
            "a p j d -> p (a j) d")

    with nc.Block() as block:
        @block.sync
        def _(sp):
            sp.dma_start(w32[:, :, 0:3 * D], weights["wqkv"].rearrange("(k p) n -> p k n", p=P)).then_inc(w_in, 16)
            sp.dma_start(w32[:, :, 3 * D:NG], weights["wg"].rearrange("(k p) n -> p k n", p=P),
                         allow_slow_non_contiguous=True).then_inc(w_in, 16)
            sp.dma_start(bias_qk[:, :], weights["bqkv"][0:2 * D].rearrange("(c p) -> p c", p=P),
                         allow_slow_non_contiguous=True).then_inc(w_in, 16)
            sp.dma_start(bias_v[:, :], weights["bqkv"][2 * D:3 * D].partition_broadcast(P)).then_inc(w_in, 16)
            sp.dma_start(bias_g[:, :], weights["bg"].partition_broadcast(P)).then_inc(w_in, 16)

            def load(i, s):
                i, b = group_turn(i, s)
                sp.wait_ge(xn_ready[b], i)
                sp.dma_start(x[b][:, :, :], group(scratch["acc1"], 2 * i + b)).then_inc(x_in[b], 16)

            def store(i, s):
                i, b = group_turn(i, s)
                tok = 2 * GTOK * i + GTOK * b
                padded = tok + 2 * WINDOW * (i // (SEQ // GTOK // 2)) + WINDOW
                for half in two:
                    rows = scratch["qs" if half == 0 else "ks"].rearrange("(h r p) t -> r p h t", h=2, p=P)
                    first = tok if half == 0 else padded
                    for r in range(KD):
                        n = 2 * half + r
                        sp.wait_ge(qk_hi[n % 2], 4 * i + 2 * b + n // 2 + 1)
                        sp.wait_ge(qk_lo[n % 2], 4 * i + 2 * b + n // 2 + 1)
                        sp.dma_start(rows[r][:, :, bass.ds(first, GTOK)], qk[b][:, n, :, :]).then_inc(qk_out[b], 16)
                sp.wait_ge(v_rows[b], i + 1)
                sp.dma_start(scratch["vs"][bass.ds(padded, GTOK), :].rearrange("(j p) n -> p j n", p=P),
                             vrow[b][:, :, :]).then_inc(v_out[b], 16)
                sp.wait_ge(gate_ready[b], i + 1)
                sp.dma_start(group(scratch["gate"], 2 * i + b), gate[b][:, :, :]).then_inc(gate_out[b], 16)

            def step(i, s):
                if group_exists(i, s + 3):
                    load(i, s + 3)
                if group_exists(i, s):
                    store(i, s)
            group_steps(sp, 3, step)
            for b in two:
                sp.wait_ge(qk_out[b], 64 * turns)
                sp.wait_ge(v_out[b], 16 * turns)
                sp.wait_ge(gate_out[b], 16 * turns)

        @block.gpsimd
        def _(pool):
            for b in two:
                ins = pool.memset(vrow[b][:, :, :], 0.0)
            ins.then_inc(consts, 1)
            pool.wait_ge(consts, 1)
            for b in two:
                for j in range(GROUP):
                    ones = vrow[b][:, j, :].rearrange("p (r h a n) -> p r h a n", r=PAIRS, h=2, a=2)
                    ins = pool.memset(ones[:, :, 0, :, HD], 1.0)
            ins.then_inc(consts, 1)
            pool.wait_ge(consts, 2)

            def root(i, s):
                i, b = group_turn(i, s)
                pool.wait_ge(ve_ready[b], i + 1)
                pool.tensor_tensor(rstd[b][:, :], ve[b][:, :], c["power"][:, :], ALU.pow).then_inc(rstd_ready[b], 1)

            def split_values(i, s):
                i, b = group_turn(i, s)
                pool.wait_ge(v_ready[b], i + 1)
                pool.wait_ge(v_out[b], 16 * i)
                pool.nop(nofuse=True)
                for part in two:
                    for j in range(GROUP):
                        rows = vrow[b][:, j, :].rearrange("p (r h a n) -> p r h a n", r=PAIRS, h=2, a=2)
                        hi, lo = rows[:, :, 0, :, 0:HD], rows[:, :, 1, :, 0:HD]
                        v = v32[b][:, j, :].rearrange("p (r a n) -> p r a n", r=PAIRS, a=2)
                        if part == 0:
                            ins = pool.tensor_copy(hi, v)
                        else:
                            ins = pool.tensor_tensor(lo, v, hi, ALU.subtract)
                    if part == 0:
                        ins.then_inc(v_hi[b], 1)
                        pool.wait_ge(v_hi[b], i + 1)
                ins.then_inc(v_rows[b], 1)

            def step(i, s):
                if group_exists(i, s + 2):
                    root(i, s + 2)
                if group_exists(i, s):
                    split_values(i, s)
            group_steps(pool, 2, step)

        @block.scalar
        def _(act):
            act.wait_ge(w_in, 80)
            act.activation(w[:, 0, :, 0:NG], w32[:, :, :], ACT.Copy, scale=W_ATT).then_inc(w_hi, 1)

            def normalise(i, s):
                i, b = group_turn(i, s)
                act.wait_ge(shift_ready[b], i + 1)
                act.wait_ge(turned[b], i)
                for j in range(GROUP):
                    ins = act.activation(xn[b][:, j, :], x[b][:, j, :], ACT.Identity,
                                         scale=rstd[b][:, j:j + 1], bias=shift[b][:, j:j + 1])
                ins.then_inc(xn_ready[b], 1)

            def high(i, s):
                i, b = group_turn(i, s)
                act.wait_ge(turned[b], i + 1)
                for k in range(KD):
                    ins = act.activation(xT[b][0][:, k, :], psT[k][:, :], ACT.Copy)
                ins.then_inc(xT_hi[b], 1)

            def queries_keys(i, s):
                i, b = group_turn(i, s)
                act.wait_ge(qk_out[b], 64 * i)
                for n in range(4):
                    act.wait_ge(qk_sum[n % 2], 4 * i + 2 * b + n // 2 + 1)
                    act.activation(qk[b][:, n, 0, :], psQ[n % 2][:, :], ACT.Identity,
                                   bias=bias_qk[:, n:n + 1]).then_inc(qk_hi[n % 2], 1)

            def gates(i, s):
                i, b = group_turn(i, s)
                act.wait_ge(v_ready[b], i + 1)
                for j in range(GROUP):
                    ins = act.activation(z[b][:, j:j + 1], psV[j][:, D:D + 1], ACT.Exp, scale=-1.0 / W_ATT,
                                         bias=bias_g[:, :])
                ins.then_inc(exp_ready[b], 1)

            def step(i, s):
                if group_exists(i, s):
                    queries_keys(i, s)
                if group_exists(i, s + 1):
                    high(i, s + 1)
                if group_exists(i, s + 2):
                    normalise(i, s + 2)
                if group_exists(i, s):
                    gates(i, s)
            group_steps(act, 2, step)

        @block.tensor
        def _(pe):
            pe.wait_ge(w_lo, 1)
            terms = ((0, 0), (0, 1), (1, 0))

            def turn(i, s):
                i, b = group_turn(i, s)
                pe.wait_ge(xn_ready[b], i + 1)
                pe.wait_ge(xT_lo[1 - b], i + b)
                for j in range(GROUP):
                    for k in range(KD):
                        ins = pe.transpose(psT[k][:, j * P:(j + 1) * P], xn[b][:, j, k * P:(k + 1) * P],
                                           c["ident"][:, :])
                ins.then_inc(turned[b], 1)

            def queries_keys(i, s):
                i, b = group_turn(i, s)
                pe.wait_ge(xT_lo[b], i + 1)
                for n in range(4):
                    pe.wait_ge(qk_lo[n % 2], 4 * i + 2 * b + n // 2)
                    for k in range(KD):
                        for wh, xh in terms:
                            ins = pe.matmul(psQ[n % 2][:, :], w[:, wh, k, n * P:(n + 1) * P], xT[b][xh][:, k, :],
                                            start=(k == 0 and (wh, xh) == terms[0]),
                                            stop=(k == KD - 1 and (wh, xh) == terms[-1]))
                    ins.then_inc(qk_sum[n % 2], 1)

            def values(i, s):
                i, b = group_turn(i, s)
                pe.wait_ge(exp_ready[1 - b], i + b)
                for j in range(GROUP):
                    for k in range(KD):
                        for wh, xh in terms:
                            ins = pe.matmul(psV[j][:, 0:D + 1], xT[b][xh][:, k, j * P:(j + 1) * P],
                                            w[:, wh, k, 2 * D:NG],
                                            start=(k == 0 and (wh, xh) == terms[0]),
                                            stop=(k == KD - 1 and (wh, xh) == terms[-1]))
                ins.then_inc(v_sum[b], 1)

            def step(i, s):
                if group_exists(i, s):
                    queries_keys(i, s)
                if group_exists(i, s + 1):
                    turn(i, s + 1)
                if group_exists(i, s):
                    values(i, s)
            group_steps(pe, 1, step)

        @block.vector
        def _(dve):
            dve.wait_ge(w_hi, 1)
            dve.scalar_tensor_tensor(w[:, 1, :, 0:NG], w32[:, :, :], W_ATT, w[:, 0, :, 0:NG],
                                     ALU.mult, ALU.subtract).then_inc(w_lo, 1)
            first = Chain(dve, chain)
            first(dve.tensor_scalar(bias_qk[:, :], bias_qk[:, :], W_ATT, None, ALU.mult))
            first(dve.tensor_scalar(bias_g[:, :], bias_g[:, :], -1.0, None, ALU.mult))
            dve.wait_ge(w_lo, 1)

            def statistics(i, s):
                i, b = group_turn(i, s)
                dve.wait_ge(x_in[b], 16 * i + 16)
                for j in range(GROUP):
                    ins = dve.bn_stats(stats[b][:, j, :], x[b][:, j, :])
                ins.then_inc(stats_ready[b], 1)

            def variance(i, s):
                i, b = group_turn(i, s)
                dve.wait_ge(stats_ready[b], i + 1)
                dve.nop(nofuse=True)
                for j in range(GROUP):
                    ins = dve.bn_aggr(mv[b][:, j, :], stats[b][:, j, :])
                ins.then_inc(mean_ready[b], 1)
                dve.wait_ge(mean_ready[b], i + 1)
                dve.tensor_scalar(ve[b][:, :], mv[b][:, :, 1], EPS, None, ALU.add).then_inc(ve_ready[b], 1)

            def shifts(i, s):
                i, b = group_turn(i, s)
                dve.wait_ge(rstd_ready[b], i + 1)
                dve.scalar_tensor_tensor(shift[b][:, :], mv[b][:, :, 0], -1.0, rstd[b][:, :],
                                         ALU.mult, ALU.mult).then_inc(shift_ready[b], 1)

            def low(i, s):
                i, b = group_turn(i, s)
                dve.wait_ge(xT_hi[b], i + 1)
                for k in range(KD):
                    ins = dve.tensor_tensor(xT[b][1][:, k, :], psT[k][:, :], xT[b][0][:, k, :], ALU.subtract)
                ins.then_inc(xT_lo[b], 1)

            def queries_keys(i, s, chunks):
                i, b = group_turn(i, s)
                for n in chunks:
                    dve.wait_ge(qk_hi[n % 2], 4 * i + 2 * b + n // 2 + 1)
                    dve.scalar_tensor_tensor(qk[b][:, n, 1, :], psQ[n % 2][:, :], bias_qk[:, n:n + 1],
                                             qk[b][:, n, 0, :], ALU.add, ALU.subtract).then_inc(qk_lo[n % 2], 1)

            def values(i, s):
                i, b = group_turn(i, s)
                dve.wait_ge(v_sum[b], i + 1)
                dve.wait_ge(v_rows[b], i)
                for j in range(GROUP):
                    ins = dve.scalar_tensor_tensor(v32[b][:, j, :], psV[j][:, 0:D], 1.0 / W_ATT, bias_v[:, :],
                                                   ALU.mult, ALU.add)
                ins.then_inc(v_ready[b], 1)

            def gates(i, s):
                i, b = group_turn(i, s)
                dve.wait_ge(exp_ready[b], i + 1)
                dve.wait_ge(gate_out[b], 16 * i)
                dve.tensor_scalar(z[b][:, :], z[b][:, :], 1.0, None, ALU.add).then_inc(z_ready[b], 1)
                dve.wait_ge(z_ready[b], i + 1)
                dve.reciprocal(gate[b][:, :, 1], z[b][:, :]).then_inc(gate_there[b], 1)
                dve.wait_ge(gate_there[b], i + 1)
                dve.tensor_scalar(gate[b][:, :, 0], gate[b][:, :, 1], -1.0, 1.0,
                                  ALU.mult, ALU.add).then_inc(gate_ready[b], 1)

            def step(i, s):
                if group_exists(i, s + 1):
                    queries_keys(i, s + 1, (0, 1))
                if group_exists(i, s):
                    gates(i, s)
                if group_exists(i, s + 3):
                    statistics(i, s + 3)
                if group_exists(i, s + 1):
                    queries_keys(i, s + 1, (2, 3))
                if group_exists(i, s + 3):
                    variance(i, s + 3)
                if group_exists(i, s + 2):
                    low(i, s + 2)
                if group_exists(i, s + 3):
                    shifts(i, s + 3)
                if group_exists(i, s + 1):
                    values(i, s + 1)
            group_steps(dve, 3, step)


def attention_phase(nc, ctx, c, scratch):
    m = Memory(nc, ctx, "att")
    two, four = range(2), range(4)
    TILES_S = SPAN // QT
    DUOS_S = TILES_S * PAIRS // 2
    BODY = 2 * DUOS_S
    TURNS = SPANS // 2
    AHEAD = 6
    PARTS = 3
    q = [m.sb(f"q{b}", [P, PAIRS, TILES_S, 2, QT], FP16) for b in two]
    k = [m.sb(f"k{b}", [P, PAIRS, SPAN_K + N_GLOBAL], FP16) for b in two]
    v0 = [m.sb(f"v0{b}", [P, TILES_S, VROW], FP16) for b in two]
    v1 = [m.sb(f"v1{b}", [P, TILES_S, 2, VROW], FP16) for b in two]
    gate = [m.sb(f"gate{b}", [P, TILES_S, 2]) for b in two]
    pad_rows = m.sb("pad_rows", [P, 2])
    most = [m.sb(f"most{b}", [P, 2, 2]) for b in four]
    shift = [m.sb(f"shift{b}", [P, 2, 2]) for b in four]
    prob = [m.sb(f"prob{b}", [P, 2, KEYS]) for b in two]
    probT = [[m.sb(f"probT{b}{h}", [P, 2, 2, P], FP16) for h in two] for b in two]
    share = [m.sb(f"share{b}", [P, 4, 2]) for b in two]
    parts = [m.sb(f"parts{b}", [P, 4, 2, HD]) for b in two]
    out = [m.sb(f"out{b}", [P, TILES_S, 2, 4, HD]) for b in two]
    psS = [m.ps(f"psS{b}", [P, 2, KEYS]) for b in four]
    psT = [m.ps(f"psT{b}", [P, 2, 2, P]) for b in two]
    psO = [m.ps(f"psO{b}", [P, 512]) for b in two]

    def both(name):
        return [m.sem(f"{name}{b}") for b in two]

    def each(name):
        return [m.sem(f"{name}{b}") for b in four]

    pad_ready, q_cleared, k_cleared, v_cleared = (
        m.sem("pad_ready"), m.sem("q_cleared"), m.sem("k_cleared"), m.sem("v_cleared"))
    qk_in, v_in = both("qk_in"), both("v_in")
    scored, reduced, maxed, exped = each("scored"), each("reduced"), each("maxed"), each("exped")
    inverted, shared = both("inverted"), both("shared")
    turned, p_hi, p_lo, used = both("turned"), both("p_hi"), both("p_lo"), both("used")
    taken, added, stored = both("taken"), both("added"), both("stored")
    QK_LOADS = 2 * PARTS * (TILES_S + 2) + 4
    V_LOADS = TILES_S + 2

    def duo(i, s):
        return i + s // BODY, s % BODY

    def exists(i, s):
        return s >= 0 and (not isinstance(i, int) or i * BODY + s < TURNS * BODY)

    def use(i, s, buffers):
        return (BODY // buffers) * i + s // buffers

    def where(s):
        return s // DUOS_S, s % DUOS_S // 4, 2 * (s % 4)

    def places(i, b):
        batch = i // (SEQ // SPAN // 2)
        tok = 2 * SPAN * i + SPAN * b
        return (tok, tok + 2 * WINDOW * batch, 2 * SPAN * (i % (SEQ // SPAN // 2)) + SPAN * b,
                SEQP * batch + WINDOW)

    def steps(eng, step):
        for s in range(-AHEAD, 0):
            step(0, s)
        with eng.Fori(0, TURNS - 1) as i:
            for s in range(BODY):
                step(i, s)
        for s in range(BODY):
            step(TURNS - 1, s)

    with nc.Block() as block:
        @block.gpsimd
        def _(pool):
            link = Chain(pool, pad_ready)
            link(pool.memset(pad_rows[:, :], 0.0))
            link(pool.affine_select(out=pad_rows[:, :], in_=pad_rows[:, :], compare_op=ALU.not_equal, fill=PAD_Q,
                                    base=-PARTS * HD, pattern=[[-QT, 2]], channel_multiplier=1))
            for b in two:
                pool.memset(v1[b][:, :, :, :].bitcast(FP32), 0.0).then_inc(v_cleared, 1)
            pool.wait_ge(v_cleared, 2)

            def load_values(i, b):
                _, first, _, global_keys = places(i, b)
                vs = scratch["vs"]
                for t in range(TILES_S):
                    pool.dma_start(v0[b][:, t, :], vs[bass.ds(first + QT * t, P), :]).then_inc(v_in[b], 16)
                pool.dma_start(v1[b][0:QT, :, 0, :],
                               vs[bass.ds(first + P, SPAN), :].rearrange("(t p) n -> p t n", p=QT)).then_inc(v_in[b], 16)
                pool.dma_start(v1[b][QT:P, :, 1, :],
                               vs[bass.ds(global_keys, N_GLOBAL), :].unsqueeze(1).to_broadcast(
                                   [N_GLOBAL, TILES_S, VROW])).then_inc(v_in[b], 16)

            def outputs(i, b):
                pool.wait_ge(stored[b], 32 * i)
                for t in range(TILES_S):
                    for half in two:
                        pool.wait_ge(taken[half], TILES_S * (2 * i + b) + t + 1)
                        pool.tensor_tensor(out[b][:, t, half, :, :], parts[half][:, :, 0, :],
                                           parts[half][:, :, 1, :], ALU.add).then_inc(added[half], 1)
                pool.wait_ge(added[1], TILES_S * (2 * i + b + 1))
                pool.nop(nofuse=True)
                for a in two:
                    rows = scratch["att"][bass.ds(2 * SPAN * i + SPAN * b, SPAN), a * P:(a + 1) * P]
                    pool.dma_start(rows.rearrange("(t p) n -> p t n", p=QT),
                                   out[b][QT * a:QT * a + QT, :, :, :, :].rearrange("p t h u n -> p t (h u n)")
                                   ).then_inc(stored[b], 16)

            for b in two:
                load_values(0, b)
            with pool.Fori(0, TURNS - 1) as i:
                for b in two:
                    outputs(i, b)
                    load_values(i + 1, b)
            for b in two:
                outputs(TURNS - 1, b)
            for b in two:
                pool.wait_ge(stored[b], 32 * TURNS)

        @block.sync
        def _(sp):
            sp.wait_ge(q_cleared, 2)
            sp.wait_ge(k_cleared, 2)
            qs = scratch["qs"].rearrange("(h r a d) t -> h a d r t", h=2, a=2, d=HD)
            ks = scratch["ks"].rearrange("(h r a d) t -> h a d r t", h=2, a=2, d=HD)

            def load(i, b):
                tok, first, at, global_keys = places(i, b)
                n = 0
                for a in two:
                    for part, (qh, kh) in enumerate(((0, 0), (0, 1), (1, 0))):
                        r0 = QT * a + HD * part
                        for t in range(TILES_S):
                            sp.dma_start(q[b][r0:r0 + HD, :, t, a, :],
                                         qs[qh, a][:, :, bass.ds(tok + QT * t, QT)]).then_inc(qk_in[b], 16)
                        sp.dma_start(k[b][r0:r0 + HD, :, 0:SPAN_K], ks[kh, a][:, :, bass.ds(first, SPAN_K)]
                                     ).then_inc(qk_in[b], 16)
                        sp.dma_start(k[b][r0:r0 + HD, :, SPAN_K:SPAN_K + N_GLOBAL],
                                     ks[kh, a][:, :, bass.ds(global_keys, N_GLOBAL)]).then_inc(qk_in[b], 16)
                        n += TILES_S + 2
                    r0 = QT * a + PARTS * HD
                    sp.dma_start(k[b][r0:r0 + 1, :, 0:SPAN_K],
                                 scratch["padk"][0:1, bass.ds(at, SPAN_K)].unsqueeze(1).to_broadcast(
                                     [1, PAIRS, SPAN_K])).then_inc(qk_in[b], 16)
                    n += 1
                if not isinstance(i, int):
                    sp.wait_ge(taken[1], TILES_S * (2 * i + b - 1))
                    sp.nop(nofuse=True)
                for a in two:
                    sp.dma_start(gate[b][QT * a:QT * a + QT, :, :],
                                 scratch["gate"][bass.ds(tok, SPAN), :].rearrange("(t q) e -> q t e", q=QT)
                                 ).then_inc(qk_in[b], 16)
                    n += 1
                assert n == QK_LOADS, n

            for b in two:
                load(0, b)
            with sp.Fori(0, TURNS - 1) as i:
                for b in two:
                    sp.wait_ge(scored[3], use(i, DUOS_S * (b + 1) - 1, 4) + 1)
                    sp.nop(nofuse=True)
                    load(i + 1, b)

        @block.tensor
        def _(pe):
            def scores(i, s):
                i, s = duo(i, s)
                sb, t, r = where(s)
                bank = s % 4
                if s % DUOS_S == 0:
                    pe.wait_ge(qk_in[sb], 16 * QK_LOADS * (i + 1))
                pe.wait_ge(exped[bank], use(i, s, 4))
                pe.matmul(psS[bank][:, :, :].rearrange("p u n -> p (u n)"), c["ident16"][:, :],
                          c["mask"][:, :, :].rearrange("p u n -> p (u n)"), start=True, stop=True)
                for u in two:
                    lhs = q[sb][:, r + u, t, :, :].rearrange("p a n -> p (a n)")
                    pe.matmul(psS[bank][:, u, 0:LOCAL], lhs, k[sb][:, r + u, t * QT:t * QT + LOCAL],
                              start=False, stop=True, skip_group_check=True)
                    ins = pe.matmul(psS[bank][:, u, LOCAL:KEYS], lhs, k[sb][:, r + u, SPAN_K:SPAN_K + N_GLOBAL],
                                    start=False, stop=True, skip_group_check=True)
                ins.then_inc(scored[bank], 1)

            def turn(i, s):
                i, s = duo(i, s)
                b = s % 2
                pe.wait_ge(exped[s % 4], use(i, s, 4) + 1)
                pe.wait_ge(p_lo[b], use(i, s, 2))
                for u in two:
                    for blk in two:
                        ins = pe.transpose(psT[b][:, u, blk, :], prob[b][:, u, blk * P:(blk + 1) * P],
                                           c["ident"][:, :])
                ins.then_inc(turned[b], 1)

            def values(i, s):
                i, s = duo(i, s)
                sb, t, r = where(s)
                b, bank = s % 2, s // 2 % 2
                if s % DUOS_S == 0:
                    pe.wait_ge(v_in[sb], 16 * V_LOADS * (i + 1))
                if s % 2 == 0:
                    pe.wait_ge(taken[bank], use(i, s, 4))
                pe.wait_ge(p_lo[b], use(i, s, 2) + 1)
                for u in two:
                    slot = 2 * (s % 2) + u
                    o = psO[bank][:, slot * 2 * VW:(slot + 1) * 2 * VW]
                    terms = ((0, 0), (0, 1), (1, 0))
                    for n, (ph, vh) in enumerate(terms):
                        col = (2 * (r + u) + vh) * VW
                        pe.matmul(o, probT[b][ph][:, u, 1, :], v1[sb][:, t, :, col:col + VW],
                                  start=(n == 0), stop=(n == 2))
                    for ph, vh in terms:
                        col = (2 * (r + u) + vh) * VW
                        ins = pe.matmul(o[:, 0:VW], probT[b][ph][:, u, 0, :], v0[sb][:, t, col:col + VW],
                                        start=False, stop=True, skip_group_check=True)
                ins.then_inc(used[b], 1)

            def step(i, s):
                if exists(i, s + 6):
                    scores(i, s + 6)
                if exists(i, s + 3):
                    turn(i, s + 3)
                if exists(i, s + 1):
                    values(i, s + 1)
            steps(pe, step)

        @block.scalar
        def _(act):
            def high(i, s):
                i, s = duo(i, s)
                b = s % 2
                act.wait_ge(turned[b], use(i, s, 2) + 1)
                act.wait_ge(used[b], use(i, s, 2))
                act.activation(probT[b][0][:, :, :, :].rearrange("p u k n -> p (u k n)"),
                               psT[b][:, :, :, :].rearrange("p u k n -> p (u k n)"), ACT.Copy).then_inc(p_hi[b], 1)

            def exps(i, s):
                i, s = duo(i, s)
                b, bank = s % 2, s % 4
                act.wait_ge(maxed[bank], use(i, s, 4) + 1)
                act.wait_ge(turned[b], use(i, s, 2))
                for u in two:
                    for seg, (lo, hi) in enumerate(((0, LOCAL), (LOCAL, KEYS))):
                        ins = act.activation(prob[b][:, u, lo:hi], psS[bank][:, u, lo:hi], ACT.Exp, scale=SCORE_SCALE,
                                             bias=shift[bank][:, u, seg:seg + 1])
                ins.then_inc(exped[bank], 1)

            def step(i, s):
                if exists(i, s + 2):
                    high(i, s + 2)
                if exists(i, s + 4):
                    exps(i, s + 4)
            act.wait_ge(pad_ready, 2)
            for b in two:
                for a in two:
                    ins = act.activation(q[b][:, :, :, a, :].rearrange("p r t n -> p (r t) n"),
                                         pad_rows[:, a:a + 1].unsqueeze(2).to_broadcast([P, PAIRS * TILES_S, QT]),
                                         ACT.Copy)
                ins.then_inc(q_cleared, 1)
            steps(act, step)

        @block.vector
        def _(dve):
            for b in two:
                dve.memset(k[b][:, :, :].bitcast(FP32), 0.0).then_inc(k_cleared, 1)

            def maxima(i, s):
                i, s = duo(i, s)
                bank, n = s % 4, use(i, s, 4)
                dve.wait_ge(scored[bank], n + 1)
                dve.tensor_reduce(most[bank][:, :, 0], psS[bank][:, :, 0:LOCAL], AX.X, ALU.max)
                dve.tensor_reduce(most[bank][:, :, 1], psS[bank][:, :, LOCAL:KEYS], AX.X,
                                  ALU.max).then_inc(reduced[bank], 1)

            def negate(i, s):
                i, s = duo(i, s)
                bank, n = s % 4, use(i, s, 4)
                dve.wait_ge(reduced[bank], n + 1)
                dve.tensor_scalar(shift[bank][:, :, :], most[bank][:, :, :], -SCORE_SCALE, None,
                                  ALU.mult).then_inc(maxed[bank], 1)

            def low(i, s):
                i, s = duo(i, s)
                b = s % 2
                dve.wait_ge(p_hi[b], use(i, s, 2) + 1)
                dve.tensor_tensor(probT[b][1][:, :, :, :].rearrange("p u k n -> p (u k n)"),
                                  psT[b][:, :, :, :].rearrange("p u k n -> p (u k n)"),
                                  probT[b][0][:, :, :, :].rearrange("p u k n -> p (u k n)"),
                                  ALU.subtract).then_inc(p_lo[b], 1)

            def bank_of(i, s):
                i, s = duo(i, s)
                b = s // 2 % 2
                return where(s)[0], where(s)[1], b, use(i, s, 4), psO[b][:, 0:8 * VW].rearrange(
                    "p (u g n) -> p u g n", u=4, g=2)

            def invert(i, s):
                sb, t, b, n, sums = bank_of(i, s)
                dve.wait_ge(used[1], 2 * n + b + 1)
                for a in two:
                    rows = slice(QT * a, QT * a + QT)
                    ins = dve.reciprocal(share[b][rows, :, :], sums[rows, :, :, (HD + 1) * a + HD])
                ins.then_inc(inverted[b], 1)

            def weigh(i, s):
                sb, t, b, n, sums = bank_of(i, s)
                dve.wait_ge(inverted[b], n + 1)
                dve.tensor_tensor(share[b][:, :, :], share[b][:, :, :],
                                  gate[sb][:, t, :].unsqueeze(1).to_broadcast([P, 4, 2]),
                                  ALU.mult).then_inc(shared[b], 1)

            def outputs(i, s):
                sb, t, b, n, sums = bank_of(i, s)
                dve.wait_ge(shared[b], n + 1)
                dve.wait_ge(added[b], n)
                for a in two:
                    rows = slice(QT * a, QT * a + QT)
                    ins = dve.tensor_tensor(parts[b][rows, :, :, :], sums[rows, :, :, (HD + 1) * a:(HD + 1) * a + HD],
                                            share[b][rows, :, :].unsqueeze(3).to_broadcast([QT, 4, 2, HD]), ALU.mult)
                ins.then_inc(taken[b], 1)

            def step(i, s):
                last = s % 2 == 1 and exists(i, s)
                if last:
                    invert(i, s)
                if exists(i, s + 5):
                    maxima(i, s + 5)
                if last:
                    weigh(i, s)
                if exists(i, s + 5):
                    negate(i, s + 5)
                if exists(i, s + 2):
                    low(i, s + 2)
                if last:
                    outputs(i, s)
            steps(dve, step)


def copy_phase(nc, ctx, scratch, out):
    m = Memory(nc, ctx, "copy")
    copied = m.sem("copied")
    PIECES = 8
    rows = TOK // PIECES
    with nc.Block() as block:
        @block.sync
        def _(sp):
            for n in range(PIECES):
                sp.dma_start(out[n * rows:(n + 1) * rows, :].rearrange("(p r) d -> p (r d)", p=P),
                             scratch["acc2"][n * rows:(n + 1) * rows, :].rearrange("(p r) d -> p (r d)", p=P)
                             ).then_inc(copied, 16)
            sp.wait_ge(copied, 16 * PIECES)


def macaron(nc, x, wqkv, bqkv, wout, bout, wg, bg, wr, w1, w2, out):
    scratch = {}

    def dram(name, shape, dt=FP32):
        scratch[name] = nc.dram_tensor(f"scratch_{name}", shape, dt, kind="Internal").ap()

    for which in (1, 2):
        dram(f"xn{which}", [TOK + SLOTS, D])
        dram(f"acc{which}", [TOK + SLOTS, D])
        dram(f"list{which}", [LIST_PAD + SLOTS, 2], I32)
    dram("qs", [2 * D, TOK], FP16)
    dram("ks", [2 * D, BATCH * SEQP], FP16)
    dram("vs", [BATCH * SEQP, VROW], FP16)
    dram("padk", [1, SEQP], FP16)
    dram("gate", [TOK, 2])
    dram("att", [TOK, D])
    weights = dict(wqkv=wqkv, bqkv=bqkv, wout=wout, bout=bout, wg=wg, bg=bg, wr=wr, w1=w1, w2=w2)
    with ExitStack() as ctx:
        c = constants(Memory(nc, ctx, "const"))

        def phase(build, *args):
            with ExitStack() as inner:
                build(nc, inner, *args)

        phase(fill_phase, c, scratch)
        phase(router_phase, c, scratch, 1, x.rearrange("b t d -> (b t) d"), weights)
        phase(table_phase, c, scratch, 1)
        phase(ffn_phase, c, scratch, 1)
        phase(qkv_phase, c, scratch, weights)
        clear_semaphores(nc)
        phase(attention_phase, c, scratch)
        phase(router_phase, c, scratch, 2, scratch["acc1"], weights)
        phase(table_phase, c, scratch, 2)
        phase(ffn_phase, c, scratch, 2)
        phase(copy_phase, scratch, out.rearrange("b t d -> (b t) d"))


_INS = ["L0_attn_hidden_states", "L0_attn_Wqkv", "L0_attn_bqkv", "L0_attn_Wout", "L0_attn_bout", "L0_attn_Wg",
        "L0_attn_bg", "L0_ffn_Wr", "L0_ffn_W1", "L0_ffn_W2"]


def kernel(**inputs):
    import numpy as np
    import concourse.bacc as bacc
    from concourse.bass_utils import run_bass_kernel_spmd

    nc = bacc.Bacc("TRN2", target_bir_lowering=False, num_devices=1)
    arrays, args = {}, []
    for name in _INS:
        a = np.ascontiguousarray(inputs[name])
        arrays[f"in_{name}"] = a
        args.append(nc.dram_tensor(f"in_{name}", a.shape, mybir.dt.from_np(a.dtype), kind="ExternalInput").ap())
    out = nc.dram_tensor("out", (BATCH, SEQ, D), FP32, kind="ExternalOutput").ap()
    macaron(nc, *args, out)
    r = run_bass_kernel_spmd(nc, [arrays], core_ids=[0])
    return r.results[0]["out"]
```

```python
import concourse.bass as bass
from concourse import mybir
from contextlib import ExitStack

FP32, FP16, BF16, I32 = mybir.dt.float32, mybir.dt.float16, mybir.dt.bfloat16, mybir.dt.int32
ALU = mybir.AluOpType
ACT = mybir.ActivationFunctionType
AX = mybir.AxisListType

P = 128
BATCH, SEQ, D = 4, 2048, 256
TOK = BATCH * SEQ
HEADS, HD = 16, 16
PAIRS = HEADS // 2
WINDOW = 64
N_GLOBAL = 64
EXPERTS, FFN, TOP_K = 8, 1024, 2
CAP = -(-TOK * TOP_K * 5 // (4 * EXPERTS))
EPS = 1e-5
KD = D // P
KF = FFN // P

GROUP = 4
GTOK = GROUP * P
GROUPS = TOK // GTOK

SLOTS = 256
HALVES = SLOTS // P
TILES = (TOK * TOP_K + EXPERTS * (SLOTS - 1)) // SLOTS
FULL_TILES = TOK * TOP_K // SLOTS
LIST_PAD = EXPERTS * TOK

SEQP = SEQ + 2 * WINDOW
QT = 64
SPAN = 4 * QT
SPAN_K = SPAN + 2 * WINDOW
SPANS = TOK // SPAN
LOCAL = QT + 2 * WINDOW
KEYS = LOCAL + N_GLOBAL
VW = 2 * (HD + 1)
VROW = PAIRS * 2 * VW

W_FFN = 32.0
W_ATT = 4.0
GATE_SCALE = 0.5 / (W_FFN * W_FFN)
SCORE_SCALE = HD ** -0.5
PAD_Q, PAD_K = 60000.0, -60000.0
MASKED = -1e30


class Memory:

    semaphores = []

    def __init__(self, nc, ctx, phase):
        self.nc, self.ctx, self.phase = nc, ctx, phase

    def sb(self, name, shape, dt=FP32):
        return self.ctx.enter_context(self.nc.sbuf_tensor(f"{self.phase}_{name}", shape, dt))

    def ps(self, name, shape=(P, 512), dt=FP32):
        return self.ctx.enter_context(self.nc.psum_tensor(f"{self.phase}_{name}", list(shape), dt))

    def sem(self, name):
        s = self.ctx.enter_context(self.nc.semaphore(f"{self.phase}_{name}"))
        self.semaphores.append(s)
        return s

    def lasting_sem(self, name):
        return self.ctx.enter_context(self.nc.semaphore(name))


class Chain:

    def __init__(self, eng, sem, base=0):
        self.eng, self.sem, self.base, self.n = eng, sem, base, 0

    def __call__(self, ins):
        self.n += 1
        ins.then_inc(self.sem, 1)
        self.eng.wait_ge(self.sem, self.base + self.n)


def clear_semaphores(nc):
    with nc.Block() as block:
        @block.gpsimd
        def _(pool):
            for s in Memory.semaphores:
                pool.sem_clear(s)
    Memory.semaphores.clear()


def constants(m):
    c = {}
    c["ident"] = m.sb("ident", [P, P])
    c["ident16"] = m.sb("ident16", [P, P], BF16)
    c["before"] = m.sb("before", [P, P], BF16)
    c["ones16"] = m.sb("ones16", [P, P], BF16)
    c["mask"] = m.sb("mask", [P, 2, KEYS], BF16)
    c["first"] = m.sb("first", [P, EXPERTS])
    c["base"] = m.sb("base", [P, EXPERTS])
    c["token"] = m.sb("token", [P, GROUP])
    c["power"] = m.sb("power", [P, GROUP])
    c["count"] = m.sb("count", [P, EXPERTS])
    c["start_of"] = m.sb("start_of", [1, TILES], I32)
    c["expert_of"] = m.sb("expert_of", [1, TILES], I32)
    c["over_cap"] = m.sb("over_cap", [1, 1], I32)
    c["in_use"] = m.sb("in_use", [1, TILES], I32)
    c["list_out"] = [[m.lasting_sem(f"list_out{b}{n}") for n in range(2 * GROUP)] for b in range(2)]
    for w in (1, 2):
        for name in (f"x_in{w}", f"added{w}"):
            c[name] = [[m.lasting_sem(f"{name}_{b}{h}") for h in range(HALVES)] for b in range(2)]
    c["v_in"] = [m.lasting_sem(f"v_in{b}") for b in range(2)]
    c["stored"] = [m.lasting_sem(f"stored{b}") for b in range(2)]
    c["w1"] = m.sb("w1", [P, EXPERTS, 2, KD * FFN], FP16)
    c["w2"] = m.sb("w2", [P, EXPERTS, 2, KF * D], FP16)
    return c


FILL_LINKS = 4


def fill_phase(nc, ctx, c, scratch):
    m = Memory(nc, ctx, "fill")
    zeros = m.sb("zeros", [P, 4 * VROW], FP16)
    empty = m.sb("empty", [P, 512, 2], I32)
    padk = m.sb("padk", [P, 2 * WINDOW], FP16)
    pool_done, filled = m.sem("pool_done"), m.sem("filled")
    zero32 = zeros[:, 0:2 * D].bitcast(FP32)
    with nc.Block() as block:
        @block.gpsimd
        def _(pool):
            link = Chain(pool, pool_done)
            link(pool.memset(empty[:, :, :], 0))
            link(pool.iota(empty[:, :, 0], pattern=[[0, 512 // SLOTS], [1, SLOTS]], base=TOK,
                           channel_multiplier=0))
            link(pool.memset(zeros[:, :], 0.0))
            link(pool.memset(padk[:, :], PAD_K))
            assert link.n == FILL_LINKS, link.n
            for t in (c["ident"], c["ident16"]):
                link(pool.memset(t[:, :], 0.0))
                link(pool.affine_select(out=t[:, :], in_=t[:, :], compare_op=ALU.not_equal, fill=1.0,
                                        base=0, pattern=[[-1, P]], channel_multiplier=1))
            link(pool.memset(c["before"][:, :], 1.0))
            link(pool.affine_select(out=c["before"][:, :], in_=c["before"][:, :], compare_op=ALU.is_gt,
                                    fill=0.0, base=0, pattern=[[1, P]], channel_multiplier=-1))
            link(pool.memset(c["ones16"][:, :], 1.0))
            link(pool.memset(c["mask"][:, :, :], 0.0))
            for half in (0, QT):
                local = c["mask"][half:half + QT, :, 0:LOCAL]
                link(pool.affine_select(out=local, in_=local, compare_op=ALU.is_ge, fill=MASKED,
                                        base=0, pattern=[[0, 2], [1, LOCAL]], channel_multiplier=-1))
                link(pool.affine_select(out=local, in_=local, compare_op=ALU.is_ge, fill=MASKED,
                                        base=2 * WINDOW, pattern=[[0, 2], [-1, LOCAL]],
                                        channel_multiplier=1))
            for t, base, step in ((c["first"], EXPERTS, -1), (c["base"], 0, TOK)):
                link(pool.iota(t[:, :], pattern=[[step, EXPERTS]], base=base, channel_multiplier=0,
                               allow_small_or_imprecise_dtypes=True))
            link(pool.memset(c["power"][:, :], -0.5))

        @block.sync
        def _(sp):
            sp.wait_ge(pool_done, FILL_LINKS)
            n = 0
            for name in ("list1", "list2"):
                sp.dma_start(scratch[name][0:LIST_PAD, :].rearrange("(p s) e -> p s e", p=P),
                             empty[:, :, :]).then_inc(filled, 16)
                sp.dma_start(scratch[name][LIST_PAD:LIST_PAD + SLOTS, :].rearrange("(p s) e -> p s e", p=1),
                             empty[0:1, 0:SLOTS, :]).then_inc(filled, 16)
                n += 2
            for name in ("xn1", "acc1", "xn2", "acc2"):
                for h in range(HALVES):
                    sp.dma_start(scratch[name][TOK + h * P:TOK + (h + 1) * P, :], zero32).then_inc(filled, 16)
                    n += 1
            ks = scratch["ks"].rearrange("(r p) (b t) -> r p b t", p=P, b=BATCH)
            zk = zeros[:, 0:BATCH * WINDOW].rearrange("p (b t) -> p b t", b=BATCH)
            for side in (0, SEQP - WINDOW):
                for r in range(2 * D // P):
                    sp.dma_start(ks[r, :, :, side:side + WINDOW], zk).then_inc(filled, 16)
                    n += 1
                vs = scratch["vs"].rearrange("(b t) n -> t b n", b=BATCH)
                sp.dma_start(vs[side:side + WINDOW, :, :],
                             zeros[0:WINDOW, :].rearrange("p (b n) -> p b n", b=BATCH)).then_inc(filled, 16)
                sp.dma_start(scratch["padk"][0:1, side:side + WINDOW], padk[0:1, 0:WINDOW]).then_inc(filled, 16)
                n += 2
            sp.dma_start(scratch["padk"][0:1, WINDOW:WINDOW + SEQ].rearrange("a (p s) -> (a p) s", p=16),
                         zeros[0:16, 0:SEQ // 16]).then_inc(filled, 16)
            n += 1
            sp.wait_ge(filled, 16 * n)



def group_turn(i, s):
    return i + s // 2, s % 2


def group_exists(i, s):
    return s >= 0 and (not isinstance(i, int) or 2 * i + s < GROUPS)


def group_steps(eng, ahead, step):
    for s in range(-ahead, 0):
        step(0, s)
    with eng.Fori(0, GROUPS // 2 - 2) as i:
        for s in range(2):
            step(i, s)
    for s in range(4):
        step(GROUPS // 2 - 2 + s // 2, s % 2)


CHOOSE_LINKS, ENTER_LINKS = 12, 4


def router_phase(nc, ctx, c, scratch, which, x_src, weights, cap=CAP):
    m = Memory(nc, ctx, f"route{which}")
    first_time = which == 1
    xn_d, acc_d, list_d = scratch[f"xn{which}"], scratch[f"acc{which}"], scratch[f"list{which}"]
    two = range(2)
    x = [m.sb(f"x{b}", [P, GROUP, D]) for b in two]
    xn = [m.sb(f"xn{b}", [P, GROUP, D]) for b in two]
    xnT = [m.sb(f"xnT{b}", [P, KD, GTOK]) for b in two]
    wr = m.sb("wr", [P, KD, EXPERTS])
    stats = [m.sb(f"stats{b}", [P, GROUP, 6]) for b in two]
    mv = [m.sb(f"mv{b}", [P, GROUP, 2]) for b in two]
    ve = [m.sb(f"ve{b}", [P, GROUP]) for b in two]
    rstd = [m.sb(f"rstd{b}", [P, GROUP]) for b in two]
    shift = [m.sb(f"shift{b}", [P, GROUP]) for b in two]
    logits = m.sb("logits", [P, GROUP, EXPERTS])
    best = m.sb("best", [P, 2, GROUP])
    key = m.sb("key", [P, GROUP, EXPERTS])
    keymax = m.sb("keymax", [P, GROUP])
    pick = [[m.sb(f"pick{b}{k}", [P, GROUP, EXPERTS]) for k in two] for b in two]
    rest = m.sb("rest", [P, GROUP, EXPERTS])
    ex = [m.sb(f"ex{b}", [P, GROUP, EXPERTS + 1]) for b in two]
    total = m.sb("total", [P, GROUP])
    chosen = [m.sb(f"chosen{b}", [P, GROUP, EXPERTS], BF16) for b in two]
    place = m.sb("place", [P, GROUP, EXPERTS])
    placed = m.sb("placed", [P, 2, GROUP, EXPERTS])
    slot = m.sb("slot", [P, 2, GROUP])
    run = m.sb("run", [P, EXPERTS])
    slot_i = [m.sb(f"slot_i{b}", [P, 2, GROUP], I32) for b in two]
    entry = [m.sb(f"entry{b}", [P, 2, GROUP, 2], I32) for b in two]
    psT = [m.ps(f"psT{k}") for k in range(KD)]
    psR = [m.ps(f"psR{b}") for b in two]

    def both(name):
        return [m.sem(f"{name}{b}") for b in two]

    x_in, xn_out, x_out = both("x_in"), both("xn_out"), both("x_out")
    list_out, list_base = c["list_out"], 16 * (GROUPS // 2) * (which - 1)
    wr_in, start, counted = m.sem("wr_in"), m.sem("start"), m.sem("counted")
    stats_ready, mean_ready, ve_ready, rstd_ready, shift_ready = (
        both("stats_ready"), both("mean_ready"), both("ve_ready"), both("rstd_ready"), both("shift_ready"))
    xn_ready, turned, kept0, kept1 = both("xn_ready"), both("turned"), both("kept0"), both("kept1")
    logits_ready, exp_in, exp_out = both("logits_ready"), both("exp_in"), both("exp_out")
    chosen_ready, places_ready, entries_ready = both("chosen_ready"), both("places_ready"), both("entries_ready")
    choosing, entering, tables = m.sem("choosing"), m.sem("entering"), m.sem("tables")
    counts_i = m.sb("counts_i", [1, EXPERTS], I32)
    tiles_of = m.sb("tiles_of", [1, EXPERTS])
    last = m.sb("last", [1, EXPERTS])
    ones = m.sb("ones", [1, EXPERTS])
    tile = m.sb("tile", [1, TILES])
    expert = m.sb("expert", [1, TILES])
    begin = m.sb("begin", [1, TILES])
    past = m.sb("past", [1, TILES])
    live = m.sb("live", [1, TILES])
    most = m.sb("most", [1, 1])
    if first_time:
        w32 = [m.sb(f"w32_{k}", [P, 2 * FFN]) for k in two]
        w_in, w_hi, w_lo = both("w_in"), both("w_hi"), both("w_lo")
        w_parts = (c["w1"], c["w2"])
    else:
        at = [m.sb(f"at{b}", [P, GROUP, D]) for b in two]
        atT = [m.sb(f"atT{h}", [P, KD, GTOK], FP16) for h in two]
        wout32 = m.sb("wout32", [P, KD, D])
        wout = m.sb("wout", [P, 2, KD, D], FP16)
        bout32 = m.sb("bout32", [1, D])
        bout = m.sb("bout", [1, 2, D], FP16)
        one_row = m.sb("one_row", [1, P], FP16)
        psA = [m.ps(f"psA{k}") for k in range(KD)]
        psP = [m.ps(f"psP{k}") for k in two]
        at_in, at_turned = both("at_in"), both("at_turned")
        at_hi, at_lo, projected, x_ready = both("at_hi"), both("at_lo"), both("projected"), both("x_ready")
        wout_in, wout_hi, wout_lo = m.sem("wout_in"), m.sem("wout_hi"), m.sem("wout_lo")
        WOUT_LOADS = 2 * PAIRS + 1

    def group(ap, g):
        return ap[0:TOK, :].rearrange("(g j p) d -> g p j d", p=P, j=GROUP)[bass.ds(g, 1)].rearrange(
            "a p j d -> p (a j) d")

    with nc.Block() as block:
        @block.sync
        def _(sp):
            sp.dma_start(wr[:, :, :], weights["wr"].rearrange("(k p) e -> p k e", p=P)).then_inc(wr_in, 16)
            if not first_time:
                for k in two:
                    for j in range(PAIRS):
                        sp.dma_start(wout32[j * HD:(j + 1) * HD, k, :],
                                     weights["wout"][(2 * j + k) * HD:(2 * j + k + 1) * HD, :]).then_inc(wout_in, 16)
                sp.dma_start(bout32[:, :], weights["bout"].unsqueeze(0)).then_inc(wout_in, 16)

            def store(i, s):
                i, b = group_turn(i, s)
                sp.wait_ge(xn_ready[b], i + 1)
                sp.dma_start(group(xn_d, 2 * i + b), xn[b][:, :, :]).then_inc(xn_out[b], 16)
                sp.dma_start(group(acc_d, 2 * i + b), x[b][:, :, :]).then_inc(x_out[b], 16)

            def load(i, s):
                i, b = group_turn(i, s)
                sp.wait_ge(x_out[b], 16 * i)
                sp.dma_start(x[b][:, :, :], group(x_src, 2 * i + b)).then_inc(x_in[b], 16)

            def load_attention(i, s):
                i, b = group_turn(i, s)
                sp.wait_ge(at_turned[b], i)
                sp.dma_start(at[b][:, :, :], group(scratch["att"], 2 * i + b)).then_inc(at_in[b], 16)

            def load_weights(i, s):
                i, b = group_turn(i, s)
                w, n = (weights["w1"], KD) if b == 0 else (weights["w2"], KF)
                sp.wait_ge(w_lo[b], i)
                sp.dma_start(w32[b][:, :].rearrange("p (k n) -> p k n", k=n),
                             w.rearrange("e (k p) n -> e p k n", p=P)[bass.ds(i, 1)].rearrange(
                                 "a p k n -> p (a k) n")).then_inc(w_in[b], 16)

            def step(i, s):
                if not first_time and group_exists(i, s + 4):
                    load_attention(i, s + 4)
                if group_exists(i, s + 2):
                    store(i, s + 2)
                if group_exists(i, s + 4):
                    load(i, s + 4)
                if first_time and group_exists(i, s + 3):
                    load_weights(i, s + 3)
            group_steps(sp, 4, step)
            for b in two:
                sp.wait_ge(xn_out[b], 16 * (GROUPS // 2))
                sp.wait_ge(x_out[b], 16 * (GROUPS // 2))

        @block.gpsimd
        def _(pool):
            pool.iota(c["token"][:, :], pattern=[[P, GROUP]], base=0, channel_multiplier=1,
                      allow_small_or_imprecise_dtypes=True).then_inc(start, 1)
            pool.iota(tile[:, :], pattern=[[1, TILES]], base=0, channel_multiplier=0,
                      allow_small_or_imprecise_dtypes=True).then_inc(start, 1)
            pool.memset(ones[:, :], 1.0).then_inc(start, 1)
            if not first_time:
                pool.memset(one_row[:, :], 1.0).then_inc(start, 1)

            def root(i, s):
                i, b = group_turn(i, s)
                pool.wait_ge(ve_ready[b], i + 1)
                pool.tensor_tensor(rstd[b][:, :], ve[b][:, :], c["power"][:, :], ALU.pow).then_inc(rstd_ready[b], 1)

            def send(i, s):
                i, b = group_turn(i, s)
                pool.wait_ge(entries_ready[b], i + 1)
                pool.nop(nofuse=True)
                for k in two:
                    for j in range(GROUP):
                        pool.indirect_dma_start(
                            out=list_d[:, :],
                            out_offset=bass.IndirectOffsetOnAxis(ap=slot_i[b][:, k, j:j + 1], axis=0),
                            in_=entry[b][:, k, j, :], in_offset=None).then_inc(list_out[b][k * GROUP + j], 16)

            def step(i, s):
                if group_exists(i, s + 3):
                    root(i, s + 3)
                if group_exists(i, s):
                    send(i, s)
            group_steps(pool, 3, step)
            for b in two:
                for done in list_out[b]:
                    pool.wait_ge(done, list_base + 16 * (GROUPS // 2))

        @block.scalar
        def _(act):
            if not first_time:
                act.wait_ge(wout_in, 16 * WOUT_LOADS)
                act.activation(bout[:, 0, :], bout32[:, :], ACT.Copy, scale=W_ATT)
                act.activation(wout[:, 0, :, :], wout32[:, :, :], ACT.Copy, scale=W_ATT).then_inc(wout_hi, 1)

            def attention_high(i, s):
                i, b = group_turn(i, s)
                act.wait_ge(at_turned[b], i + 1)
                act.wait_ge(projected[1 - b], i + b)
                for k in range(KD):
                    ins = act.activation(atT[0][:, k, :], psA[k][:, :], ACT.Copy)
                ins.then_inc(at_hi[b], 1)

            def normalise(i, s):
                i, b = group_turn(i, s)
                act.wait_ge(shift_ready[b], i + 1)
                act.wait_ge(turned[b], i)
                act.wait_ge(xn_out[b], 16 * i)
                for j in range(GROUP):
                    ins = act.activation(xn[b][:, j, :], x[b][:, j, :], ACT.Identity,
                                         scale=rstd[b][:, j:j + 1], bias=shift[b][:, j:j + 1])
                ins.then_inc(xn_ready[b], 1)

            def keep(i, s):
                i, b = group_turn(i, s)
                act.wait_ge(turned[b], i + 1)
                act.wait_ge(logits_ready[b], i)
                act.activation(xnT[b][:, 0, :], psT[0][:, :], ACT.Copy).then_inc(kept0[b], 1)

            def exponentials(i, s):
                i, b = group_turn(i, s)
                act.wait_ge(exp_in[b], i + 1)
                act.activation(ex[b][:, :, :], ex[b][:, :, :], ACT.Exp).then_inc(exp_out[b], 1)

            def weights_high(i, s):
                i, b = group_turn(i, s)
                act.wait_ge(w_in[b], 16 * i + 16)
                act.activation(w_parts[b][:, bass.ds(i, 1), 0, :].rearrange("p a n -> p (a n)"),
                               w32[b][:, :], ACT.Copy, scale=W_FFN).then_inc(w_hi[b], 1)

            def step(i, s):
                if not first_time and group_exists(i, s + 4):
                    attention_high(i, s + 4)
                if group_exists(i, s + 2):
                    keep(i, s + 2)
                if first_time and group_exists(i, s + 2):
                    weights_high(i, s + 2)
                if group_exists(i, s + 1):
                    exponentials(i, s + 1)
                if group_exists(i, s + 3):
                    normalise(i, s + 3)
            group_steps(act, 4, step)

        @block.tensor
        def _(pe):
            pe.wait_ge(wr_in, 16)
            if not first_time:
                pe.wait_ge(wout_lo, 1)

            def turn_attention(i, s):
                i, b = group_turn(i, s)
                pe.wait_ge(at_in[b], 16 * i + 16)
                pe.wait_ge(at_lo[1 - b], i + b)
                for j in range(GROUP):
                    for k in range(KD):
                        ins = pe.transpose(psA[k][:, j * P:(j + 1) * P], at[b][:, j, k * P:(k + 1) * P],
                                           c["ident"][:, :])
                ins.then_inc(at_turned[b], 1)

            def project(i, s):
                i, b = group_turn(i, s)
                pe.wait_ge(at_lo[b], i + 1)
                pe.wait_ge(x_ready[1 - b], i + b)
                for j in range(GROUP):
                    out = psP[j // 2][:, (j % 2) * D:(j % 2 + 1) * D]
                    for h in two:
                        pe.matmul(out, one_row[:, :], bout[:, h, :], start=(h == 0), stop=False)
                    for k in range(KD):
                        for ah, wh in ((0, 0), (0, 1), (1, 0)):
                            ins = pe.matmul(out, atT[ah][:, k, j * P:(j + 1) * P], wout[:, wh, k, :],
                                            start=False, stop=(k == KD - 1 and ah == 1))
                ins.then_inc(projected[b], 1)

            def turn(i, s):
                i, b = group_turn(i, s)
                pe.wait_ge(xn_ready[b], i + 1)
                pe.wait_ge(kept0[1 - b], i + b)
                pe.wait_ge(kept1[1 - b], i + b)
                for j in range(GROUP):
                    for k in range(KD):
                        ins = pe.transpose(psT[k][:, j * P:(j + 1) * P], xn[b][:, j, k * P:(k + 1) * P],
                                           c["ident"][:, :])
                ins.then_inc(turned[b], 1)

            def score(i, s):
                i, b = group_turn(i, s)
                pe.wait_ge(kept0[b], i + 1)
                pe.wait_ge(kept1[b], i + 1)
                pe.wait_ge(entries_ready[b], i)
                for j in range(GROUP):
                    for k in range(KD):
                        ins = pe.matmul(psR[b][:, j * EXPERTS:(j + 1) * EXPERTS], xnT[b][:, k, j * P:(j + 1) * P],
                                        wr[:, k, :], start=(k == 0), stop=(k == KD - 1))
                ins.then_inc(logits_ready[b], 1)

            def places(i, s):
                i, b = group_turn(i, s)
                pe.wait_ge(chosen_ready[b], i + 1)
                for j in range(GROUP):
                    out = psR[b][:, 64 + j * EXPERTS:64 + (j + 1) * EXPERTS]
                    pe.matmul(out, c["before"][:, :], chosen[b][:, j, :], start=True, stop=(j == 0))
                    for earlier in range(j):
                        pe.matmul(out, c["ones16"][:, :], chosen[b][:, earlier, :], start=False,
                                  stop=(earlier == j - 1))
                for j in range(GROUP):
                    ins = pe.matmul(psR[b][:, 128:128 + EXPERTS], c["ones16"][:, :], chosen[b][:, j, :],
                                    start=(j == 0), stop=(j == GROUP - 1))
                ins.then_inc(places_ready[b], 1)

            def step(i, s):
                if not first_time and group_exists(i, s + 4):
                    turn_attention(i, s + 4)
                if group_exists(i, s + 2):
                    turn(i, s + 2)
                if not first_time and group_exists(i, s + 4):
                    project(i, s + 4)
                if group_exists(i, s + 1):
                    places(i, s + 1)
                if group_exists(i, s + 2):
                    score(i, s + 2)
            group_steps(pe, 4, step)

        @block.vector
        def _(dve):
            dve.wait_ge(start, 3 if first_time else 4)
            dve.tensor_copy(run[:, :], c["base"][:, :]).then_inc(counted, 1)
            dve.wait_ge(counted, 1)
            if not first_time:
                dve.wait_ge(wout_hi, 1)
                dve.scalar_tensor_tensor(bout[:, 1, :], bout32[:, :], W_ATT, bout[:, 0, :], ALU.mult, ALU.subtract)
                dve.scalar_tensor_tensor(wout[:, 1, :, :], wout32[:, :, :], W_ATT, wout[:, 0, :, :],
                                         ALU.mult, ALU.subtract).then_inc(wout_lo, 1)

            def wide(t):
                return t.unsqueeze(2).to_broadcast([P, GROUP, EXPERTS])

            def over(t):
                return t[:, :].unsqueeze(1).to_broadcast([P, GROUP, EXPERTS])

            def attention_low(i, s):
                i, b = group_turn(i, s)
                dve.wait_ge(at_hi[b], i + 1)
                for k in range(KD):
                    ins = dve.tensor_tensor(atT[1][:, k, :], psA[k][:, :], atT[0][:, k, :], ALU.subtract)
                ins.then_inc(at_lo[b], 1)

            def add_projection(i, s):
                i, b = group_turn(i, s)
                dve.wait_ge(projected[b], i + 1)
                dve.wait_ge(x_in[b], 16 * i + 16)
                for h in range(GROUP // 2):
                    rows = x[b][:, 2 * h:2 * h + 2, :].rearrange("p j d -> p (j d)")
                    ins = dve.scalar_tensor_tensor(rows, psP[h][:, :], 1.0 / W_ATT, rows, ALU.mult, ALU.add)
                ins.then_inc(x_ready[b], 1)

            def statistics(i, s):
                i, b = group_turn(i, s)
                if first_time:
                    dve.wait_ge(x_in[b], 16 * i + 16)
                else:
                    dve.wait_ge(x_ready[b], i + 1)
                for j in range(GROUP):
                    ins = dve.bn_stats(stats[b][:, j, :], x[b][:, j, :])
                ins.then_inc(stats_ready[b], 1)
                dve.wait_ge(stats_ready[b], i + 1)
                dve.nop(nofuse=True)
                for j in range(GROUP):
                    ins = dve.bn_aggr(mv[b][:, j, :], stats[b][:, j, :])
                ins.then_inc(mean_ready[b], 1)
                dve.wait_ge(mean_ready[b], i + 1)
                dve.tensor_scalar(ve[b][:, :], mv[b][:, :, 1], EPS, None, ALU.add).then_inc(ve_ready[b], 1)

            def shifts(i, s):
                i, b = group_turn(i, s)
                dve.wait_ge(rstd_ready[b], i + 1)
                dve.scalar_tensor_tensor(shift[b][:, :], mv[b][:, :, 0], -1.0, rstd[b][:, :],
                                         ALU.mult, ALU.mult).then_inc(shift_ready[b], 1)

            def keep(i, s):
                i, b = group_turn(i, s)
                dve.wait_ge(turned[b], i + 1)
                dve.wait_ge(logits_ready[b], i)
                dve.tensor_copy(xnT[b][:, 1, :], psT[1][:, :]).then_inc(kept1[b], 1)

            def weights_low(i, s):
                i, b = group_turn(i, s)
                dve.wait_ge(w_hi[b], i + 1)
                dve.scalar_tensor_tensor(
                    w_parts[b][:, bass.ds(i, 1), 1, :].rearrange("p a n -> p (a n)"), w32[b][:, :], W_FFN,
                    w_parts[b][:, bass.ds(i, 1), 0, :].rearrange("p a n -> p (a n)"),
                    ALU.mult, ALU.subtract).then_inc(w_lo[b], 1)

            def choose(i, s):
                i, b = group_turn(i, s)
                link = Chain(dve, choosing, CHOOSE_LINKS * (2 * i + b))
                dve.wait_ge(logits_ready[b], i + 1)
                link(dve.tensor_copy(logits[:, :, :].rearrange("p j e -> p (j e)"), psR[b][:, 0:GROUP * EXPERTS]))
                for k in two:
                    of = logits if k == 0 else rest
                    link(dve.tensor_reduce(best[:, k, :], of[:, :, :], AX.X, ALU.max))
                    link(dve.tensor_tensor(key[:, :, :], of[:, :, :], wide(best[:, k, :]), ALU.is_equal))
                    link(dve.tensor_tensor(key[:, :, :], key[:, :, :], over(c["first"]), ALU.mult))
                    link(dve.tensor_reduce(keymax[:, :], key[:, :, :], AX.X, ALU.max))
                    link(dve.tensor_tensor(pick[b][k][:, :, :], key[:, :, :], wide(keymax[:, :]), ALU.is_equal))
                    if k == 0:
                        link(dve.scalar_tensor_tensor(rest[:, :, :], pick[b][0][:, :, :], MASKED,
                                                      logits[:, :, :], ALU.mult, ALU.add))
                assert link.n == CHOOSE_LINKS, link.n
                dve.tensor_tensor(chosen[b][:, :, :], pick[b][0][:, :, :], pick[b][1][:, :, :],
                                  ALU.add).then_inc(chosen_ready[b], 1)
                dve.tensor_tensor(ex[b][:, :, 0:EXPERTS], logits[:, :, :], wide(best[:, 0, :]), ALU.subtract)
                dve.tensor_tensor(ex[b][:, :, EXPERTS], best[:, 1, :], best[:, 0, :],
                                  ALU.subtract).then_inc(exp_in[b], 1)

            def enter(i, s):
                i, b = group_turn(i, s)
                link = Chain(dve, entering, ENTER_LINKS * (2 * i + b))
                for done in list_out[b]:
                    dve.wait_ge(done, list_base + 16 * i)
                dve.wait_ge(exp_out[b], i + 1)
                dve.wait_ge(places_ready[b], i + 1)
                dve.tensor_reduce(total[:, :], ex[b][:, :, 0:EXPERTS], AX.X, ALU.add)
                link(dve.tensor_tensor(place[:, :, :], psR[b][:, 64:64 + GROUP * EXPERTS].rearrange(
                    "p (j e) -> p j e", j=GROUP), over(run), ALU.add))
                dve.tensor_tensor(run[:, :], run[:, :], psR[b][:, 128:128 + EXPERTS], ALU.add)
                dve.reciprocal(total[:, :], total[:, :])
                for k in two:
                    ins = dve.tensor_tensor(placed[:, k, :, :], pick[b][k][:, :, :], place[:, :, :], ALU.mult)
                link(ins)
                dve.tensor_scalar(entry[b][:, 0, :, 1].bitcast(FP32), total[:, :], GATE_SCALE, None, ALU.mult)
                dve.scalar_tensor_tensor(entry[b][:, 1, :, 1].bitcast(FP32), ex[b][:, :, EXPERTS], GATE_SCALE,
                                         total[:, :], ALU.mult, ALU.mult)
                link(dve.tensor_reduce(slot[:, :, :], placed[:, :, :, :], AX.X, ALU.add))
                for k in two:
                    dve.tensor_copy(entry[b][:, k, :, 0], c["token"][:, :])
                link(dve.tensor_copy(slot_i[b][:, :, :], slot[:, :, :]))
                dve.tensor_scalar(c["token"][:, :], c["token"][:, :], float(GTOK), None,
                                  ALU.add).then_inc(entries_ready[b], 1)
                dve.wait_ge(entries_ready[b], i + 1)
                assert link.n == ENTER_LINKS, link.n

            def step(i, s):
                if group_exists(i, s):
                    enter(i, s)
                if group_exists(i, s + 3):
                    statistics(i, s + 3)
                if not first_time and group_exists(i, s + 4):
                    attention_low(i, s + 4)
                if group_exists(i, s + 1):
                    choose(i, s + 1)
                if group_exists(i, s + 3):
                    shifts(i, s + 3)
                if group_exists(i, s + 2):
                    keep(i, s + 2)
                if first_time and group_exists(i, s + 2):
                    weights_low(i, s + 2)
                if not first_time and group_exists(i, s + 4):
                    add_projection(i, s + 4)
            group_steps(dve, 4, step)
            link = Chain(dve, tables)
            link(dve.tensor_tensor(c["count"][:, :], run[:, :], c["base"][:, :], ALU.subtract))
            count = c["count"][0:1, :]
            link(dve.tensor_reduce(most[:, :], count, AX.X, ALU.max))
            link(dve.tensor_scalar(c["over_cap"][:, :], most[:, :], float(cap), None, ALU.is_gt))
            link(dve.tensor_scalar(counts_i[:, :], count, float(SLOTS - 1), None, ALU.add))
            link(dve.tensor_scalar(counts_i[:, :], counts_i[:, :], SLOTS.bit_length() - 1, None,
                                   ALU.arith_shift_right))
            link(dve.tensor_copy(tiles_of[:, :], counts_i[:, :]))
            link(dve.tensor_tensor_scan(last[:, :], ones[:, :], tiles_of[:, :], 0.0, ALU.mult, ALU.add))
            link(dve.memset(expert[:, :], 0.0))
            link(dve.memset(begin[:, :], 0.0))
            for e in range(EXPERTS - 1):
                link(dve.tensor_scalar(past[:, :], tile[:, :], last[:, e:e + 1], None, ALU.is_ge))
                link(dve.tensor_tensor(expert[:, :], expert[:, :], past[:, :], ALU.add))
                link(dve.scalar_tensor_tensor(begin[:, :], past[:, :], tiles_of[:, e:e + 1], begin[:, :],
                                              ALU.mult, ALU.add))
            link(dve.tensor_tensor(begin[:, :], tile[:, :], begin[:, :], ALU.subtract))
            link(dve.tensor_scalar(begin[:, :], begin[:, :], float(SLOTS), float(-LIST_PAD), ALU.mult, ALU.add))
            link(dve.scalar_tensor_tensor(begin[:, :], expert[:, :], float(TOK), begin[:, :], ALU.mult, ALU.add))
            link(dve.tensor_scalar(live[:, :], tile[:, :], last[:, EXPERTS - 1:EXPERTS], None, ALU.is_lt))
            link(dve.tensor_tensor(begin[:, :], begin[:, :], live[:, :], ALU.mult))
            link(dve.tensor_scalar(c["start_of"][:, :], begin[:, :], float(LIST_PAD), None, ALU.add))
            link(dve.tensor_copy(c["expert_of"][:, :], expert[:, :]))
            link(dve.tensor_copy(c["in_use"][:, :], live[:, :]))


SEARCH_BITS = 31
SEARCH_LINKS = 5


def capacity_phase(nc, ctx, c, scratch, which, cap=CAP):
    m = Memory(nc, ctx, f"cap{which}")
    over_cap, iotas = c["over_cap"], m.sem("iotas")
    S = TOK * EXPERTS // P
    entries = m.sb("entries", [P, S, 2], I32)
    gates = m.sb("gates", [P, S])
    above = m.sb("above", [P, S])
    equal = m.sb("equal", [P, S])
    rank = m.sb("rank", [P, S])
    one_row = m.sb("one_row", [P, S])
    same = m.sb("same", [P, P])
    earlier = m.sb("earlier", [P, P])
    bit = m.sb("bit", [P, 1], I32)
    one_i = m.sb("one_i", [P, 1], I32)
    floor_i = m.sb("floor_i", [P, 1], I32)
    guess = m.sb("guess", [P, 1], I32)
    in_row = m.sb("in_row", [P, 2])
    enough = m.sb("enough", [P, 1], I32)
    room = m.sb("room", [P, 1])
    ps = m.ps("ps", [P, 512])
    entries_in, entries_out = m.sem("entries_in"), m.sem("entries_out")
    rows_ready, sums_ready = m.sem("rows_ready"), m.sem("sums_ready")
    search, gates_done = m.sem("search"), m.sem("gates_done")
    pool_links = 8
    lists = scratch[f"list{which}"][0:LIST_PAD, :].rearrange("(p s) e -> p s e", p=P)

    with nc.Block() as block:
        @block.gpsimd
        def _(pool):
            link = Chain(pool, iotas)
            for t, least in ((same, 0), (earlier, 1)):
                v = t[:, :].rearrange("p (e r) -> p e r", r=P // EXPERTS)
                link(pool.memset(t[:, :], 1.0))
                link(pool.affine_select(out=v, in_=v, compare_op=ALU.is_ge, fill=0.0, base=0,
                                        pattern=[[-(P // EXPERTS), EXPERTS], [0, P // EXPERTS]],
                                        channel_multiplier=1))
                end = P // EXPERTS - 1 if least == 0 else -1
                link(pool.affine_select(out=v, in_=v, compare_op=ALU.is_ge, fill=0.0, base=end,
                                        pattern=[[P // EXPERTS, EXPERTS], [least, P // EXPERTS]],
                                        channel_multiplier=-1))
            link(pool.memset(one_row[:, :], 1.0))
            link(pool.memset(one_i[:, :], 1))
            assert link.n == pool_links, link.n

        @block.vector
        def _(dve):
            flag = dve.value_load(over_cap[0:1, 0:1], min_val=0, max_val=1)
            with dve.If(flag > 0):
                s = Chain(dve, search)
                dve.wait_ge(iotas, pool_links)
                dve.wait_ge(entries_in, 16)
                s(dve.tensor_copy(gates[:, :], entries[:, :, 1].bitcast(FP32)))
                s(dve.memset(floor_i[:, :], 0))
                s(dve.memset(bit[:, :], 1 << (SEARCH_BITS - 1)))
                with dve.Fori(0, SEARCH_BITS) as i:
                    t = Chain(dve, search, 3 + i * SEARCH_LINKS)
                    t(dve.tensor_tensor(guess[:, :], floor_i[:, :], bit[:, :], ALU.bitwise_or))
                    dve.tensor_scalar(above[:, :], gates[:, :], guess[:, :].bitcast(FP32), None, ALU.is_ge, ALU.add,
                                      accum_out=in_row[:, 0:1]).then_inc(rows_ready, 1)
                    dve.wait_ge(sums_ready, i + 1)
                    t(dve.tensor_scalar(enough[:, :], ps[:, 0:1], float(cap), -1.0, ALU.is_ge, ALU.mult))
                    t(dve.tensor_tensor(enough[:, :], enough[:, :], bit[:, :], ALU.bitwise_and))
                    t(dve.tensor_tensor(floor_i[:, :], floor_i[:, :], enough[:, :], ALU.bitwise_or))
                    t(dve.tensor_tensor(bit[:, :], bit[:, :], one_i[:, :], ALU.logical_shift_right))
                    assert t.n == SEARCH_LINKS
                s = Chain(dve, search, 3 + SEARCH_BITS * SEARCH_LINKS)
                level = floor_i[:, :].bitcast(FP32)
                s(dve.tensor_scalar(above[:, :], gates[:, :], level, None, ALU.is_gt, ALU.add,
                                    accum_out=in_row[:, 0:1]))
                s(dve.tensor_scalar(equal[:, :], gates[:, :], level, None, ALU.is_equal, ALU.add,
                                    accum_out=in_row[:, 1:2]))
                dve.sem_inc(rows_ready, 1)
                dve.wait_ge(sums_ready, SEARCH_BITS + 1)
                s(dve.tensor_scalar(room[:, :], ps[:, 0:1], -1.0, float(cap), ALU.mult, ALU.add))
                s(dve.tensor_tensor(room[:, :], room[:, :], ps[:, 1:2], ALU.subtract))
                s(dve.tensor_tensor_scan(rank[:, :], one_row[:, :], equal[:, :], 0.0, ALU.mult, ALU.add))
                s(dve.scalar_tensor_tensor(equal[:, :], rank[:, :], room[:, :], equal[:, :], ALU.is_le, ALU.mult))
                s(dve.tensor_tensor(above[:, :], above[:, :], equal[:, :], ALU.add))
                s(dve.tensor_tensor(entries[:, :, 1].bitcast(FP32), gates[:, :], above[:, :], ALU.mult))
                dve.sem_inc(gates_done, 1)

        @block.tensor
        def _(pe):
            flag = pe.value_load(over_cap[0:1, 0:1], min_val=0, max_val=1)
            with pe.If(flag > 0):
                with pe.Fori(0, SEARCH_BITS) as i:
                    pe.wait_ge(rows_ready, i + 1)
                    pe.matmul(ps[:, 0:1], same[:, :], in_row[:, 0:1], start=True, stop=True).then_inc(sums_ready, 1)
                pe.wait_ge(rows_ready, SEARCH_BITS + 1)
                pe.matmul(ps[:, 0:1], same[:, :], in_row[:, 0:1], start=True, stop=True)
                pe.matmul(ps[:, 1:2], earlier[:, :], in_row[:, 1:2], start=True, stop=True).then_inc(sums_ready, 1)

        @block.sync
        def _(sp):
            flag = sp.value_load(over_cap[0:1, 0:1], min_val=0, max_val=1)
            with sp.If(flag > 0):
                sp.dma_start(entries[:, :, :], lists).then_inc(entries_in, 16)
                sp.wait_ge(gates_done, 1)
                sp.dma_start(lists, entries[:, :, :]).then_inc(entries_out, 16)
                sp.wait_ge(entries_out, 16)


def ffn_phase(nc, ctx, c, scratch, which):
    m = Memory(nc, ctx, f"ffn{which}")
    xn_d, acc_d, list_d = scratch[f"xn{which}"], scratch[f"acc{which}"], scratch[f"list{which}"]
    two = range(2)
    PAIRS_F = KF // 2
    wanted = [m.sb(f"wanted{b}", [P, HALVES, 2], I32) for b in two]
    entry = [m.sb(f"entry{b}", [P, HALVES, 2], I32) for b in two]
    x = [m.sb(f"x{b}", [P, HALVES, D]) for b in two]
    xT = [[m.sb(f"xT{b}{h}", [P, KD, SLOTS], FP16) for h in two] for b in two]
    hT = [[m.sb(f"hT{b}{h}", [P, KF, SLOTS], FP16) for h in two] for b in two]
    y = [m.sb(f"y{b}", [P, HALVES, D]) for b in two]
    psT = m.ps("psT")
    psH = [m.ps(f"psH{f}") for f in range(PAIRS_F)]
    psY = [m.ps(f"psY{b}") for b in two]

    def both(name):
        return [m.sem(f"{name}{b}") for b in two]

    wanted_in = both("wanted_in")
    entry_in, turned, xT_hi, xT_lo = both("entry_in"), both("turned"), both("xT_hi"), both("xT_lo")
    summed, y_ready = both("summed"), both("y_ready")
    x_in, added = c[f"x_in{which}"], c[f"added{which}"]
    hidden = [m.sem(f"hidden{f}") for f in range(PAIRS_F)]
    h_hi = [m.sem(f"h_hi{f}") for f in range(PAIRS_F)]
    h_lo = [m.sem(f"h_lo{f}") for f in range(PAIRS_F)]

    def tile_loop(eng, body, between=None):
        with eng.Fori(0, FULL_TILES // 2) as i:
            for b in two:
                body(2 * i + b, i, b)
        if between is not None:
            between()
        for n in range(FULL_TILES, TILES):
            used = eng.value_load(c["in_use"][0:1, n:n + 1], min_val=0, max_val=1)
            with eng.If(used > 0):
                body(n, n // 2, n % 2)

    def follows(n, by):
        return not isinstance(n, int) or n + by < TILES

    with nc.Block() as block:
        @block.sync
        def _(sp):
            def load_entries(dst, n, done):
                start = sp.value_load(c["start_of"][0:1, bass.ds(n, 1)], min_val=0, max_val=LIST_PAD)
                sp.dma_start(dst[:, :, :],
                             list_d[bass.ds(start, SLOTS), :].rearrange("(h p) e -> p h e", p=P)).then_inc(done, 16)

            def tile(n, i, b):
                if follows(n, 2):
                    for h in two:
                        sp.wait_ge(x_in[b][h], 16 * i + 16)
                    load_entries(wanted[b], n + 2, wanted_in[b])
                for h in two:
                    sp.wait_ge(added[b][h], 16 * i)
                load_entries(entry[b], n, entry_in[b])

            for b in two:
                load_entries(wanted[b], b, wanted_in[b])
            tile_loop(sp, tile)

        @block.gpsimd
        def _(pool):
            def gather(i, b):
                pool.wait_ge(wanted_in[b], 16 * i + 16)
                pool.wait_ge(turned[b], i)
                pool.nop(nofuse=True)
                for h in two:
                    pool.indirect_dma_start(
                        out=x[b][:, h, :], out_offset=None, in_=xn_d[:, :],
                        in_offset=bass.IndirectOffsetOnAxis(ap=wanted[b][:, h, 0:1], axis=0)
                    ).then_inc(x_in[b][h], 16)

            def tile(n, i, b):
                if follows(n, 2):
                    gather(i + 1, b)
                pool.wait_ge(y_ready[b], i + 1)
                pool.wait_ge(entry_in[b], 16 * i + 16)
                for h in two:
                    pool.wait_ge(added[1 - b][h], 16 * (i + b))
                pool.nop(nofuse=True)
                for h in two:
                    pool.indirect_dma_start(
                        out=acc_d[:, :], in_=y[b][:, h, :], in_offset=None, compute_op=ALU.add,
                        out_offset=bass.IndirectOffsetOnAxis(ap=entry[b][:, h, 0:1], axis=0)
                    ).then_inc(added[b][h], 16)
                if isinstance(n, int):
                    landed(n)

            def landed(n):
                for t in (n - 1, n):
                    for h in two:
                        pool.wait_ge(added[t % 2][h], 16 * (t // 2 + 1))
                for t in range(n + 1, min(n + 3, TILES)):
                    for h in two:
                        pool.wait_ge(x_in[t % 2][h], 16 * (t // 2 + 1))

            for b in two:
                gather(0, b)
            tile_loop(pool, tile, lambda: landed(FULL_TILES - 1))

        @block.tensor
        def _(pe):
            def turn_tokens(i, b):
                for h in two:
                    pe.wait_ge(x_in[b][h], 16 * i + 16)
                pe.wait_ge(xT_hi[1 - b], i + b)
                pe.wait_ge(xT_lo[1 - b], i + b)
                for k in range(KD):
                    for h in two:
                        ins = pe.transpose(psT[:, k * SLOTS + h * P:k * SLOTS + (h + 1) * P],
                                           x[b][:, h, k * P:(k + 1) * P], c["ident"][:, :])
                ins.then_inc(turned[b], 1)

            def tile(n, i, b):
                e = pe.value_load(c["expert_of"][0:1, bass.ds(n, 1)], min_val=0, max_val=EXPERTS - 1)
                w1 = c["w1"][:, bass.ds(e, 1), :, :].rearrange("p a h n -> p (a h) n")
                w2 = c["w2"][:, bass.ds(e, 1), :, :].rearrange("p a h n -> p (a h) n")
                terms = ((0, 0), (0, 1), (1, 0))
                pe.wait_ge(xT_hi[b], i + 1)
                pe.wait_ge(xT_lo[b], i + 1)
                for f2 in range(PAIRS_F):
                    pe.wait_ge(h_hi[f2], n)
                    pe.wait_ge(h_lo[f2], n)
                    for f in two:
                        col = (2 * f2 + f) * P
                        for k in range(KD):
                            for wh, xh in terms:
                                ins = pe.matmul(psH[f2][:, f * SLOTS:(f + 1) * SLOTS],
                                                w1[:, wh, k * FFN + col:k * FFN + col + P], xT[b][xh][:, k, :],
                                                start=(k == 0 and (wh, xh) == terms[0]),
                                                stop=(k == KD - 1 and (wh, xh) == terms[-1]))
                    ins.then_inc(hidden[f2], 1)
                if follows(n, 1):
                    turn_tokens(i + b, 1 - b)
                pe.wait_ge(y_ready[b], i)
                for h in two:
                    for f in range(KF):
                        if h == 0 and f % 2 == 0:
                            pe.wait_ge(h_hi[f // 2], n + 1)
                            pe.wait_ge(h_lo[f // 2], n + 1)
                        for wh, hh in terms:
                            ins = pe.matmul(psY[b][:, h * D:(h + 1) * D], hT[b][hh][:, f, h * P:(h + 1) * P],
                                            w2[:, wh, f * D:(f + 1) * D],
                                            start=(f == 0 and (wh, hh) == terms[0]),
                                            stop=(f == KF - 1 and (wh, hh) == terms[-1]))
                ins.then_inc(summed[b], 1)

            turn_tokens(0, 0)
            tile_loop(pe, tile)

        @block.scalar
        def _(act):
            def tokens_hi(i, b):
                act.wait_ge(turned[b], i + 1)
                act.activation(xT[b][0][:, :, :].rearrange("p k n -> p (k n)"), psT[:, :],
                               ACT.Copy).then_inc(xT_hi[b], 1)

            def tile(n, i, b):
                for f2 in range(PAIRS_F):
                    act.wait_ge(hidden[f2], n + 1)
                    act.activation(hT[b][0][:, 2 * f2:2 * f2 + 2, :].rearrange("p f n -> p (f n)"),
                                   psH[f2][:, :], ACT.Relu).then_inc(h_hi[f2], 1)
                if follows(n, 1):
                    tokens_hi(i + b, 1 - b)
                act.wait_ge(summed[b], i + 1)
                act.wait_ge(entry_in[b], 16 * i + 16)
                for h in two:
                    act.wait_ge(added[b][h], 16 * i)
                for h in two:
                    ins = act.activation(y[b][:, h, :], psY[b][:, h * D:(h + 1) * D], ACT.Copy,
                                         scale=entry[b][:, h, 1:2].bitcast(FP32))
                ins.then_inc(y_ready[b], 1)

            tokens_hi(0, 0)
            tile_loop(act, tile)

        @block.vector
        def _(dve):
            def tokens_lo(i, b):
                dve.wait_ge(xT_hi[b], i + 1)
                dve.tensor_tensor(xT[b][1][:, :, :].rearrange("p k n -> p (k n)"), psT[:, :],
                                  xT[b][0][:, :, :].rearrange("p k n -> p (k n)"),
                                  ALU.subtract).then_inc(xT_lo[b], 1)

            def tile(n, i, b):
                for f2 in range(PAIRS_F):
                    dve.wait_ge(h_hi[f2], n + 1)
                    dve.scalar_tensor_tensor(
                        hT[b][1][:, 2 * f2:2 * f2 + 2, :].rearrange("p f n -> p (f n)"), psH[f2][:, :], 0.0,
                        hT[b][0][:, 2 * f2:2 * f2 + 2, :].rearrange("p f n -> p (f n)"),
                        ALU.max, ALU.subtract).then_inc(h_lo[f2], 1)
                if follows(n, 1):
                    tokens_lo(i + b, 1 - b)

            tokens_lo(0, 0)
            tile_loop(dve, tile)


def qkv_phase(nc, ctx, c, scratch, weights):
    m = Memory(nc, ctx, "qkv")
    two = range(2)
    NG = 3 * D + 1
    W_COLUMNS = ((0, D, W_ATT), (D, 2 * D, W_ATT * SCORE_SCALE), (2 * D, NG, W_ATT))
    x = [m.sb(f"x{b}", [P, GROUP, D]) for b in two]
    xn = [m.sb(f"xn{b}", [P, GROUP, D]) for b in two]
    xT = [[m.sb(f"xT{b}{h}", [P, KD, GTOK], FP16) for h in two] for b in two]
    stats = [m.sb(f"stats{b}", [P, GROUP, 6]) for b in two]
    mv = [m.sb(f"mv{b}", [P, GROUP, 2]) for b in two]
    ve = [m.sb(f"ve{b}", [P, GROUP]) for b in two]
    rstd = [m.sb(f"rstd{b}", [P, GROUP]) for b in two]
    shift = [m.sb(f"shift{b}", [P, GROUP]) for b in two]
    w32 = m.sb("w32", [P, KD, NG])
    w = m.sb("w", [P, 2, KD, NG + 1], FP16)
    bias_qk = m.sb("bias_qk", [P, 4])
    bias_v = m.sb("bias_v", [P, D])
    bias_g = m.sb("bias_g", [P, 1])
    qk = [m.sb(f"qk{b}", [P, 4, 2, GTOK], FP16) for b in two]
    v32 = [m.sb(f"v32{b}", [P, GROUP, D]) for b in two]
    vrow = [m.sb(f"vrow{b}", [P, GROUP, VROW], FP16) for b in two]
    z = [m.sb(f"z{b}", [P, GROUP]) for b in two]
    gate = [m.sb(f"gate{b}", [P, GROUP, 2]) for b in two]
    psT = [m.ps(f"psT{k}") for k in range(KD)]
    psQ = [m.ps(f"psQ{k}") for k in two]
    psV = [m.ps(f"psV{k}") for k in range(GROUP)]

    def both(name):
        return [m.sem(f"{name}{b}") for b in two]

    stats_ready, mean_ready, z_ready, gate_there = (
        both("stats_ready"), both("mean_ready"), both("z_ready"), both("gate_there"))
    w_in, w_hi, w_lo, consts, chain = m.sem("w_in"), m.sem("w_hi"), m.sem("w_lo"), m.sem("consts"), m.sem("chain")
    x_in, ve_ready, rstd_ready, shift_ready, xn_ready = (
        both("x_in"), both("ve_ready"), both("rstd_ready"), both("shift_ready"), both("xn_ready"))
    turned, xT_hi, xT_lo = both("turned"), both("xT_hi"), both("xT_lo")
    qk_sum, qk_hi, qk_lo = both("qk_sum"), both("qk_hi"), both("qk_lo")
    qk_out, v_out, gate_out = both("qk_out"), both("v_out"), both("gate_out")
    v_sum, v_ready, v_hi, v_rows = both("v_sum"), both("v_ready"), both("v_hi"), both("v_rows")
    exp_ready, gate_ready = both("exp_ready"), both("gate_ready")
    turns = GROUPS // 2

    def group(ap, g):
        return ap[0:TOK, :].rearrange("(g j p) d -> g p j d", p=P, j=GROUP)[bass.ds(g, 1)].rearrange(
            "a p j d -> p (a j) d")

    with nc.Block() as block:
        @block.sync
        def _(sp):
            sp.dma_start(w32[:, :, 0:3 * D], weights["wqkv"].rearrange("(k p) n -> p k n", p=P)).then_inc(w_in, 16)
            sp.dma_start(w32[:, :, 3 * D:NG], weights["wg"].rearrange("(k p) n -> p k n", p=P),
                         allow_slow_non_contiguous=True).then_inc(w_in, 16)
            sp.dma_start(bias_qk[:, :], weights["bqkv"][0:2 * D].rearrange("(c p) -> p c", p=P),
                         allow_slow_non_contiguous=True).then_inc(w_in, 16)
            sp.dma_start(bias_v[:, :], weights["bqkv"][2 * D:3 * D].partition_broadcast(P)).then_inc(w_in, 16)
            sp.dma_start(bias_g[:, :], weights["bg"].partition_broadcast(P)).then_inc(w_in, 16)

            def load(i, s):
                i, b = group_turn(i, s)
                sp.wait_ge(xn_ready[b], i)
                sp.dma_start(x[b][:, :, :], group(scratch["acc1"], 2 * i + b)).then_inc(x_in[b], 16)

            def store(i, s):
                i, b = group_turn(i, s)
                tok = 2 * GTOK * i + GTOK * b
                padded = tok + 2 * WINDOW * (i // (SEQ // GTOK // 2)) + WINDOW
                for half in two:
                    rows = scratch["qs" if half == 0 else "ks"].rearrange("(h r p) t -> r p h t", h=2, p=P)
                    first = tok if half == 0 else padded
                    for r in range(KD):
                        n = 2 * half + r
                        sp.wait_ge(qk_hi[n % 2], 4 * i + 2 * b + n // 2 + 1)
                        sp.wait_ge(qk_lo[n % 2], 4 * i + 2 * b + n // 2 + 1)
                        sp.dma_start(rows[r][:, :, bass.ds(first, GTOK)], qk[b][:, n, :, :]).then_inc(qk_out[b], 16)
                sp.wait_ge(v_rows[b], i + 1)
                sp.dma_start(scratch["vs"][bass.ds(padded, GTOK), :].rearrange("(j p) n -> p j n", p=P),
                             vrow[b][:, :, :]).then_inc(v_out[b], 16)
                sp.wait_ge(gate_ready[b], i + 1)
                sp.dma_start(group(scratch["gate"], 2 * i + b), gate[b][:, :, :]).then_inc(gate_out[b], 16)

            def step(i, s):
                if group_exists(i, s + 3):
                    load(i, s + 3)
                if group_exists(i, s):
                    store(i, s)
            group_steps(sp, 3, step)
            for b in two:
                sp.wait_ge(qk_out[b], 64 * turns)
                sp.wait_ge(v_out[b], 16 * turns)
                sp.wait_ge(gate_out[b], 16 * turns)

        @block.gpsimd
        def _(pool):
            for b in two:
                ins = pool.memset(vrow[b][:, :, :], 0.0)
            ins.then_inc(consts, 1)
            pool.wait_ge(consts, 1)
            for b in two:
                for j in range(GROUP):
                    ones = vrow[b][:, j, :].rearrange("p (r h a n) -> p r h a n", r=PAIRS, h=2, a=2)
                    ins = pool.memset(ones[:, :, 0, :, HD], 1.0)
            ins.then_inc(consts, 1)
            pool.wait_ge(consts, 2)

            def root(i, s):
                i, b = group_turn(i, s)
                pool.wait_ge(ve_ready[b], i + 1)
                pool.tensor_tensor(rstd[b][:, :], ve[b][:, :], c["power"][:, :], ALU.pow).then_inc(rstd_ready[b], 1)

            def split_values(i, s):
                i, b = group_turn(i, s)
                pool.wait_ge(v_ready[b], i + 1)
                pool.wait_ge(v_out[b], 16 * i)
                pool.nop(nofuse=True)
                for part in two:
                    for j in range(GROUP):
                        rows = vrow[b][:, j, :].rearrange("p (r h a n) -> p r h a n", r=PAIRS, h=2, a=2)
                        hi, lo = rows[:, :, 0, :, 0:HD], rows[:, :, 1, :, 0:HD]
                        v = v32[b][:, j, :].rearrange("p (r a n) -> p r a n", r=PAIRS, a=2)
                        if part == 0:
                            ins = pool.tensor_copy(hi, v)
                        else:
                            ins = pool.tensor_tensor(lo, v, hi, ALU.subtract)
                    if part == 0:
                        ins.then_inc(v_hi[b], 1)
                        pool.wait_ge(v_hi[b], i + 1)
                ins.then_inc(v_rows[b], 1)

            def step(i, s):
                if group_exists(i, s + 2):
                    root(i, s + 2)
                if group_exists(i, s):
                    split_values(i, s)
            group_steps(pool, 2, step)

        @block.scalar
        def _(act):
            act.wait_ge(w_in, 80)
            for lo, hi, scale in W_COLUMNS:
                ins = act.activation(w[:, 0, :, lo:hi], w32[:, :, lo:hi], ACT.Copy, scale=scale)
            ins.then_inc(w_hi, 1)

            def normalise(i, s):
                i, b = group_turn(i, s)
                act.wait_ge(shift_ready[b], i + 1)
                act.wait_ge(turned[b], i)
                for j in range(GROUP):
                    ins = act.activation(xn[b][:, j, :], x[b][:, j, :], ACT.Identity,
                                         scale=rstd[b][:, j:j + 1], bias=shift[b][:, j:j + 1])
                ins.then_inc(xn_ready[b], 1)

            def high(i, s):
                i, b = group_turn(i, s)
                act.wait_ge(turned[b], i + 1)
                for k in range(KD):
                    ins = act.activation(xT[b][0][:, k, :], psT[k][:, :], ACT.Copy)
                ins.then_inc(xT_hi[b], 1)

            def queries_keys(i, s):
                i, b = group_turn(i, s)
                act.wait_ge(qk_out[b], 64 * i)
                for n in range(4):
                    act.wait_ge(qk_sum[n % 2], 4 * i + 2 * b + n // 2 + 1)
                    act.activation(qk[b][:, n, 0, :], psQ[n % 2][:, :], ACT.Identity,
                                   bias=bias_qk[:, n:n + 1]).then_inc(qk_hi[n % 2], 1)

            def gates(i, s):
                i, b = group_turn(i, s)
                act.wait_ge(v_ready[b], i + 1)
                for j in range(GROUP):
                    ins = act.activation(z[b][:, j:j + 1], psV[j][:, D:D + 1], ACT.Exp, scale=-1.0,
                                         bias=bias_g[:, :])
                ins.then_inc(exp_ready[b], 1)

            def step(i, s):
                if group_exists(i, s):
                    queries_keys(i, s)
                if group_exists(i, s + 1):
                    high(i, s + 1)
                if group_exists(i, s + 2):
                    normalise(i, s + 2)
                if group_exists(i, s):
                    gates(i, s)
            group_steps(act, 2, step)

        @block.tensor
        def _(pe):
            pe.wait_ge(w_lo, 1)
            terms = ((0, 0), (0, 1), (1, 0))

            def turn(i, s):
                i, b = group_turn(i, s)
                pe.wait_ge(xn_ready[b], i + 1)
                pe.wait_ge(xT_lo[1 - b], i + b)
                for j in range(GROUP):
                    for k in range(KD):
                        ins = pe.transpose(psT[k][:, j * P:(j + 1) * P], xn[b][:, j, k * P:(k + 1) * P],
                                           c["ident"][:, :])
                ins.then_inc(turned[b], 1)

            def queries_keys(i, s):
                i, b = group_turn(i, s)
                pe.wait_ge(xT_lo[b], i + 1)
                for n in range(4):
                    pe.wait_ge(qk_lo[n % 2], 4 * i + 2 * b + n // 2)
                    for k in range(KD):
                        for wh, xh in terms:
                            ins = pe.matmul(psQ[n % 2][:, :], w[:, wh, k, n * P:(n + 1) * P], xT[b][xh][:, k, :],
                                            start=(k == 0 and (wh, xh) == terms[0]),
                                            stop=(k == KD - 1 and (wh, xh) == terms[-1]))
                    ins.then_inc(qk_sum[n % 2], 1)

            def values(i, s):
                i, b = group_turn(i, s)
                pe.wait_ge(exp_ready[1 - b], i + b)
                for j in range(GROUP):
                    for k in range(KD):
                        for wh, xh in terms:
                            ins = pe.matmul(psV[j][:, 0:D + 1], xT[b][xh][:, k, j * P:(j + 1) * P],
                                            w[:, wh, k, 2 * D:NG],
                                            start=(k == 0 and (wh, xh) == terms[0]),
                                            stop=(k == KD - 1 and (wh, xh) == terms[-1]))
                ins.then_inc(v_sum[b], 1)

            def step(i, s):
                if group_exists(i, s):
                    queries_keys(i, s)
                if group_exists(i, s + 1):
                    turn(i, s + 1)
                if group_exists(i, s):
                    values(i, s)
            group_steps(pe, 1, step)

        @block.vector
        def _(dve):
            dve.wait_ge(w_hi, 1)
            for lo, hi, scale in W_COLUMNS:
                ins = dve.scalar_tensor_tensor(w[:, 1, :, lo:hi], w32[:, :, lo:hi], scale, w[:, 0, :, lo:hi],
                                               ALU.mult, ALU.subtract)
            ins.then_inc(w_lo, 1)
            first = Chain(dve, chain)
            first(dve.tensor_scalar(bias_qk[:, 2:4], bias_qk[:, 2:4], SCORE_SCALE, None, ALU.mult))
            first(dve.tensor_scalar(bias_g[:, :], bias_g[:, :], -1.0, None, ALU.mult))
            dve.wait_ge(w_lo, 1)

            def statistics(i, s):
                i, b = group_turn(i, s)
                dve.wait_ge(x_in[b], 16 * i + 16)
                for j in range(GROUP):
                    ins = dve.bn_stats(stats[b][:, j, :], x[b][:, j, :])
                ins.then_inc(stats_ready[b], 1)

            def variance(i, s):
                i, b = group_turn(i, s)
                dve.wait_ge(stats_ready[b], i + 1)
                dve.nop(nofuse=True)
                for j in range(GROUP):
                    ins = dve.bn_aggr(mv[b][:, j, :], stats[b][:, j, :])
                ins.then_inc(mean_ready[b], 1)
                dve.wait_ge(mean_ready[b], i + 1)
                dve.tensor_scalar(ve[b][:, :], mv[b][:, :, 1], EPS, W_ATT * W_ATT, ALU.add,
                                  ALU.mult).then_inc(ve_ready[b], 1)

            def shifts(i, s):
                i, b = group_turn(i, s)
                dve.wait_ge(rstd_ready[b], i + 1)
                dve.scalar_tensor_tensor(shift[b][:, :], mv[b][:, :, 0], -1.0, rstd[b][:, :],
                                         ALU.mult, ALU.mult).then_inc(shift_ready[b], 1)

            def low(i, s):
                i, b = group_turn(i, s)
                dve.wait_ge(xT_hi[b], i + 1)
                for k in range(KD):
                    ins = dve.tensor_tensor(xT[b][1][:, k, :], psT[k][:, :], xT[b][0][:, k, :], ALU.subtract)
                ins.then_inc(xT_lo[b], 1)

            def queries_keys(i, s, chunks):
                i, b = group_turn(i, s)
                for n in chunks:
                    dve.wait_ge(qk_hi[n % 2], 4 * i + 2 * b + n // 2 + 1)
                    dve.scalar_tensor_tensor(qk[b][:, n, 1, :], psQ[n % 2][:, :], bias_qk[:, n:n + 1],
                                             qk[b][:, n, 0, :], ALU.add, ALU.subtract).then_inc(qk_lo[n % 2], 1)

            def values(i, s):
                i, b = group_turn(i, s)
                dve.wait_ge(v_sum[b], i + 1)
                dve.wait_ge(v_rows[b], i)
                for j in range(GROUP):
                    ins = dve.tensor_tensor(v32[b][:, j, :], psV[j][:, 0:D], bias_v[:, :], ALU.add)
                ins.then_inc(v_ready[b], 1)

            def gates(i, s):
                i, b = group_turn(i, s)
                dve.wait_ge(exp_ready[b], i + 1)
                dve.wait_ge(gate_out[b], 16 * i)
                dve.tensor_scalar(z[b][:, :], z[b][:, :], 1.0, None, ALU.add).then_inc(z_ready[b], 1)
                dve.wait_ge(z_ready[b], i + 1)
                dve.reciprocal(gate[b][:, :, 1], z[b][:, :]).then_inc(gate_there[b], 1)
                dve.wait_ge(gate_there[b], i + 1)
                dve.tensor_scalar(gate[b][:, :, 0], gate[b][:, :, 1], -1.0, 1.0,
                                  ALU.mult, ALU.add).then_inc(gate_ready[b], 1)

            def step(i, s):
                if group_exists(i, s + 1):
                    queries_keys(i, s + 1, (0, 1))
                if group_exists(i, s):
                    gates(i, s)
                if group_exists(i, s + 3):
                    statistics(i, s + 3)
                if group_exists(i, s + 1):
                    queries_keys(i, s + 1, (2, 3))
                if group_exists(i, s + 3):
                    variance(i, s + 3)
                if group_exists(i, s + 2):
                    low(i, s + 2)
                if group_exists(i, s + 3):
                    shifts(i, s + 3)
                if group_exists(i, s + 1):
                    values(i, s + 1)
            group_steps(dve, 3, step)


def attention_phase(nc, ctx, c, scratch):
    m = Memory(nc, ctx, "att")
    two, four = range(2), range(4)
    TILES_S = SPAN // QT
    DUOS_S = TILES_S * PAIRS // 2
    BODY = 2 * DUOS_S
    TURNS = SPANS // 2
    AHEAD = 6
    PARTS = 3
    q = [m.sb(f"q{b}", [P, PAIRS, TILES_S, 2, QT], FP16) for b in two]
    k = [m.sb(f"k{b}", [P, PAIRS, SPAN_K + N_GLOBAL], FP16) for b in two]
    v0 = [m.sb(f"v0{b}", [P, TILES_S, VROW], FP16) for b in two]
    v1 = [m.sb(f"v1{b}", [P, TILES_S, 2, VROW], FP16) for b in two]
    gate = [m.sb(f"gate{b}", [P, TILES_S, 2]) for b in two]
    pad_rows = m.sb("pad_rows", [P, 2])
    shift = [m.sb(f"shift{b}", [P, 2, 2]) for b in four]
    prob = [m.sb(f"prob{b}", [P, 2, KEYS]) for b in two]
    probT = [[m.sb(f"probT{b}{h}", [P, 2, 2, P], FP16) for h in two] for b in two]
    share = [m.sb(f"share{b}", [P, 4, 2]) for b in two]
    parts = [m.sb(f"parts{b}", [P, 4, 2, HD]) for b in two]
    out = [m.sb(f"out{b}", [P, TILES_S, 2, 4, HD]) for b in two]
    psS = [m.ps(f"psS{b}", [P, 2, KEYS]) for b in four]
    psT = [m.ps(f"psT{b}", [P, 2, 2, P]) for b in two]
    psO = [m.ps(f"psO{b}", [P, 512]) for b in two]

    def both(name):
        return [m.sem(f"{name}{b}") for b in two]

    def each(name):
        return [m.sem(f"{name}{b}") for b in four]

    pad_ready, q_cleared, k_cleared, v_cleared = (
        m.sem("pad_ready"), m.sem("q_cleared"), m.sem("k_cleared"), m.sem("v_cleared"))
    q_in = [[m.sem(f"q_in{b}{t}") for t in range(SPAN // QT)] for b in two]
    k_in, gate_in, v_in, stored = both("k_in"), both("gate_in"), c["v_in"], c["stored"]
    scored, maxed, exped = each("scored"), each("maxed"), each("exped")
    inverted, shared = both("inverted"), both("shared")
    turned, p_hi, p_lo, used = both("turned"), both("p_hi"), both("p_lo"), both("used")
    taken, added = both("taken"), both("added")
    Q_LOADS, K_LOADS, V_LOADS = 2 * PARTS, 2 * (2 * PARTS + 1), TILES_S + 2

    def duo(i, s):
        return i + s // BODY, s % BODY

    def exists(i, s):
        return s >= 0 and (not isinstance(i, int) or i * BODY + s < TURNS * BODY)

    def use(i, s, buffers):
        return (BODY // buffers) * i + s // buffers

    def where(s):
        return s // DUOS_S, s % DUOS_S // 4, 2 * (s % 4)

    def places(i, b):
        batch = i // (SEQ // SPAN // 2)
        tok = 2 * SPAN * i + SPAN * b
        return (tok, tok + 2 * WINDOW * batch, 2 * SPAN * (i % (SEQ // SPAN // 2)) + SPAN * b,
                SEQP * batch + WINDOW)

    def steps(eng, step):
        for s in range(-AHEAD, 0):
            step(0, s)
        with eng.Fori(0, TURNS - 1) as i:
            for s in range(BODY):
                step(i, s)
        for s in range(BODY):
            step(TURNS - 1, s)

    with nc.Block() as block:
        @block.gpsimd
        def _(pool):
            link = Chain(pool, pad_ready)
            link(pool.memset(pad_rows[:, :], 0.0))
            link(pool.affine_select(out=pad_rows[:, :], in_=pad_rows[:, :], compare_op=ALU.not_equal, fill=PAD_Q,
                                    base=-PARTS * HD, pattern=[[-QT, 2]], channel_multiplier=1))
            for b in two:
                pool.memset(v1[b][:, :, :, :].bitcast(FP32), 0.0).then_inc(v_cleared, 1)
            pool.wait_ge(v_cleared, 2)

            def load_values(i, b):
                _, first, _, global_keys = places(i, b)
                vs = scratch["vs"]
                for t in range(TILES_S):
                    pool.dma_start(v0[b][:, t, :], vs[bass.ds(first + QT * t, P), :]).then_inc(v_in[b], 16)
                pool.dma_start(v1[b][0:QT, :, 0, :],
                               vs[bass.ds(first + P, SPAN), :].rearrange("(t p) n -> p t n", p=QT)).then_inc(v_in[b], 16)
                pool.dma_start(v1[b][QT:P, :, 1, :],
                               vs[bass.ds(global_keys, N_GLOBAL), :].unsqueeze(1).to_broadcast(
                                   [N_GLOBAL, TILES_S, VROW])).then_inc(v_in[b], 16)

            def outputs(i, b):
                pool.wait_ge(stored[b], 32 * i)
                for t in range(TILES_S):
                    for half in two:
                        pool.wait_ge(taken[half], TILES_S * (2 * i + b) + t + 1)
                        pool.tensor_tensor(out[b][:, t, half, :, :], parts[half][:, :, 0, :],
                                           parts[half][:, :, 1, :], ALU.add).then_inc(added[half], 1)
                pool.wait_ge(added[1], TILES_S * (2 * i + b + 1))
                pool.nop(nofuse=True)
                for a in two:
                    rows = scratch["att"][bass.ds(2 * SPAN * i + SPAN * b, SPAN), a * P:(a + 1) * P]
                    pool.dma_start(rows.rearrange("(t p) n -> p t n", p=QT),
                                   out[b][QT * a:QT * a + QT, :, :, :, :].rearrange("p t h u n -> p t (h u n)")
                                   ).then_inc(stored[b], 16)

            for b in two:
                load_values(0, b)
            with pool.Fori(0, TURNS - 1) as i:
                for b in two:
                    outputs(i, b)
                    load_values(i + 1, b)
            for b in two:
                outputs(TURNS - 1, b)
            for b in two:
                pool.wait_ge(stored[b], 32 * TURNS)

        @block.sync
        def _(sp):
            sp.wait_ge(k_cleared, 2)
            qs = scratch["qs"].rearrange("(h r a d) t -> h a d r t", h=2, a=2, d=HD)
            ks = scratch["ks"].rearrange("(h r a d) t -> h a d r t", h=2, a=2, d=HD)

            def load(i, b):
                tok, first, at, global_keys = places(i, b)
                n = 0
                for a in two:
                    for part, kh in enumerate((0, 1, 0)):
                        r0 = QT * a + HD * part
                        sp.dma_start(k[b][r0:r0 + HD, :, 0:SPAN_K], ks[kh, a][:, :, bass.ds(first, SPAN_K)]
                                     ).then_inc(k_in[b], 16)
                        sp.dma_start(k[b][r0:r0 + HD, :, SPAN_K:SPAN_K + N_GLOBAL],
                                     ks[kh, a][:, :, bass.ds(global_keys, N_GLOBAL)]).then_inc(k_in[b], 16)
                        n += 2
                    r0 = QT * a + PARTS * HD
                    sp.dma_start(k[b][r0:r0 + 1, :, 0:SPAN_K],
                                 scratch["padk"][0:1, bass.ds(at, SPAN_K)].unsqueeze(1).to_broadcast(
                                     [1, PAIRS, SPAN_K])).then_inc(k_in[b], 16)
                    n += 1
                assert n == K_LOADS, n
                if isinstance(i, int):
                    sp.wait_ge(q_cleared, 2)
                for t in range(TILES_S):
                    for a in two:
                        for part, qh in enumerate((0, 0, 1)):
                            r0 = QT * a + HD * part
                            sp.dma_start(q[b][r0:r0 + HD, :, t, a, :],
                                         qs[qh, a][:, :, bass.ds(tok + QT * t, QT)]).then_inc(q_in[b][t], 16)
                if not isinstance(i, int):
                    sp.wait_ge(taken[1], TILES_S * (2 * i + b - 1))
                    sp.nop(nofuse=True)
                for a in two:
                    sp.dma_start(gate[b][QT * a:QT * a + QT, :, :],
                                 scratch["gate"][bass.ds(tok, SPAN), :].rearrange("(t q) e -> q t e", q=QT)
                                 ).then_inc(gate_in[b], 16)

            for b in two:
                load(0, b)
            with sp.Fori(0, TURNS - 1) as i:
                for b in two:
                    sp.wait_ge(scored[3], use(i, DUOS_S * (b + 1) - 1, 4) + 1)
                    sp.nop(nofuse=True)
                    load(i + 1, b)

        @block.tensor
        def _(pe):
            def scores(i, s):
                i, s = duo(i, s)
                sb, t, r = where(s)
                bank = s % 4
                if s % DUOS_S == 0:
                    pe.wait_ge(k_in[sb], 16 * K_LOADS * (i + 1))
                if s % 4 == 0:
                    pe.wait_ge(q_in[sb][t], 16 * Q_LOADS * (i + 1))
                pe.wait_ge(exped[bank], use(i, s, 4))
                pe.matmul(psS[bank][:, :, :].rearrange("p u n -> p (u n)"), c["ident16"][:, :],
                          c["mask"][:, :, :].rearrange("p u n -> p (u n)"), start=True, stop=True)
                for u in two:
                    lhs = q[sb][:, r + u, t, :, :].rearrange("p a n -> p (a n)")
                    pe.matmul(psS[bank][:, u, 0:LOCAL], lhs, k[sb][:, r + u, t * QT:t * QT + LOCAL],
                              start=False, stop=True, skip_group_check=True)
                    ins = pe.matmul(psS[bank][:, u, LOCAL:KEYS], lhs, k[sb][:, r + u, SPAN_K:SPAN_K + N_GLOBAL],
                                    start=False, stop=True, skip_group_check=True)
                ins.then_inc(scored[bank], 1)

            def turn(i, s):
                i, s = duo(i, s)
                b = s % 2
                pe.wait_ge(exped[s % 4], use(i, s, 4) + 1)
                pe.wait_ge(p_lo[b], use(i, s, 2))
                for u in two:
                    for blk in two:
                        ins = pe.transpose(psT[b][:, u, blk, :], prob[b][:, u, blk * P:(blk + 1) * P],
                                           c["ident"][:, :])
                ins.then_inc(turned[b], 1)

            def values(i, s):
                i, s = duo(i, s)
                sb, t, r = where(s)
                b, bank = s % 2, s // 2 % 2
                if s % DUOS_S == 0:
                    pe.wait_ge(v_in[sb], 16 * V_LOADS * (i + 1))
                if s % 2 == 0:
                    pe.wait_ge(taken[bank], use(i, s, 4))
                pe.wait_ge(p_lo[b], use(i, s, 2) + 1)
                for u in two:
                    slot = 2 * (s % 2) + u
                    o = psO[bank][:, slot * 2 * VW:(slot + 1) * 2 * VW]
                    terms = ((0, 0), (0, 1), (1, 0))
                    for n, (ph, vh) in enumerate(terms):
                        col = (2 * (r + u) + vh) * VW
                        pe.matmul(o, probT[b][ph][:, u, 1, :], v1[sb][:, t, :, col:col + VW],
                                  start=(n == 0), stop=(n == 2))
                    for ph, vh in terms:
                        col = (2 * (r + u) + vh) * VW
                        ins = pe.matmul(o[:, 0:VW], probT[b][ph][:, u, 0, :], v0[sb][:, t, col:col + VW],
                                        start=False, stop=True, skip_group_check=True)
                ins.then_inc(used[b], 1)

            def step(i, s):
                if exists(i, s + 6):
                    scores(i, s + 6)
                if exists(i, s + 3):
                    turn(i, s + 3)
                if exists(i, s + 1):
                    values(i, s + 1)
            steps(pe, step)

        @block.scalar
        def _(act):
            def high(i, s):
                i, s = duo(i, s)
                b = s % 2
                act.wait_ge(turned[b], use(i, s, 2) + 1)
                act.wait_ge(used[b], use(i, s, 2))
                act.activation(probT[b][0][:, :, :, :].rearrange("p u k n -> p (u k n)"),
                               psT[b][:, :, :, :].rearrange("p u k n -> p (u k n)"), ACT.Copy).then_inc(p_hi[b], 1)

            def exps(i, s):
                i, s = duo(i, s)
                b, bank = s % 2, s % 4
                act.wait_ge(maxed[bank], use(i, s, 4) + 1)
                act.wait_ge(turned[b], use(i, s, 2))
                for u in two:
                    for seg, (lo, hi) in enumerate(((0, LOCAL), (LOCAL, KEYS))):
                        ins = act.activation(prob[b][:, u, lo:hi], psS[bank][:, u, lo:hi], ACT.Exp,
                                             bias=shift[bank][:, u, seg:seg + 1])
                ins.then_inc(exped[bank], 1)

            def step(i, s):
                if exists(i, s + 2):
                    high(i, s + 2)
                if exists(i, s + 4):
                    exps(i, s + 4)
            act.wait_ge(pad_ready, 2)
            for b in two:
                for a in two:
                    ins = act.activation(q[b][:, :, :, a, :].rearrange("p r t n -> p (r t) n"),
                                         pad_rows[:, a:a + 1].unsqueeze(2).to_broadcast([P, PAIRS * TILES_S, QT]),
                                         ACT.Copy)
                ins.then_inc(q_cleared, 1)
            steps(act, step)

        @block.vector
        def _(dve):
            for b in two:
                dve.memset(k[b][:, :, :].bitcast(FP32), 0.0).then_inc(k_cleared, 1)

            def maxima(i, s):
                i, s = duo(i, s)
                bank, n = s % 4, use(i, s, 4)
                dve.wait_ge(scored[bank], n + 1)
                dve.tensor_reduce(shift[bank][:, :, 0], psS[bank][:, :, 0:LOCAL], AX.X, ALU.max, negate=True)
                dve.tensor_reduce(shift[bank][:, :, 1], psS[bank][:, :, LOCAL:KEYS], AX.X, ALU.max,
                                  negate=True).then_inc(maxed[bank], 1)

            def low(i, s):
                i, s = duo(i, s)
                b = s % 2
                dve.wait_ge(p_hi[b], use(i, s, 2) + 1)
                dve.tensor_tensor(probT[b][1][:, :, :, :].rearrange("p u k n -> p (u k n)"),
                                  psT[b][:, :, :, :].rearrange("p u k n -> p (u k n)"),
                                  probT[b][0][:, :, :, :].rearrange("p u k n -> p (u k n)"),
                                  ALU.subtract).then_inc(p_lo[b], 1)

            def bank_of(i, s):
                i, s = duo(i, s)
                b = s // 2 % 2
                return where(s)[0], where(s)[1], b, use(i, s, 4), psO[b][:, 0:8 * VW].rearrange(
                    "p (u g n) -> p u g n", u=4, g=2)

            def invert(i, s):
                _, _, b, n, sums = bank_of(i, s)
                dve.wait_ge(used[1], 2 * n + b + 1)
                dve.reciprocal(share[b][:, :, :], sums[:, :, :, HD]).then_inc(inverted[b], 1)

            def weigh(i, s):
                sb, t, b, n, _ = bank_of(i, s)
                if s % DUOS_S == 1:
                    dve.wait_ge(gate_in[sb], 32 * (i + 1))
                dve.wait_ge(inverted[b], n + 1)
                dve.tensor_tensor(share[b][:, :, :], share[b][:, :, :],
                                  gate[sb][:, t, :].unsqueeze(1).to_broadcast([P, 4, 2]),
                                  ALU.mult).then_inc(shared[b], 1)

            def outputs(i, s):
                _, _, b, n, sums = bank_of(i, s)
                dve.wait_ge(shared[b], n + 1)
                dve.wait_ge(added[b], n)
                for a in two:
                    rows = slice(QT * a, QT * a + QT)
                    ins = dve.tensor_tensor(parts[b][rows, :, :, :], sums[rows, :, :, (HD + 1) * a:(HD + 1) * a + HD],
                                            share[b][rows, :, :].unsqueeze(3).to_broadcast([QT, 4, 2, HD]), ALU.mult)
                ins.then_inc(taken[b], 1)

            def step(i, s):
                last = s % 2 == 1 and exists(i, s)
                if last:
                    invert(i, s)
                if exists(i, s + 5):
                    maxima(i, s + 5)
                if last:
                    weigh(i, s)
                if exists(i, s + 2):
                    low(i, s + 2)
                if last:
                    outputs(i, s)
            steps(dve, step)


def copy_phase(nc, ctx, scratch, out):
    m = Memory(nc, ctx, "copy")
    copied = m.sem("copied")
    PIECES = 8
    rows = TOK // PIECES
    with nc.Block() as block:
        @block.sync
        def _(sp):
            for n in range(PIECES):
                sp.dma_start(out[n * rows:(n + 1) * rows, :].rearrange("(p r) d -> p (r d)", p=P),
                             scratch["acc2"][n * rows:(n + 1) * rows, :].rearrange("(p r) d -> p (r d)", p=P)
                             ).then_inc(copied, 16)
            sp.wait_ge(copied, 16 * PIECES)


def macaron(nc, x, wqkv, bqkv, wout, bout, wg, bg, wr, w1, w2, out):
    scratch = {}

    def dram(name, shape, dt=FP32):
        scratch[name] = nc.dram_tensor(f"scratch_{name}", shape, dt, kind="Internal").ap()

    for which in (1, 2):
        dram(f"xn{which}", [TOK + SLOTS, D])
        dram(f"acc{which}", [TOK + SLOTS, D])
        dram(f"list{which}", [LIST_PAD + SLOTS, 2], I32)
    dram("qs", [2 * D, TOK], FP16)
    dram("ks", [2 * D, BATCH * SEQP], FP16)
    dram("vs", [BATCH * SEQP, VROW], FP16)
    dram("padk", [1, SEQP], FP16)
    dram("gate", [TOK, 2])
    dram("att", [TOK, D])
    weights = dict(wqkv=wqkv, bqkv=bqkv, wout=wout, bout=bout, wg=wg, bg=bg, wr=wr, w1=w1, w2=w2)
    with ExitStack() as ctx:
        c = constants(Memory(nc, ctx, "const"))

        def phase(build, *args):
            with ExitStack() as inner:
                build(nc, inner, *args)

        phase(fill_phase, c, scratch)
        phase(router_phase, c, scratch, 1, x.rearrange("b t d -> (b t) d"), weights)
        phase(capacity_phase, c, scratch, 1)
        phase(ffn_phase, c, scratch, 1)
        clear_semaphores(nc)
        phase(qkv_phase, c, scratch, weights)
        phase(attention_phase, c, scratch)
        clear_semaphores(nc)
        phase(router_phase, c, scratch, 2, scratch["acc1"], weights)
        phase(capacity_phase, c, scratch, 2)
        phase(ffn_phase, c, scratch, 2)
        phase(copy_phase, scratch, out.rearrange("b t d -> (b t) d"))


_INS = ["L0_attn_hidden_states", "L0_attn_Wqkv", "L0_attn_bqkv", "L0_attn_Wout", "L0_attn_bout", "L0_attn_Wg",
        "L0_attn_bg", "L0_ffn_Wr", "L0_ffn_W1", "L0_ffn_W2"]


def kernel(**inputs):
    import numpy as np
    import concourse.bacc as bacc
    from concourse.bass_utils import run_bass_kernel_spmd

    nc = bacc.Bacc("TRN2", target_bir_lowering=False, num_devices=1)
    arrays, args = {}, []
    for name in _INS:
        a = np.ascontiguousarray(inputs[name])
        arrays[f"in_{name}"] = a
        args.append(nc.dram_tensor(f"in_{name}", a.shape, mybir.dt.from_np(a.dtype), kind="ExternalInput").ap())
    out = nc.dram_tensor("out", (BATCH, SEQ, D), FP32, kind="ExternalOutput").ap()
    macaron(nc, *args, out)
    r = run_bass_kernel_spmd(nc, [arrays], core_ids=[0])
    return r.results[0]["out"]
```
